# Optimizing a Trainium2 kernel written in Bass

```python
import numpy as np
import jax
import jax.numpy as jnp

def _softmax(x, axis=-1):
    return jax.nn.softmax(x, axis=axis)

def _gelu(x):
    return jax.nn.gelu(x, approximate=True)

def _silu(x):
    return jax.nn.silu(x)

def _sigmoid(x):
    return jax.nn.sigmoid(x)

def _layernorm(x, axis=-1, eps=1e-05):
    m = jnp.mean(x, axis=axis, keepdims=True)
    v = jnp.var(x, axis=axis, keepdims=True)
    return (x - m) / jnp.sqrt(v + eps)

def _scatter_add(tgt, idx, src, axis=0):
    return tgt.at[idx].add(src)

def _segment_sum(src, seg, n):
    return jax.ops.segment_sum(src, seg, n)
kernel_name = 'mk_perceiver_d4_seqx_r8_cae50e'

def setup_inputs(seed: int=0):
    np.random.seed(seed)
    _w = jnp.asarray

    def _rec_inputs():
        import jax
        import jax.numpy as jnp
        _rk = jax.random.key(seed)
        x = 7.22e-05 + 1 * jax.random.normal(jax.random.fold_in(_rk, 1), (2, 128, 256), jnp.float32)
        _lenS = 128 - jax.random.randint(jax.random.fold_in(_rk, 7), (2,), 0, max(1, 128 // 4) + 1, jnp.int32)
        _lenS2 = 2048 - jax.random.randint(jax.random.fold_in(_rk, 8), (2,), 0, max(1, 2048 // 4) + 1, jnp.int32)
        _ctx_2048P = jax.random.normal(jax.random.fold_in(_rk, 11), (2, 16, 256), jnp.float32)
        _ctx_2048c = jax.random.dirichlet(jax.random.fold_in(_rk, 511), 0.3 * jnp.ones((16,), jnp.float32), (2, 2048))
        _ctx_2048t = jnp.einsum('bsk,bkd->bsd', _ctx_2048c, _ctx_2048P)
        _ctx_2048t = _ctx_2048t * jax.lax.rsqrt(jnp.mean(jnp.square(_ctx_2048t)) + 1e-12) * 0.953939
        ctx_2048 = -0.000514642 + 1.00011 * (_ctx_2048t + 0.3 * jax.random.normal(jax.random.fold_in(_rk, 611), (2, 2048, 256), jnp.float32))
        pos_BxS2 = jnp.broadcast_to(jnp.arange(2048, dtype=jnp.int32), (2, 2048))
        itok_BxS_4096_4607 = jax.random.randint(jax.random.fold_in(_rk, 14), (2, 128), 512, 576, jnp.int32)
        _validS = jnp.arange(128)[None, :] < _lenS[:, None]
        _validS2 = jnp.arange(2048)[None, :] < _lenS2[:, None]
        _causal = jnp.tril(jnp.ones((128, 128), dtype=bool))
        mask_BxS2_bk0 = jnp.logical_not(jnp.broadcast_to(_validS2[:, :], (2, 2048)))
        return (x, ctx_2048, pos_BxS2, itok_BxS_4096_4607, mask_BxS2_bk0)
    x, ctx_2048, pos_BxS2, itok_BxS_4096_4607, mask_BxS2_bk0 = _rec_inputs()

    def _L0_xattn_setup():
        import jax, jax.numpy as jnp
        import numpy as np
        D_MODEL = 256
        NUM_HEADS = 16
        HEAD_DIM = D_MODEL // NUM_HEADS

        def _fq_sym(x, axis):
            s = jnp.max(jnp.abs(x), axis=axis, keepdims=True) / 127.0
            s = jnp.maximum(s, 1e-08)
            q = jnp.clip(jnp.round(x / s), -127.0, 127.0) * s
            return x + jax.lax.stop_gradient(q - x)

        def _fq_unsigned(x, axis):
            s = jnp.max(x, axis=axis, keepdims=True) / 255.0
            s = jnp.maximum(s, 1e-08)
            q = jnp.clip(jnp.round(x / s), 0.0, 255.0) * s
            return x + jax.lax.stop_gradient(q - x)
        key = jax.random.key(seed)
        ks = jax.random.split(key, 8)
        B, N, M, C = (2, 256, 64, D_MODEL)
        return {'x': jax.random.normal(ks[0], (B, N, C), jnp.float32), 'cond': jax.random.normal(ks[1], (B, M, C), jnp.float32), 'Wq': jax.random.normal(ks[2], (C, C), jnp.float32) * 0.02, 'bq': jnp.zeros((C,), jnp.float32), 'Wkv': jax.random.normal(ks[3], (C, 2 * C), jnp.float32) * 0.02, 'bkv': jnp.zeros((2 * C,), jnp.float32), 'Wp': jax.random.normal(ks[4], (C, C), jnp.float32) * 0.02, 'bp': jnp.zeros((C,), jnp.float32)}
    _L0_xattn_all = _L0_xattn_setup()
    _L0_xattn_in = {k: v for k, v in _L0_xattn_all.items() if k in ('Wq', 'bq', 'Wkv', 'bkv', 'Wp', 'bp')}
    del _L0_xattn_all

    def _L0_attn_setup():
        import jax, jax.numpy as jnp
        import numpy as np
        EPS = 1e-05
        key = jax.random.key(seed)
        ks = jax.random.split(key, 6)
        B, T, H = (4, 256, 256)
        scale = 2 ** (-2.5) * (6.0 / (H + H)) ** 0.5
        return {'hidden_states': jax.random.normal(ks[0], (B, T, H), dtype=jnp.float32), 'Wi': jax.random.normal(ks[1], (H, H), dtype=jnp.float32) * scale, 'Wf': jax.random.normal(ks[2], (H, H), dtype=jnp.float32) * scale, 'Wg': jax.random.normal(ks[3], (H, H), dtype=jnp.float32) * scale, 'Wo': jax.random.normal(ks[4], (H, H), dtype=jnp.float32) * scale, 'gnorm_w': jnp.ones((H,), dtype=jnp.float32)}
    _L0_attn_all = _L0_attn_setup()
    _L0_attn_in = {k: v for k, v in _L0_attn_all.items() if k in ('Wi', 'Wf', 'Wg', 'Wo', 'gnorm_w')}
    del _L0_attn_all

    def _L0_ffn_setup():
        import jax, jax.numpy as jnp
        import numpy as np
        B, S, H = (1, 256, 256)
        E, K, I = (16, 4, 176)
        IS = 352
        CAP = 128
        key = jax.random.key(seed)
        ks = jax.random.split(key, 8)
        sc = 0.02
        return {'hidden_states': jax.random.normal(ks[0], (B, S, H), jnp.float32), 'gate_w': jax.random.normal(ks[1], (E, H), jnp.float32) * sc, 'w_gate': jax.random.normal(ks[2], (E, H, I), jnp.float32) * sc, 'w_up': jax.random.normal(ks[3], (E, H, I), jnp.float32) * sc, 'w_down': jax.random.normal(ks[4], (E, I, H), jnp.float32) * sc, 'sw_gate': jax.random.normal(ks[5], (H, IS), jnp.float32) * sc, 'sw_up': jax.random.normal(ks[6], (H, IS), jnp.float32) * sc, 'sw_down': jax.random.normal(ks[7], (IS, H), jnp.float32) * sc}
    _L0_ffn_all = _L0_ffn_setup()
    _L0_ffn_in = {k: v for k, v in _L0_ffn_all.items() if k in ('gate_w', 'w_gate', 'w_up', 'w_down', 'sw_gate', 'sw_up', 'sw_down')}
    del _L0_ffn_all

    def _L1_xattn_setup():
        import jax, jax.numpy as jnp
        import numpy as np
        key = jax.random.key(seed)
        k1, k2, k3 = jax.random.split(key, 3)
        B, S, D, M = (8, 256, 256, 128)
        hidden_states = jax.random.normal(k1, (B, S, D), dtype=jnp.float32)
        memory_tokens = jax.random.normal(k2, (B, M, D), dtype=jnp.float32)
        memory_mask = jax.random.randint(k3, (B, M), 0, 2).astype(jnp.bool_)
        return {'hidden_states': hidden_states, 'memory_tokens': memory_tokens, 'memory_mask': memory_mask}
    _L1_xattn_all = _L1_xattn_setup()
    _L1_xattn_in = {k: v for k, v in _L1_xattn_all.items() if k in ()}
    del _L1_xattn_all

    def _L1_attn_setup():
        import jax, jax.numpy as jnp
        import numpy as np
        H = 16
        EPS_DEN = 1e-06

        def _decay_scan(x, decay, init):
            xT = jnp.moveaxis(x, 2, 0)

            def step(s, xt):
                s = decay * s + xt
                return (s, s)
            _, ys = jax.lax.scan(step, init, xT)
            return jnp.moveaxis(ys, 0, 2)

        def _phi(z):
            return jax.nn.elu(z) + 1.0

        def _reference_tuple_inner(x, w_qkv, w_out, decay_param):
            B, T, Hid = x.shape
            D = Hid // H
            qkv = x @ w_qkv
            q, k, v = jnp.split(qkv, 3, axis=-1)

            def to_bhtd(t):
                return t.reshape(B, T, H, D).transpose(0, 2, 1, 3)
            q = _phi(to_bhtd(q))
            k = _phi(to_bhtd(k))
            v = to_bhtd(v)
            decay = jax.nn.sigmoid(decay_param).reshape(1, H, 1)
            init = jnp.zeros((B, H, D), dtype=x.dtype)
            running_kv = _decay_scan(k * v, decay, init)
            running_ksum = _decay_scan(k, decay, init)
            den = jnp.clip(jnp.sum(q * running_ksum, axis=-1, keepdims=True), EPS_DEN, None)
            out = q * running_kv / den
            out = out.transpose(0, 2, 1, 3).reshape(B, T, Hid) @ w_out
            new_kv = running_kv[:, :, -1, :]
            new_ksum = running_ksum[:, :, -1, :]
            return (out, new_kv, new_ksum)
        key = jax.random.key(seed)
        k1, k2, k3 = jax.random.split(key, 3)
        x = jax.random.normal(k1, (2, 512, 256), dtype=jnp.float32)
        w_qkv = jax.random.normal(k2, (256, 768), dtype=jnp.float32) * 0.02
        w_out = jax.random.normal(k3, (256, 256), dtype=jnp.float32) * 0.02
        decay_param = jnp.full((H,), 0.95, dtype=jnp.float32)
        return {'x': x, 'w_qkv': w_qkv, 'w_out': w_out, 'decay_param': decay_param}
    _L1_attn_all = _L1_attn_setup()
    _L1_attn_in = {k: v for k, v in _L1_attn_all.items() if k in ('w_qkv', 'w_out', 'decay_param')}
    del _L1_attn_all

    def _L1_ffn_setup():
        import jax, jax.numpy as jnp
        import numpy as np
        LN_EPS = 1e-05
        L2_EPS = 1e-12

        def _l2norm(v, axis):
            n = jnp.sqrt(jnp.sum(v * v, axis=axis, keepdims=True))
            return v / jnp.maximum(n, L2_EPS)
        key = jax.random.key(seed)
        ks = jax.random.split(key, 4)
        B, N, D, E, S, H = (8, 256, 256, 16, 128, 64)
        x = jax.random.normal(ks[0], (B, N, D), dtype=jnp.float32)
        mu = jax.random.normal(ks[1], (D, E, S), dtype=jnp.float32) / np.sqrt(D)
        W1 = jax.random.normal(ks[2], (E, D, H), dtype=jnp.float32) * np.sqrt(2.0 / D)
        W2 = jax.random.normal(ks[3], (E, H, D), dtype=jnp.float32) * np.sqrt(2.0 / (H + D))
        return {'x': x, 'gamma': jnp.ones((D,), jnp.float32), 'beta': jnp.zeros((D,), jnp.float32), 'mu': mu, 'scale': jnp.ones((1,), jnp.float32), 'W1': W1, 'b1': jnp.zeros((E, H), jnp.float32), 'W2': W2, 'b2': jnp.zeros((E, D), jnp.float32)}
    _L1_ffn_all = _L1_ffn_setup()
    _L1_ffn_in = {k: v for k, v in _L1_ffn_all.items() if k in ('gamma', 'beta', 'mu', 'scale', 'W1', 'b1', 'W2', 'b2')}
    del _L1_ffn_all

    def _L2_xattn_setup():
        import jax, jax.numpy as jnp
        import numpy as np
        EPS = 1e-06
        NUM_HEADS = 16

        def _feature_map(x):
            return jnp.where(x > 0, x + 1.0, jnp.exp(x))
        key = jax.random.key(seed)
        ks = jax.random.split(key, 7)
        B, L, S, D = (4, 512, 512, 256)
        sc = 1.0 / np.sqrt(D)
        return {'query': jax.random.normal(ks[0], (B, L, D), jnp.float32), 'kv': jax.random.normal(ks[1], (B, S, D), jnp.float32), 'Wq': jax.random.normal(ks[2], (D, D), jnp.float32) * sc, 'Wg': jax.random.normal(ks[3], (D, D), jnp.float32) * sc, 'bg': jnp.ones((D,), jnp.float32), 'Wkv': jax.random.normal(ks[4], (2 * D, D), jnp.float32) * sc, 'Wo': jax.random.normal(ks[5], (D, D), jnp.float32) * sc}
    _L2_xattn_all = _L2_xattn_setup()
    _L2_xattn_in = {k: v for k, v in _L2_xattn_all.items() if k in ('Wq', 'Wg', 'bg', 'Wkv', 'Wo')}
    del _L2_xattn_all

    def _L2_attn_setup():
        import jax, jax.numpy as jnp
        import numpy as np
        B, T, E, H = (2, 256, 256, 16)
        D = E // H
        ROPE_BASE = 10000.0

        def _rope(x):
            t, d = (x.shape[-2], x.shape[-1])
            j = jnp.arange(d // 2, dtype=x.dtype)
            thetas = ROPE_BASE ** (-2.0 * j / d)
            m = jnp.arange(1, t + 1, dtype=x.dtype)
            ang = m[:, None] * thetas[None, :]
            C = jnp.concatenate([ang, ang], axis=-1)
            x_rot = jnp.concatenate([-x[..., d // 2:], x[..., :d // 2]], axis=-1)
            return x * jnp.cos(C) + x_rot * jnp.sin(C)
        key = jax.random.key(seed)
        ks = jax.random.split(key, 9)
        s = 1.0 / np.sqrt(E)
        return {'x': jax.random.normal(ks[0], (B, T, E), jnp.float32), 'Wq': jax.random.normal(ks[1], (E, E), jnp.float32) * s, 'bq': jax.random.normal(ks[2], (E,), jnp.float32) * s, 'Wk': jax.random.normal(ks[3], (E, E), jnp.float32) * s, 'bk': jax.random.normal(ks[4], (E,), jnp.float32) * s, 'Wv': jax.random.normal(ks[5], (E, E), jnp.float32) * s, 'bv': jax.random.normal(ks[6], (E,), jnp.float32) * s, 'Wo': jax.random.normal(ks[7], (E, E), jnp.float32) * s, 'bo': jax.random.normal(ks[8], (E,), jnp.float32) * s}
    _L2_attn_all = _L2_attn_setup()
    _L2_attn_in = {k: v for k, v in _L2_attn_all.items() if k in ('Wq', 'bq', 'Wk', 'bk', 'Wv', 'bv', 'Wo', 'bo')}
    del _L2_attn_all

    def _L2_ffn_setup():
        import jax, jax.numpy as jnp
        import numpy as np
        K = 2
        SCALING = 16.0 / 16.0
        key = jax.random.key(seed)
        ks = jax.random.split(key, 7)
        B, T, D, O, E, R = (2, 512, 256, 256, 8, 16)
        return {'x': jax.random.normal(ks[0], (B, T, D), dtype=jnp.float32), 'W': jax.random.normal(ks[1], (O, D), dtype=jnp.float32) * (1.0 / np.sqrt(D)), 'b': jax.random.normal(ks[2], (O,), dtype=jnp.float32) * 0.02, 'lora_A': jax.random.normal(ks[3], (E, R, D), dtype=jnp.float32) * (1.0 / np.sqrt(D)), 'lora_B': jax.random.normal(ks[4], (E, O, R), dtype=jnp.float32) * 0.02, 'gate_w': jax.random.normal(ks[5], (E, D), dtype=jnp.float32) * 0.02, 'gate_b': jax.random.normal(ks[6], (E,), dtype=jnp.float32) * 0.02}
    _L2_ffn_all = _L2_ffn_setup()
    _L2_ffn_in = {k: v for k, v in _L2_ffn_all.items() if k in ('W', 'b', 'lora_A', 'lora_B', 'gate_w', 'gate_b')}
    del _L2_ffn_all

    def _L3_xattn_setup():
        import jax, jax.numpy as jnp
        import numpy as np
        B, CTX, DRAFT, D = (2, 512, 64, 256)
        H, KVH, HD = (16, 4, 128)
        N_REP = H // KVH
        EPS = 1e-06
        THETA = 10000.0
        SCALE = 1.0 / np.sqrt(HD).astype(np.float32)

        def _rms_norm(x, w):
            v = jnp.mean(jnp.square(x.astype(jnp.float32)), axis=-1, keepdims=True)
            return (w * (x.astype(jnp.float32) * jax.lax.rsqrt(v + EPS))).astype(x.dtype)

        def _rotate_half(x):
            x1, x2 = jnp.split(x, 2, axis=-1)
            return jnp.concatenate((-x2, x1), axis=-1)

        def _rope(x, pos):
            inv_freq = 1.0 / THETA ** (jnp.arange(0, HD, 2, dtype=jnp.float32) / HD)
            freqs = pos.astype(jnp.float32)[:, None, :, None] * inv_freq
            emb = jnp.concatenate((freqs, freqs), axis=-1)
            return x * jnp.cos(emb) + _rotate_half(x) * jnp.sin(emb)
        key = jax.random.key(seed)
        ks = jax.random.split(key, 6)
        return {'draft_hidden': jax.random.normal(ks[0], (B, DRAFT, D), jnp.float32), 'context_hidden': jax.random.normal(ks[1], (B, CTX, D), jnp.float32), 'Wq': jax.random.normal(ks[2], (H * HD, D), jnp.float32) * 0.02, 'Wk': jax.random.normal(ks[3], (KVH * HD, D), jnp.float32) * 0.02, 'Wv': jax.random.normal(ks[4], (KVH * HD, D), jnp.float32) * 0.02, 'Wo': jax.random.normal(ks[5], (D, H * HD), jnp.float32) * 0.02, 'q_norm_w': jnp.ones((HD,), jnp.float32), 'k_norm_w': jnp.ones((HD,), jnp.float32), 'context_position_ids': jnp.broadcast_to(jnp.arange(CTX, dtype=jnp.int32), (B, CTX)), 'draft_position_ids': jnp.broadcast_to(CTX + jnp.arange(DRAFT, dtype=jnp.int32), (B, DRAFT))}
    _L3_xattn_all = _L3_xattn_setup()
    _L3_xattn_in = {k: v for k, v in _L3_xattn_all.items() if k in ('Wq', 'Wk', 'Wv', 'Wo', 'q_norm_w', 'k_norm_w')}
    del _L3_xattn_all

    def _L3_attn_setup():
        import jax, jax.numpy as jnp
        import numpy as np
        EPS = 1e-06

        def rmsnorm(x, w):
            return x * jax.lax.rsqrt(jnp.mean(x * x, axis=-1, keepdims=True) + EPS) * w

        def rope(x, freqs):
            xr = x.reshape(x.shape[:-1] + (-1, 2))
            c, s = (jnp.cos(freqs), jnp.sin(freqs))
            x0, x1 = (xr[..., 0], xr[..., 1])
            return jnp.stack([x0 * c - x1 * s, x0 * s + x1 * c], axis=-1).reshape(x.shape)
        B_, L, D = (2, 256, 256)
        Din, H, P, N = (512, 64, 64, 128)
        key = jax.random.key(seed)
        ks = jax.random.split(key, 10)
        sd = lambda fan: 1.0 / np.sqrt(fan)
        f32 = jnp.float32
        return {'x': jax.random.normal(ks[0], (B_, L, D), f32), 'Wx': (jax.random.normal(ks[1], (Din, D)) * sd(D)).astype(f32), 'Wz': (jax.random.normal(ks[2], (Din, D)) * sd(D)).astype(f32), 'WB': (jax.random.normal(ks[3], (H * N, D)) * sd(D)).astype(f32), 'WC': (jax.random.normal(ks[4], (H * N, D)) * sd(D)).astype(f32), 'Wdt': jax.random.uniform(ks[5], (H, D), f32, -0.0001, 0.0001), 'Wlam': (jax.random.normal(ks[6], (H, D)) * sd(D)).astype(f32), 'Wth': (jax.random.normal(ks[7], (H * (N // 2), D)) * sd(D)).astype(f32), 'A_log': jnp.log(jnp.linspace(1.0, N, H)).astype(f32), 'Bn_w': jnp.ones((N,), f32), 'Cn_w': jnp.ones((N,), f32), 'B_bias': jnp.ones((H, N), f32), 'C_bias': jnp.ones((H, N), f32), 'Wout': (jax.random.normal(ks[8], (D, Din)) * sd(Din)).astype(f32)}
    _L3_attn_all = _L3_attn_setup()
    _L3_attn_in = {k: v for k, v in _L3_attn_all.items() if k in ('Wx', 'Wz', 'WB', 'WC', 'Wdt', 'Wlam', 'Wth', 'A_log', 'Bn_w', 'Cn_w', 'B_bias', 'C_bias', 'Wout')}
    del _L3_attn_all

    def _L3_ffn_setup():
        import jax, jax.numpy as jnp
        import numpy as np
        BLOCK_SIZE = 32
        HIDDEN_SIZE = 256
        MLP_DIM = 2048
        NVFP4_LUT = jnp.array([0.0, 0.5, 1.0, 1.5, 2.0, 3.0, 4.0, 6.0, 0.0, -0.5, -1.0, -1.5, -2.0, -3.0, -4.0, -6.0], dtype=jnp.float32)

        def dequant_nvfp4(W_packed, scales, block=BLOCK_SIZE):
            N = W_packed.shape[0]
            low = W_packed & 15
            high = W_packed >> 4 & 15
            idx = jnp.stack([low, high], axis=-1).reshape(N, -1)
            vals = NVFP4_LUT[idx]
            K = vals.shape[1]
            vals = vals.reshape(N, K // block, block) * scales[:, :, None]
            return vals.reshape(N, K)
        key = jax.random.key(seed)
        ks = jax.random.split(key, 7)
        x = jax.random.normal(ks[0], (4, 32, HIDDEN_SIZE), dtype=jnp.float32)
        gate_W_packed = jax.random.randint(ks[1], (MLP_DIM, HIDDEN_SIZE // 2), 0, 32, dtype=jnp.int32)
        gate_scales = jax.random.uniform(ks[2], (MLP_DIM, HIDDEN_SIZE // BLOCK_SIZE), dtype=jnp.float32) * 0.1 + 0.001
        up_W_packed = jax.random.randint(ks[3], (MLP_DIM, HIDDEN_SIZE // 2), 0, 32, dtype=jnp.int32)
        up_scales = jax.random.uniform(ks[4], (MLP_DIM, HIDDEN_SIZE // BLOCK_SIZE), dtype=jnp.float32) * 0.1 + 0.001
        down_W_packed = jax.random.randint(ks[5], (HIDDEN_SIZE, MLP_DIM // 2), 0, 32, dtype=jnp.int32)
        down_scales = jax.random.uniform(ks[6], (HIDDEN_SIZE, MLP_DIM // BLOCK_SIZE), dtype=jnp.float32) * 0.1 + 0.001
        return {'x': x, 'gate_W_packed': gate_W_packed, 'gate_scales': gate_scales, 'up_W_packed': up_W_packed, 'up_scales': up_scales, 'down_W_packed': down_W_packed, 'down_scales': down_scales}
    _L3_ffn_all = _L3_ffn_setup()
    _L3_ffn_in = {k: v for k, v in _L3_ffn_all.items() if k in ('gate_W_packed', 'gate_scales', 'up_W_packed', 'up_scales', 'down_W_packed', 'down_scales')}
    del _L3_ffn_all
    return {'x': x, 'ctx_2048': ctx_2048, 'pos_BxS2': pos_BxS2, 'itok_BxS_4096_4607': itok_BxS_4096_4607, 'mask_BxS2_bk0': mask_BxS2_bk0, 'L0_xattn_Wq': _L0_xattn_in['Wq'], 'L0_xattn_bq': _L0_xattn_in['bq'], 'L0_xattn_Wkv': _L0_xattn_in['Wkv'], 'L0_xattn_bkv': _L0_xattn_in['bkv'], 'L0_xattn_Wp': _L0_xattn_in['Wp'], 'L0_xattn_bp': _L0_xattn_in['bp'], 'L0_attn_Wi': _L0_attn_in['Wi'], 'L0_attn_Wf': _L0_attn_in['Wf'], 'L0_attn_Wg': _L0_attn_in['Wg'], 'L0_attn_Wo': _L0_attn_in['Wo'], 'L0_attn_gnorm_w': _L0_attn_in['gnorm_w'], 'L0_ffn_gate_w': _L0_ffn_in['gate_w'], 'L0_ffn_w_gate': _L0_ffn_in['w_gate'], 'L0_ffn_w_up': _L0_ffn_in['w_up'], 'L0_ffn_w_down': _L0_ffn_in['w_down'], 'L0_ffn_sw_gate': _L0_ffn_in['sw_gate'], 'L0_ffn_sw_up': _L0_ffn_in['sw_up'], 'L0_ffn_sw_down': _L0_ffn_in['sw_down'], 'L1_attn_w_qkv': _L1_attn_in['w_qkv'], 'L1_attn_w_out': _L1_attn_in['w_out'], 'L1_attn_decay_param': _L1_attn_in['decay_param'], 'L1_ffn_gamma': _L1_ffn_in['gamma'], 'L1_ffn_beta': _L1_ffn_in['beta'], 'L1_ffn_mu': _L1_ffn_in['mu'], 'L1_ffn_scale': _L1_ffn_in['scale'], 'L1_ffn_W1': _L1_ffn_in['W1'], 'L1_ffn_b1': _L1_ffn_in['b1'], 'L1_ffn_W2': _L1_ffn_in['W2'], 'L1_ffn_b2': _L1_ffn_in['b2'], 'L2_xattn_Wq': _L2_xattn_in['Wq'], 'L2_xattn_Wg': _L2_xattn_in['Wg'], 'L2_xattn_bg': _L2_xattn_in['bg'], 'L2_xattn_Wkv': _L2_xattn_in['Wkv'], 'L2_xattn_Wo': _L2_xattn_in['Wo'], 'L2_attn_Wq': _L2_attn_in['Wq'], 'L2_attn_bq': _L2_attn_in['bq'], 'L2_attn_Wk': _L2_attn_in['Wk'], 'L2_attn_bk': _L2_attn_in['bk'], 'L2_attn_Wv': _L2_attn_in['Wv'], 'L2_attn_bv': _L2_attn_in['bv'], 'L2_attn_Wo': _L2_attn_in['Wo'], 'L2_attn_bo': _L2_attn_in['bo'], 'L2_ffn_W': _L2_ffn_in['W'], 'L2_ffn_b': _L2_ffn_in['b'], 'L2_ffn_lora_A': _L2_ffn_in['lora_A'], 'L2_ffn_lora_B': _L2_ffn_in['lora_B'], 'L2_ffn_gate_w': _L2_ffn_in['gate_w'], 'L2_ffn_gate_b': _L2_ffn_in['gate_b'], 'L3_xattn_Wq': _L3_xattn_in['Wq'], 'L3_xattn_Wk': _L3_xattn_in['Wk'], 'L3_xattn_Wv': _L3_xattn_in['Wv'], 'L3_xattn_Wo': _L3_xattn_in['Wo'], 'L3_xattn_q_norm_w': _L3_xattn_in['q_norm_w'], 'L3_xattn_k_norm_w': _L3_xattn_in['k_norm_w'], 'L3_attn_Wx': _L3_attn_in['Wx'], 'L3_attn_Wz': _L3_attn_in['Wz'], 'L3_attn_WB': _L3_attn_in['WB'], 'L3_attn_WC': _L3_attn_in['WC'], 'L3_attn_Wdt': _L3_attn_in['Wdt'], 'L3_attn_Wlam': _L3_attn_in['Wlam'], 'L3_attn_Wth': _L3_attn_in['Wth'], 'L3_attn_A_log': _L3_attn_in['A_log'], 'L3_attn_Bn_w': _L3_attn_in['Bn_w'], 'L3_attn_Cn_w': _L3_attn_in['Cn_w'], 'L3_attn_B_bias': _L3_attn_in['B_bias'], 'L3_attn_C_bias': _L3_attn_in['C_bias'], 'L3_attn_Wout': _L3_attn_in['Wout'], 'L3_ffn_gate_W_packed': _L3_ffn_in['gate_W_packed'], 'L3_ffn_gate_scales': _L3_ffn_in['gate_scales'], 'L3_ffn_up_W_packed': _L3_ffn_in['up_W_packed'], 'L3_ffn_up_scales': _L3_ffn_in['up_scales'], 'L3_ffn_down_W_packed': _L3_ffn_in['down_W_packed'], 'L3_ffn_down_scales': _L3_ffn_in['down_scales']}

def reference(x, ctx_2048, pos_BxS2, itok_BxS_4096_4607, mask_BxS2_bk0, L0_xattn_Wq, L0_xattn_bq, L0_xattn_Wkv, L0_xattn_bkv, L0_xattn_Wp, L0_xattn_bp, L0_attn_Wi, L0_attn_Wf, L0_attn_Wg, L0_attn_Wo, L0_attn_gnorm_w, L0_ffn_gate_w, L0_ffn_w_gate, L0_ffn_w_up, L0_ffn_w_down, L0_ffn_sw_gate, L0_ffn_sw_up, L0_ffn_sw_down, L1_attn_w_qkv, L1_attn_w_out, L1_attn_decay_param, L1_ffn_gamma, L1_ffn_beta, L1_ffn_mu, L1_ffn_scale, L1_ffn_W1, L1_ffn_b1, L1_ffn_W2, L1_ffn_b2, L2_xattn_Wq, L2_xattn_Wg, L2_xattn_bg, L2_xattn_Wkv, L2_xattn_Wo, L2_attn_Wq, L2_attn_bq, L2_attn_Wk, L2_attn_bk, L2_attn_Wv, L2_attn_bv, L2_attn_Wo, L2_attn_bo, L2_ffn_W, L2_ffn_b, L2_ffn_lora_A, L2_ffn_lora_B, L2_ffn_gate_w, L2_ffn_gate_b, L3_xattn_Wq, L3_xattn_Wk, L3_xattn_Wv, L3_xattn_Wo, L3_xattn_q_norm_w, L3_xattn_k_norm_w, L3_attn_Wx, L3_attn_Wz, L3_attn_WB, L3_attn_WC, L3_attn_Wdt, L3_attn_Wlam, L3_attn_Wth, L3_attn_A_log, L3_attn_Bn_w, L3_attn_Cn_w, L3_attn_B_bias, L3_attn_C_bias, L3_attn_Wout, L3_ffn_gate_W_packed, L3_ffn_gate_scales, L3_ffn_up_W_packed, L3_ffn_up_scales, L3_ffn_down_W_packed, L3_ffn_down_scales):
    import jax
    import jax.numpy as jnp

    def _L0_xattn_ref(x, cond, Wq, bq, Wkv, bkv, Wp, bp):
        import jax, jax.numpy as jnp
        import numpy as np
        D_MODEL = 256
        NUM_HEADS = 16
        HEAD_DIM = D_MODEL // NUM_HEADS

        def _fq_sym(x, axis):
            s = jnp.max(jnp.abs(x), axis=axis, keepdims=True) / 127.0
            s = jnp.maximum(s, 1e-08)
            q = jnp.clip(jnp.round(x / s), -127.0, 127.0) * s
            return x + jax.lax.stop_gradient(q - x)

        def _fq_unsigned(x, axis):
            s = jnp.max(x, axis=axis, keepdims=True) / 255.0
            s = jnp.maximum(s, 1e-08)
            q = jnp.clip(jnp.round(x / s), 0.0, 255.0) * s
            return x + jax.lax.stop_gradient(q - x)
        B, N, C = x.shape
        H, hd = (NUM_HEADS, HEAD_DIM)
        q = (x @ Wq + bq).reshape(1, B * N, H, hd)
        kv = (cond @ Wkv + bkv).reshape(1, -1, 2, H, hd)
        k, v = (kv[:, :, 0], kv[:, :, 1])
        scale = 1.0 / np.sqrt(hd).astype(np.float32)
        q = jnp.transpose(q * scale, (0, 2, 1, 3))
        k = jnp.transpose(k, (0, 2, 1, 3))
        v = jnp.transpose(v, (0, 2, 1, 3))
        q = _fq_sym(q, axis=-1)
        k = _fq_sym(k, axis=-1)
        v = _fq_sym(v, axis=2)
        attn = jnp.einsum('bhqd,bhkd->bhqk', q, k)
        attn = jax.nn.softmax(attn.astype(jnp.float32), axis=-1)
        attn = _fq_unsigned(attn, axis=-1)
        out = jnp.einsum('bhqk,bhkd->bhqd', attn, v)
        out = jnp.transpose(out, (0, 2, 1, 3)).reshape(B, N, C)
        return out @ Wp + bp

    def _L0_attn_ref(hidden_states, Wi, Wf, Wg, Wo, gnorm_w):
        import jax, jax.numpy as jnp
        import numpy as np
        EPS = 1e-05
        i = jnp.einsum('bth,dh->btd', hidden_states, Wi)
        f = jnp.einsum('bth,dh->btd', hidden_states, Wf)
        g = jnp.einsum('bth,dh->btd', hidden_states, Wg)
        gate = jax.nn.sigmoid(f)
        v = jax.nn.silu(i) * (1.0 - gate)

        def combine(c1, c2):
            a1, b1 = c1
            a2, b2 = c2
            return (a1 * a2, a2 * b1 + b2)
        _, o = jax.lax.associative_scan(combine, (gate, v), axis=1)
        rms = o * jax.lax.rsqrt(jnp.mean(o * o, axis=-1, keepdims=True) + EPS)
        o = rms * gnorm_w * g * jax.nn.sigmoid(g)
        return jnp.einsum('btd,hd->bth', o, Wo)

    def _L0_ffn_ref(hidden_states, gate_w, w_gate, w_up, w_down, sw_gate, sw_up, sw_down):
        import jax, jax.numpy as jnp
        import numpy as np
        B, S, H = (1, 256, 256)
        E, K, I = (16, 4, 176)
        IS = 352
        CAP = 128
        b, s, h = hidden_states.shape
        x = hidden_states.reshape(-1, h)
        T = x.shape[0]
        scores = jax.nn.softmax(x @ gate_w.T, axis=-1)
        topk_w, topk_i = jax.lax.top_k(scores, K)
        topk_w = topk_w / (topk_w.sum(-1, keepdims=True) + 1e-20)
        flat_i = topk_i.reshape(-1)
        flat_w = topk_w.reshape(-1)
        order = jnp.argsort(flat_i)
        se = flat_i[order]
        counts = jax.ops.segment_sum(jnp.ones_like(flat_i), flat_i, num_segments=E)
        starts = jnp.cumsum(counts) - counts
        rank = jnp.arange(T * K) - starts[se]
        tok = order // K
        slot = jnp.where(rank < CAP, rank, CAP)
        buf = jnp.full((E, CAP + 1), T, dtype=jnp.int32).at[se, slot].set(tok)[:, :CAP]
        wbuf = jnp.zeros((E, CAP + 1), x.dtype).at[se, slot].set(flat_w[order])[:, :CAP]
        xpad = jnp.concatenate([x, jnp.zeros((1, h), x.dtype)], axis=0)
        xg = xpad[buf]
        gact = jax.nn.silu(jnp.einsum('ech,ehi->eci', xg, w_gate))
        mid = gact * jnp.einsum('ech,ehi->eci', xg, w_up)
        eout = jnp.einsum('eci,eih->ech', mid, w_down) * wbuf[..., None]
        y = jnp.zeros((T + 1, h), x.dtype).at[buf.reshape(-1)].add(eout.reshape(-1, h))[:T]
        shared = jax.nn.silu(x @ sw_gate) * (x @ sw_up) @ sw_down
        return (y + shared).reshape(b, s, h)

    def _L1_xattn_ref(hidden_states, memory_tokens, memory_mask):
        import jax, jax.numpy as jnp
        import numpy as np
        B, S, D = hidden_states.shape
        scale = 1.0 / jnp.sqrt(jnp.asarray(D, hidden_states.dtype))
        scores = jnp.einsum('bsd,bmd->bsm', hidden_states, memory_tokens) * scale
        neg_inf = jnp.asarray(-1e+30, scores.dtype)
        scores = jnp.where(memory_mask[:, None, :], scores, neg_inf)
        attn = jax.nn.softmax(scores, axis=-1)
        readout = jnp.einsum('bsm,bmd->bsd', attn, memory_tokens)
        valid_b = jnp.any(memory_mask, axis=-1)
        out = jnp.where(valid_b[:, None, None], readout, jnp.zeros_like(readout))
        return out

    def _L1_attn_ref(x, w_qkv, w_out, decay_param):
        import jax, jax.numpy as jnp
        import numpy as np
        H = 16
        EPS_DEN = 1e-06

        def _decay_scan(x, decay, init):
            xT = jnp.moveaxis(x, 2, 0)

            def step(s, xt):
                s = decay * s + xt
                return (s, s)
            _, ys = jax.lax.scan(step, init, xT)
            return jnp.moveaxis(ys, 0, 2)

        def _phi(z):
            return jax.nn.elu(z) + 1.0

        def _reference_tuple_inner(x, w_qkv, w_out, decay_param):
            B, T, Hid = x.shape
            D = Hid // H
            qkv = x @ w_qkv
            q, k, v = jnp.split(qkv, 3, axis=-1)

            def to_bhtd(t):
                return t.reshape(B, T, H, D).transpose(0, 2, 1, 3)
            q = _phi(to_bhtd(q))
            k = _phi(to_bhtd(k))
            v = to_bhtd(v)
            decay = jax.nn.sigmoid(decay_param).reshape(1, H, 1)
            init = jnp.zeros((B, H, D), dtype=x.dtype)
            running_kv = _decay_scan(k * v, decay, init)
            running_ksum = _decay_scan(k, decay, init)
            den = jnp.clip(jnp.sum(q * running_ksum, axis=-1, keepdims=True), EPS_DEN, None)
            out = q * running_kv / den
            out = out.transpose(0, 2, 1, 3).reshape(B, T, Hid) @ w_out
            new_kv = running_kv[:, :, -1, :]
            new_ksum = running_ksum[:, :, -1, :]
            return (out, new_kv, new_ksum)
        return _reference_tuple_inner(x, w_qkv, w_out, decay_param)[0]

    def _L1_ffn_ref(x, gamma, beta, mu, scale, W1, b1, W2, b2):
        import jax, jax.numpy as jnp
        import numpy as np
        LN_EPS = 1e-05
        L2_EPS = 1e-12

        def _l2norm(v, axis):
            n = jnp.sqrt(jnp.sum(v * v, axis=axis, keepdims=True))
            return v / jnp.maximum(n, L2_EPS)
        B, N, D = x.shape
        _, E, S = mu.shape
        mean = jnp.mean(x, axis=-1, keepdims=True)
        var = jnp.mean(jnp.square(x - mean), axis=-1, keepdims=True)
        x_ln = (x - mean) / jnp.sqrt(var + LN_EPS) * gamma + beta
        x_n = _l2norm(x_ln, -1) * scale
        mu_n = _l2norm(mu, 0)
        logits = jnp.einsum('bnd,des->bnes', x_n, mu_n)
        dispatch = jax.nn.softmax(logits, axis=1)
        combine = jax.nn.softmax(logits.reshape(B, N, E * S), axis=-1)
        slot_in = jnp.einsum('bnd,bnes->besd', x_ln, dispatch)
        h = jax.nn.gelu(jnp.einsum('besd,edh->besh', slot_in, W1) + b1[None, :, None, :], approximate=False)
        slot_out = jnp.einsum('besh,ehd->besd', h, W2) + b2[None, :, None, :]
        out = jnp.einsum('bsd,bns->bnd', slot_out.reshape(B, E * S, D), combine)
        return out

    def _L2_xattn_ref(query, kv, Wq, Wg, bg, Wkv, Wo):
        import jax, jax.numpy as jnp
        import numpy as np
        EPS = 1e-06
        NUM_HEADS = 16

        def _feature_map(x):
            return jnp.where(x > 0, x + 1.0, jnp.exp(x))
        B, L, D = query.shape
        S = kv.shape[1]
        H = NUM_HEADS
        hd = D // H
        q = query @ Wq.T
        gate = jax.nn.sigmoid(query @ Wg.T + bg)
        kvp = kv @ Wkv.T
        k, v = jnp.split(kvp, 2, axis=-1)
        q = _feature_map(q.reshape(B, L, H, hd).transpose(0, 2, 1, 3))
        k = _feature_map(k.reshape(B, S, H, hd).transpose(0, 2, 1, 3))
        v = v.reshape(B, S, H, hd).transpose(0, 2, 1, 3)
        kv_summary = jnp.einsum('bhsd,bhse->bhde', k, v)
        k_sum = k.sum(axis=-2)
        z = 1.0 / (jnp.einsum('bhld,bhd->bhl', q, k_sum)[..., None] + EPS)
        attn = jnp.einsum('bhld,bhde->bhle', q, kv_summary) * z
        attn = attn.transpose(0, 2, 1, 3).reshape(B, L, D)
        out = attn * gate @ Wo.T
        return out

    def _L2_attn_ref(x, Wq, bq, Wk, bk, Wv, bv, Wo, bo):
        import jax, jax.numpy as jnp
        import numpy as np
        B, T, E, H = (2, 256, 256, 16)
        D = E // H
        ROPE_BASE = 10000.0

        def _rope(x):
            t, d = (x.shape[-2], x.shape[-1])
            j = jnp.arange(d // 2, dtype=x.dtype)
            thetas = ROPE_BASE ** (-2.0 * j / d)
            m = jnp.arange(1, t + 1, dtype=x.dtype)
            ang = m[:, None] * thetas[None, :]
            C = jnp.concatenate([ang, ang], axis=-1)
            x_rot = jnp.concatenate([-x[..., d // 2:], x[..., :d // 2]], axis=-1)
            return x * jnp.cos(C) + x_rot * jnp.sin(C)
        b, t, e = x.shape

        def proj(W, bias):
            y = jnp.einsum('bte,fe->btf', x, W) + bias
            return y.reshape(b, t, H, D).transpose(0, 2, 1, 3)
        q = _rope(proj(Wq, bq))
        k = _rope(proj(Wk, bk))
        v = proj(Wv, bv)
        scale = jnp.sqrt(jnp.asarray(D, x.dtype))
        att = jnp.einsum('bhqd,bhkd->bhqk', q, k) / scale
        causal = jnp.tril(jnp.ones((t, t), bool))
        att = jnp.where(causal, att, -jnp.inf)
        att = jax.nn.softmax(att, axis=-1)
        y = jnp.einsum('bhqk,bhkd->bhqd', att, v)
        y = y.transpose(0, 2, 1, 3).reshape(b, t, e)
        y = jnp.einsum('bte,fe->btf', y, Wo) + bo
        return y

    def _L2_ffn_ref(x, W, b, lora_A, lora_B, gate_w, gate_b):
        import jax, jax.numpy as jnp
        import numpy as np
        K = 2
        SCALING = 16.0 / 16.0
        orig_shape = x.shape
        D = orig_shape[-1]
        O = W.shape[0]
        x_flat = x.reshape(-1, D)
        base = x_flat @ W.T + b
        logits = x_flat @ gate_w.T + gate_b
        topk_logits, topk_idx = jax.lax.top_k(logits, K)
        gates = jax.nn.softmax(topk_logits, axis=-1)
        xA = jnp.einsum('nd,erd->ner', x_flat, lora_A)
        delta_all = jnp.einsum('ner,eor->neo', xA, lora_B)
        delta_topk = jnp.take_along_axis(delta_all, topk_idx[:, :, None], axis=1)
        lora_update = jnp.sum(delta_topk * gates[:, :, None], axis=1)
        out = base + SCALING * lora_update
        return out.reshape(*orig_shape[:-1], O)

    def _L3_xattn_ref(draft_hidden, context_hidden, Wq, Wk, Wv, Wo, q_norm_w, k_norm_w, context_position_ids, draft_position_ids):
        import jax, jax.numpy as jnp
        import numpy as np
        B, CTX, DRAFT, D = (2, 512, 64, 256)
        H, KVH, HD = (16, 4, 128)
        N_REP = H // KVH
        EPS = 1e-06
        THETA = 10000.0
        SCALE = 1.0 / np.sqrt(HD).astype(np.float32)

        def _rms_norm(x, w):
            v = jnp.mean(jnp.square(x.astype(jnp.float32)), axis=-1, keepdims=True)
            return (w * (x.astype(jnp.float32) * jax.lax.rsqrt(v + EPS))).astype(x.dtype)

        def _rotate_half(x):
            x1, x2 = jnp.split(x, 2, axis=-1)
            return jnp.concatenate((-x2, x1), axis=-1)

        def _rope(x, pos):
            inv_freq = 1.0 / THETA ** (jnp.arange(0, HD, 2, dtype=jnp.float32) / HD)
            freqs = pos.astype(jnp.float32)[:, None, :, None] * inv_freq
            emb = jnp.concatenate((freqs, freqs), axis=-1)
            return x * jnp.cos(emb) + _rotate_half(x) * jnp.sin(emb)
        bsz, draft_len, _ = draft_hidden.shape
        ctx_len = context_hidden.shape[1]
        total_len = ctx_len + draft_len
        q = (draft_hidden @ Wq.T).reshape(bsz, draft_len, H, HD)
        q = _rms_norm(q, q_norm_w).transpose(0, 2, 1, 3)
        kv_in = jnp.concatenate([context_hidden, draft_hidden], axis=1)
        k = (kv_in @ Wk.T).reshape(bsz, total_len, KVH, HD)
        v = (kv_in @ Wv.T).reshape(bsz, total_len, KVH, HD).transpose(0, 2, 1, 3)
        k = _rms_norm(k, k_norm_w).transpose(0, 2, 1, 3)
        full_position_ids = jnp.concatenate([context_position_ids, draft_position_ids], axis=1)
        q = _rope(q, draft_position_ids)
        k = _rope(k, full_position_ids)
        k = jnp.repeat(k, N_REP, axis=1)
        v = jnp.repeat(v, N_REP, axis=1)
        scores = jnp.einsum('bhqd,bhkd->bhqk', q, k) * SCALE
        probs = jax.nn.softmax(scores, axis=-1)
        attn = jnp.einsum('bhqk,bhkd->bhqd', probs, v)
        attn = attn.transpose(0, 2, 1, 3).reshape(bsz, draft_len, H * HD)
        return attn @ Wo.T

    def _L3_attn_ref(x, Wx, Wz, WB, WC, Wdt, Wlam, Wth, A_log, Bn_w, Cn_w, B_bias, C_bias, Wout):
        import jax, jax.numpy as jnp
        import numpy as np
        EPS = 1e-06

        def rmsnorm(x, w):
            return x * jax.lax.rsqrt(jnp.mean(x * x, axis=-1, keepdims=True) + EPS) * w

        def rope(x, freqs):
            xr = x.reshape(x.shape[:-1] + (-1, 2))
            c, s = (jnp.cos(freqs), jnp.sin(freqs))
            x0, x1 = (xr[..., 0], xr[..., 1])
            return jnp.stack([x0 * c - x1 * s, x0 * s + x1 * c], axis=-1).reshape(x.shape)
        B_, L, D = x.shape
        H = A_log.shape[0]
        N = B_bias.shape[1]
        Din = Wx.shape[0]
        P = Din // H
        xp = x @ Wx.T
        z = x @ Wz.T
        Bm = (x @ WB.T).reshape(B_, L, H, N)
        Cm = (x @ WC.T).reshape(B_, L, H, N)
        Bm = rmsnorm(Bm, Bn_w) + B_bias
        Cm = rmsnorm(Cm, Cn_w) + C_bias
        dt = jax.nn.softplus(x @ Wdt.T)
        lam = jax.nn.sigmoid(x @ Wlam.T)
        theta = (x @ Wth.T).reshape(B_, L, H, N // 2)
        theta_cumsum = jnp.cumsum(theta * dt[..., None], axis=1)
        Bm = rope(Bm, theta_cumsum)
        Cm = rope(Cm, theta_cumsum)
        xh = xp.reshape(B_, L, H, P)
        A = -jnp.exp(A_log)
        alpha = jnp.exp(dt * A)
        beta = (1.0 - lam) * dt * alpha
        gamma = lam * dt

        def step(carry, inputs):
            h, B_prev, x_prev = carry
            Bt, Ct, xt, at, bt, gt = inputs
            h = at[..., None, None] * h + jnp.einsum('bh,bhn,bhp->bhnp', bt, B_prev, x_prev) + jnp.einsum('bh,bhn,bhp->bhnp', gt, Bt, xt)
            yt = jnp.einsum('bhn,bhnp->bhp', Ct, h)
            return ((h, Bt, xt), yt)
        h0 = jnp.zeros((B_, H, N, P), x.dtype)
        carry0 = (h0, jnp.zeros((B_, H, N), x.dtype), jnp.zeros((B_, H, P), x.dtype))
        seq = (Bm.transpose(1, 0, 2, 3), Cm.transpose(1, 0, 2, 3), xh.transpose(1, 0, 2, 3), alpha.transpose(1, 0, 2), beta.transpose(1, 0, 2), gamma.transpose(1, 0, 2))
        _, ys = jax.lax.scan(step, carry0, seq)
        y = ys.transpose(1, 0, 2, 3).reshape(B_, L, H * P)
        y = y * jax.nn.silu(z)
        return y @ Wout.T

    def _L3_ffn_ref(x, gate_W_packed, gate_scales, up_W_packed, up_scales, down_W_packed, down_scales):
        import jax, jax.numpy as jnp
        import numpy as np
        BLOCK_SIZE = 32
        HIDDEN_SIZE = 256
        MLP_DIM = 2048
        NVFP4_LUT = jnp.array([0.0, 0.5, 1.0, 1.5, 2.0, 3.0, 4.0, 6.0, 0.0, -0.5, -1.0, -1.5, -2.0, -3.0, -4.0, -6.0], dtype=jnp.float32)

        def dequant_nvfp4(W_packed, scales, block=BLOCK_SIZE):
            N = W_packed.shape[0]
            low = W_packed & 15
            high = W_packed >> 4 & 15
            idx = jnp.stack([low, high], axis=-1).reshape(N, -1)
            vals = NVFP4_LUT[idx]
            K = vals.shape[1]
            vals = vals.reshape(N, K // block, block) * scales[:, :, None]
            return vals.reshape(N, K)
        B, S, H = x.shape
        xt = x.reshape(B * S, H)
        Wg = dequant_nvfp4(gate_W_packed, gate_scales)
        Wu = dequant_nvfp4(up_W_packed, up_scales)
        Wd = dequant_nvfp4(down_W_packed, down_scales)
        gate = jnp.einsum('th,nh->tn', xt, Wg)
        up = jnp.einsum('th,nh->tn', xt, Wu)
        gelu = jnp.tanh(0.7978845608028654 * (gate + 0.044715 * gate ** 3)) * gate * 0.5 + gate * 0.5
        inter = gelu * up
        out = jnp.einsum('tn,hn->th', inter, Wd)
        return out.reshape(B, S, H)
    x = x + _L0_xattn_ref(_layernorm(x, axis=-1), ctx_2048, L0_xattn_Wq, L0_xattn_bq, L0_xattn_Wkv, L0_xattn_bkv, L0_xattn_Wp, L0_xattn_bp)
    x = x + _L0_attn_ref(_layernorm(x, axis=-1), L0_attn_Wi, L0_attn_Wf, L0_attn_Wg, L0_attn_Wo, L0_attn_gnorm_w)
    x = x + _L0_ffn_ref(_layernorm(x, axis=-1), L0_ffn_gate_w, L0_ffn_w_gate, L0_ffn_w_up, L0_ffn_w_down, L0_ffn_sw_gate, L0_ffn_sw_up, L0_ffn_sw_down)
    x = x + _L1_xattn_ref(_layernorm(x, axis=-1), ctx_2048, mask_BxS2_bk0)
    x = x + _L1_attn_ref(_layernorm(x, axis=-1), L1_attn_w_qkv, L1_attn_w_out, L1_attn_decay_param)
    x = x + _L1_ffn_ref(_layernorm(x, axis=-1), L1_ffn_gamma, L1_ffn_beta, L1_ffn_mu, L1_ffn_scale, L1_ffn_W1, L1_ffn_b1, L1_ffn_W2, L1_ffn_b2)
    x = x + _L2_xattn_ref(_layernorm(x, axis=-1), ctx_2048, L2_xattn_Wq, L2_xattn_Wg, L2_xattn_bg, L2_xattn_Wkv, L2_xattn_Wo)
    x = x + _L2_attn_ref(_layernorm(x, axis=-1), L2_attn_Wq, L2_attn_bq, L2_attn_Wk, L2_attn_bk, L2_attn_Wv, L2_attn_bv, L2_attn_Wo, L2_attn_bo)
    x = x + _L2_ffn_ref(_layernorm(x, axis=-1), L2_ffn_W, L2_ffn_b, L2_ffn_lora_A, L2_ffn_lora_B, L2_ffn_gate_w, L2_ffn_gate_b)
    x = x + _L3_xattn_ref(_layernorm(x, axis=-1), ctx_2048, L3_xattn_Wq, L3_xattn_Wk, L3_xattn_Wv, L3_xattn_Wo, L3_xattn_q_norm_w, L3_xattn_k_norm_w, pos_BxS2, itok_BxS_4096_4607)
    x = x + _L3_attn_ref(_layernorm(x, axis=-1), L3_attn_Wx, L3_attn_Wz, L3_attn_WB, L3_attn_WC, L3_attn_Wdt, L3_attn_Wlam, L3_attn_Wth, L3_attn_A_log, L3_attn_Bn_w, L3_attn_Cn_w, L3_attn_B_bias, L3_attn_C_bias, L3_attn_Wout)
    x = x + _L3_ffn_ref(_layernorm(x, axis=-1), L3_ffn_gate_W_packed, L3_ffn_gate_scales, L3_ffn_up_W_packed, L3_ffn_up_scales, L3_ffn_down_W_packed, L3_ffn_down_scales)
    return x

_drawn_inputs = setup_inputs


def setup_inputs(seed=0):
    import zlib

    import numpy as np

    out = dict(_drawn_inputs(seed))
    spreads = {'L0_xattn_bq': (0.0, 0.8),
     'L0_xattn_bkv': (0.0, 0.1),
     'L0_xattn_bp': (0.0, 0.1),
     'L0_attn_gnorm_w': (1.0, 0.6),
     'L1_attn_decay_param': (0.949999988079071, 0.6),
     'L1_ffn_gamma': (1.0, 0.6),
     'L1_ffn_beta': (0.0, 0.383),
     'L1_ffn_b1': (0.0, 0.533),
     'L1_ffn_b2': (0.0, 0.427),
     'L2_xattn_bg': (1.0, 0.6),
     'L3_xattn_q_norm_w': (1.0, 0.6),
     'L3_xattn_k_norm_w': (1.0, 0.6),
     'L3_attn_Bn_w': (1.0, 0.6),
     'L3_attn_Cn_w': (1.0, 0.6),
     'L3_attn_B_bias': (1.0, 0.2),
     'L3_attn_C_bias': (1.0, 0.2)}
    factors = {'L0_xattn_Wq': 8.0,
     'L0_attn_Wf': 6.449,
     'L0_ffn_gate_w': 7.109,
     'L0_ffn_w_gate': 5.346,
     'L0_ffn_w_up': 5.379,
     'L0_ffn_w_down': 5.459,
     'L1_attn_w_qkv': 8.0,
     'L1_attn_w_out': 8.0,
     'L1_ffn_mu': 64.0,
     'L2_xattn_Wq': 10.697,
     'L2_attn_bq': 4.851,
     'L2_attn_bk': 5.431,
     'L2_ffn_b': 2.881,
     'L2_ffn_gate_b': 17.549,
     'L3_xattn_Wq': 2.704,
     'L3_xattn_Wk': 2.729,
     'L3_attn_Wdt': 64.0,
     'L3_attn_Wth': 3.088,
     'L0_ffn_sw_gate': 3.861,
     'L0_ffn_sw_up': 3.804,
     'L0_ffn_sw_down': 3.828}
    for name, (base, spread) in spreads.items():
        noise = np.random.default_rng([zlib.crc32(name.encode()), seed]).standard_normal(out[name].shape)
        drawn = base * np.exp(spread * noise) if base else spread * noise
        out[name] = jnp.asarray(drawn.astype(out[name].dtype))
    for name, factor in factors.items():
        out[name] = (out[name] * factor).astype(out[name].dtype)
    return out
```

```python
from contextlib import ExitStack, contextmanager

import numpy as np
import concourse.bass as bass
from concourse import mybir

ALU = mybir.AluOpType
ACT = mybir.ActivationFunctionType
AX = mybir.AxisListType
F32 = mybir.dt.float32
BF16 = mybir.dt.bfloat16
I32 = mybir.dt.int32

P = 128
B = 2
T = 128
D = 256
DC = D // P
BT = B * T
S2 = 2048
KEYS = B * S2
NKT = KEYS // P
LN_EPS = 1e-5
ROUND = float(3 * 2 ** 22)
NEG = -1e30


class Signals:

    def __init__(self, names, pool):
        self.of = dict(zip(names, pool))

    def __getattr__(self, name):
        return self.of[name]


@contextmanager
def signals(nc, pool, names):
    names = names.split()
    assert len(names) <= len(pool), len(names)
    yield Signals(names, pool)
    with nc.Block() as block:
        @block.sync
        def _(sp):
            for sem in pool[:len(names)]:
                sp.sem_clear(sem)


def chain(engine, sem):
    count = [0]

    def link(ins):
        count[0] += 1
        ins.then_inc(sem, 1)
        engine.wait_ge(sem, count[0])
    return link


class Core:

    def __init__(self, nc, ctx, A):
        self.nc, self.A, self.ctx = nc, A, ctx
        self.n = 0
        self.x = self.sb("x_res", [P, B, D])
        self.xn = self.sb("x_normed", [P, B, D])
        self.xt = self.sb("x_normed_T", [P, DC, BT])
        self.ident = self.sb("ident", [P, P])
        self.ones = self.sb("ones", [P, P])
        self.blocks = self.sb("head_blocks", [P, P])
        self.keep = self.sb("upper_incl", [P, P])
        self.ctxt = self.sb("ctx_T", [P, DC, KEYS])
        self.ctx_loaded = [ctx.enter_context(nc.semaphore(f"ctx_loaded_{i}")) for i in range(4)]
        self.stat = self.sb("ln_stats", [P, B, 6])
        self.mv = self.sb("ln_mean_var", [P, B, 2])
        self.rstd = self.sb("ln_rstd", [P, B, 2])
        self.ps = ctx.enter_context(nc.psum_tensor("banks", [P, 8, 512], F32))
        self.w_loaded = [ctx.enter_context(nc.semaphore(f"weights_loaded_{i}")) for i in range(12)]
        self.p_loaded = [ctx.enter_context(nc.semaphore(f"packed_loaded_{i}")) for i in range(4)]
        self.pool = [ctx.enter_context(nc.semaphore(f"signal_{i}")) for i in range(44)]

    def sb(self, name, shape, dt=F32, ctx=None):
        return (ctx or self.ctx).enter_context(self.nc.sbuf_tensor(name, shape, dt))

    def bank(self, i, p=P, n=512, a=0):
        return self.ps[0:p, i, a:a + n]


def constants(k, x_in):
    nc = k.nc
    with signals(nc, k.pool, "x_loaded filled") as s, nc.Block() as block:
        @block.sync
        def _(sp):
            sp.dma_start(k.x[:], x_in.rearrange("b t d -> t b d")).then_inc(s.x_loaded, 16)
            ctx_dram = k.A["ctxT"].rearrange("(c p) s -> p c s", p=P)
            for i in range(4):
                part = slice(i * KEYS // 4, (i + 1) * KEYS // 4)
                sp.dma_start(k.ctxt[:, :, part], ctx_dram[:, :, part]).then_inc(k.ctx_loaded[i], 16)
            sp.wait_ge(s.x_loaded, 16)

        @block.gpsimd
        def _(pool):
            nc.gpsimd.memset(k.ones[:], 1.0).then_inc(s.filled, 1)
            pool.wait_ge(s.filled, 1)
            nc.gpsimd.affine_select(out=k.ident[:], in_=k.ones[:], compare_op=ALU.is_equal, fill=0.0,
                                    base=0, pattern=[[-1, P]], channel_multiplier=1)
            nc.gpsimd.affine_select(out=k.keep[:], in_=k.ones[:], compare_op=ALU.is_ge, fill=0.0,
                                    base=0, pattern=[[1, P]], channel_multiplier=-1)
            heads = k.blocks[:].rearrange("p (h d) -> p h d", d=16)
            nc.gpsimd.affine_select(out=heads, in_=k.ones[:].rearrange("p (h d) -> p h d", d=16), compare_op=ALU.is_ge, fill=0.0,
                                    base=0, pattern=[[-16, P // 16], [0, 16]], channel_multiplier=1).then_inc(s.filled, 1)
            pool.wait_ge(s.filled, 2)
            nc.gpsimd.affine_select(out=heads, in_=heads, compare_op=ALU.is_ge, fill=0.0,
                                    base=15, pattern=[[16, P // 16], [0, 16]], channel_multiplier=-1)


def layernorm(k, load=None, n_loads=0):
    nc = k.nc
    with signals(nc, k.pool, "dve_step var_ready std_ready xn_ready xt_in_psum") as s, nc.Block() as block:
        @block.sync
        def _(sp):
            if load:
                load(sp)

        @block.vector
        def _(dve):
            link = chain(dve, s.dve_step)
            for b in range(B):
                nc.vector.bn_stats(k.stat[:, b, :], k.x[:, b, :]).then_inc(s.dve_step, 1)
            dve.wait_ge(s.dve_step, 2)
            for b in range(B):
                nc.vector.bn_aggr(k.mv[:, b, :], k.stat[:, b, :]).then_inc(s.dve_step, 1)
            dve.wait_ge(s.dve_step, 4)
            nc.vector.tensor_scalar(k.rstd[:, :, 0], k.mv[:, :, 1], LN_EPS, None, ALU.add).then_inc(s.var_ready, 1)
            dve.wait_ge(s.std_ready, 1)
            nc.vector.reciprocal(k.rstd[:, :, 0], k.rstd[:, :, 1]).then_inc(s.dve_step, 1)
            dve.wait_ge(s.dve_step, 5)
            for b in range(B):
                nc.vector.tensor_scalar(k.xn[:, b, :], k.x[:, b, :], k.mv[:, b, 0:1], k.rstd[:, b, 0:1],
                                        ALU.subtract, ALU.mult).then_inc(s.xn_ready, 1)

        @block.scalar
        def _(act):
            act.wait_ge(s.var_ready, 1)
            nc.scalar.activation(k.rstd[:, :, 1], k.rstd[:, :, 0], ACT.Sqrt).then_inc(s.std_ready, 1)
            act.wait_ge(s.xt_in_psum, 1)
            nc.scalar.copy(k.xt[:].rearrange("p c t -> p (c t)"), k.bank(0))

        @block.tensor
        def _(pe):
            for b in range(B):
                pe.wait_ge(s.xn_ready, b + 1)
                for c in range(DC):
                    last = nc.tensor.transpose(k.bank(0, P, T, c * BT + b * T),
                                               k.xn[:, b, c * P:(c + 1) * P], k.ident[:])
            last.then_inc(s.xt_in_psum, 1)


def matmul_acc(nc, out, pairs):
    for i, (lhsT, rhs) in enumerate(pairs):
        last = nc.tensor.matmul(out, lhsT, rhs, start=(i == 0), stop=(i == len(pairs) - 1))
    return last


HEADS = 16
HD = D // HEADS
LN255 = float(np.log(255.0))
TINY = 1e-8


def l0_xattn(k):
    nc, A = k.nc, k.A
    nh = HEADS
    with ExitStack() as ctx:
        def sb(name, shape, dt=F32):
            return k.sb("x0_" + name, shape, dt, ctx)
        wq, wkv, wp = sb("wq", [P, DC, D]), sb("wkv", [P, DC, 2 * D]), sb("wp", [P, DC, D])
        bq, bkv, bp = sb("bq", [P, D]), sb("bkv", [P, 2 * D]), sb("bp", [P, D])
        vf = sb("v_full", [P, NKT, D])
        vq = sb("v_int", [P, NKT, D], BF16)
        kt = sb("kT_parts", [P, nh // 2, KEYS], BF16)
        qt = sb("qT_int", [P, nh // 2, BT], BF16)
        kp = sb("k_parts", [P, 2, nh, 4, HD], BF16)
        qp = sb("q_parts", [P, B, nh, 4, HD], BF16)
        kf, kr = sb("k_full", [P, 2, D]), sb("k_rest", [P, 2, D])
        ks, kri = sb("k_scale", [P, 2, nh]), sb("k_rscale", [P, 2, nh])
        sq, qri = sb("q_scale", [P, B, nh]), sb("q_rscale", [P, B, nh])
        qf = sb("q_full", [P, B, D])
        vmax, vall, vri, vabs = sb("v_max", [P, D]), sb("v_scale", [P, D]), sb("v_rscale", [P, D]), sb("v_abs", [P, 2, D])
        identb = sb("identb", [P, P], BF16)
        mx, nb = sb("row_max4", [P, 2, 4]), sb("neg_max", [P, 2, 2])
        sums = sb("row_sum4", [P, 2, 4])
        rs = sb("row_sum", [P, 2, 2])
        pt = sb("probsT", [P, 2, 8, P], BF16)
        attn = sb("attn", [P, B, D])
        att = sb("attnT", [P, DC, BT])
        layernorm(k)
        scores = lambda r: k.ps[:, 2 * (r % 2):2 * (r % 2) + 2, :].rearrange("p a n -> p (a n)")
        exps = [vf[:, 0:16, :].rearrange("p a n -> p (a n)"), vf[:, 16:32, :].rearrange("p a n -> p (a n)")]

        names = ("dve_step w_loaded kv_in_psum kv_taken parts_ready kT_in_psum kT_taken "
                 "q_in_psum q_parts_ready qT_in_psum qT_taken vmax_ready vscale_ready v_ready "
                 "max_scores max_taken bias_ready exp_scores exp_done eT_in_psum pT_ready pv_done attn_ready "
                 "attnT_in_psum attnT_ready out_in_psum pool_step act_step pT_used zeroed")
        with signals(nc, k.pool, names) as s, nc.Block() as block:
            @block.sync
            def _(sp):
                for dst, src in ((wq, A["L0_xattn_Wq"]), (wkv, A["L0_xattn_Wkv"]), (wp, A["L0_xattn_Wp"])):
                    sp.dma_start(dst[:], src.rearrange("(c p) n -> p c n", p=P)).then_inc(s.w_loaded, 16)
                for dst, src, n in ((bq, A["L0_xattn_bq"], D), (bkv, A["L0_xattn_bkv"], 2 * D), (bp, A["L0_xattn_bp"], D)):
                    sp.dma_start(dst[:], src.rearrange("(a n) -> a n", a=1).to_broadcast([P, n])).then_inc(s.w_loaded, 16)

            @block.tensor
            def _(pe):
                pe.wait_ge(s.w_loaded, 96)
                for b in range(B):
                    last = matmul_acc(nc, k.bank(7, P, D, b * D), [(k.xt[:, c, b * T:(b + 1) * T], wq[:, c]) for c in range(DC)])
                last.then_inc(s.q_in_psum, 1)

                def transpose_keys(i):
                    pe.wait_ge(s.parts_ready, i + 1)
                    if i >= 2:
                        pe.wait_ge(s.kT_taken, i - 1)
                    tgt = k.ps[:, 4 + i % 2, :].bitcast(BF16)
                    for h in range(nh // 2):
                        last = nc.tensor.transpose(tgt[:, h * P:(h + 1) * P],
                                                   kp[:, i % 2, 2 * h:2 * h + 2].rearrange("p a c d -> p (a c d)"), identb[:])
                    last.then_inc(s.kT_in_psum, 1)
                for i in range(NKT):
                    if i % 8 == 0:
                        pe.wait_ge(k.ctx_loaded[i // 8], 16)
                    if i >= 4:
                        pe.wait_ge(s.kv_taken, 2 * (i - 3))
                    matmul_acc(nc, k.bank(i % 4), [(k.ctxt[:, c, i * P:(i + 1) * P], wkv[:, c]) for c in range(DC)]).then_inc(s.kv_in_psum, 1)
                    if i == 1:
                        pe.wait_ge(s.q_parts_ready, 1)
                        pe.wait_ge(s.zeroed, 1)
                        for b in range(B):
                            for h in range(nh // 2):
                                last = nc.tensor.transpose(k.ps[:, 6 + b, :].bitcast(BF16)[:, h * P:(h + 1) * P],
                                                           qp[:, b, 2 * h:2 * h + 2].rearrange("p a c d -> p (a c d)"), identb[:])
                        last.then_inc(s.qT_in_psum, 1)
                    if i >= 2:
                        transpose_keys(i - 2)
                transpose_keys(NKT - 2)
                transpose_keys(NKT - 1)

                def score_chunk(u, c):
                    b, h = divmod(u, nh)
                    lo = 64 * (h % 2)
                    for j in range(2):
                        a = (2 * c + j) * 512
                        last = nc.tensor.matmul(k.bank(2 * (c % 2) + j), qt[lo:lo + 64, h // 2, b * T:(b + 1) * T],
                                                kt[lo:lo + 64, h // 2, a:a + 512], start=True, stop=True)
                    return last

                def pv(v, g):
                    b, h = divmod(v, nh)
                    n = 8 * v + g
                    pe.wait_ge(s.pT_ready, n + 1)
                    if g == 0 and v >= 2:
                        pe.wait_ge(s.attn_ready, v - 1)
                    for j in range(4):
                        i = 4 * g + j
                        last = nc.tensor.matmul(k.bank(6 + v % 2, P, HD), pt[:, n % 2, j, :], vq[:, i, h * HD:(h + 1) * HD],
                                                start=(i == 0), stop=(i == NKT - 1))
                    last.then_inc(s.pT_used, 1)

                pe.wait_ge(s.kT_taken, NKT)
                pe.wait_ge(s.qT_taken, 1)
                pe.wait_ge(s.kv_taken, 2 * NKT)
                for u in range(B * nh + 1):
                    if u < B * nh:
                        for c in range(4):
                            if c >= 2:
                                pe.wait_ge(s.max_taken, 4 * u + c - 1)
                            elif u >= 2:
                                pe.wait_ge(s.exp_done, 4 * (u - 2) + c + 3)
                            elif u == 1:
                                pe.wait_ge(s.max_taken, 3 + c)
                            score_chunk(u, c).then_inc(s.max_scores, 1)
                    if u == 0:
                        continue
                    v = u - 1
                    for c in range(4):
                        if c >= 2:
                            pe.wait_ge(s.exp_done, 4 * v + c - 1)
                        elif u < B * nh:
                            pe.wait_ge(s.max_taken, 4 * u + c + 3)
                        else:
                            pe.wait_ge(s.exp_done, 4 * (v - 1) + c + 3)
                        score_chunk(v, c).then_inc(s.exp_scores, 1)
                    for g in range(8):
                        if g % 2 == 0:
                            pe.wait_ge(s.exp_done, 4 * v + g // 2 + 1)
                        n = 8 * v + g
                        if n >= 2:
                            pe.wait_ge(s.pT_ready, n - 1)
                        for j in range(4):
                            a = (4 * g + j) * P
                            last = nc.tensor.transpose(k.bank(4 + g % 2, P, P, j * P), exps[v % 2][:, a:a + P], k.ident[:])
                        last.then_inc(s.eT_in_psum, 1)
                        if g >= 1:
                            pv(v, g - 1)
                    pv(v, 7)
                for b in range(B):
                    pe.wait_ge(s.attn_ready, nh * (b + 1))
                    for c in range(DC):
                        last = nc.tensor.transpose(k.bank(0, P, T, c * BT + b * T), attn[:, b, c * P:(c + 1) * P], k.ident[:])
                last.then_inc(s.attnT_in_psum, 1)
                pe.wait_ge(s.attnT_ready, 1)
                for b in range(B):
                    last = matmul_acc(nc, k.bank(1, P, D, b * D), [(att[:, c, b * T:(b + 1) * T], wp[:, c]) for c in range(DC)])
                last.then_inc(s.out_in_psum, 1)

            @block.gpsimd
            def _(pool):
                pool.memset(kp[:], 0.0)
                pool.memset(qp[:], 0.0)
                nc.gpsimd.tensor_copy(identb[:], k.ident[:]).then_inc(s.zeroed, 1)
                pool.wait_ge(s.vmax_ready, 1)
                nc.gpsimd.partition_all_reduce(vall[:], vmax[:], P, bass.bass_isa.ReduceOp.max).then_inc(s.vscale_ready, 1)

            @block.scalar
            def _(act):
                for i in range(NKT):
                    act.wait_ge(s.kT_in_psum, i + 1)
                    nc.scalar.copy(kt[:, :, i * P:(i + 1) * P],
                                   k.ps[:, 4 + i % 2, :].bitcast(BF16).rearrange("p (h n) -> p h n", n=P)).then_inc(s.kT_taken, 1)
                    if i == 0:
                        act.wait_ge(s.qT_in_psum, 1)
                        for b in range(B):
                            last = nc.scalar.copy(qt[:, :, b * T:(b + 1) * T],
                                                  k.ps[:, 6 + b, :].bitcast(BF16).rearrange("p (h n) -> p h n", n=P))
                        last.then_inc(s.qT_taken, 1)
                act.wait_ge(s.v_ready, 1)
                for v in range(B * nh):
                    b, h = divmod(v, nh)
                    act.wait_ge(s.bias_ready, v + 1)
                    if v >= 2:
                        act.wait_ge(s.eT_in_psum, 8 * (v - 1))
                        act.wait_ge(s.attn_ready, v - 1)
                    for c in range(4):
                        act.wait_ge(s.exp_scores, 4 * v + c + 1)
                        nc.scalar.activation(exps[v % 2][:, c * 1024:(c + 1) * 1024], scores(c), ACT.Exp,
                                             bias=nb[:, v % 2, 1:2], scale=sq[:, b, h:h + 1],
                                             accum_out=sums[:, v % 2, c:c + 1]).then_inc(s.exp_done, 1)
                act.wait_ge(s.attnT_in_psum, 1)
                nc.scalar.copy(att[:].rearrange("p c t -> p (c t)"), k.bank(0)).then_inc(s.attnT_ready, 1)

            @block.vector
            def _(dve):
                link = chain(dve, s.dve_step)

                def quantise(full, scale, rscale, n=nh):
                    link(nc.vector.tensor_reduce(scale, full, AX.X, ALU.max, apply_absolute_value=True))
                    link(nc.vector.tensor_scalar(scale, scale, 1.0 / 127.0, TINY, ALU.mult, ALU.max))
                    link(nc.vector.reciprocal(rscale, scale))
                    link(nc.vector.tensor_tensor(full, full, rscale.unsqueeze(2).to_broadcast([P, n, HD]), ALU.mult))
                    link(nc.vector.tensor_scalar(full, full, ROUND, ROUND, ALU.add, ALU.subtract))

                dve.wait_ge(s.q_in_psum, 1)
                dve.wait_ge(s.w_loaded, 96)
                dve.wait_ge(s.zeroed, 1)
                for b in range(B):
                    link(nc.vector.tensor_tensor(qf[:, b], k.bank(7, P, D, b * D), bq[:], ALU.add))
                    link(nc.vector.tensor_scalar(qf[:, b], qf[:, b], 1.0 / float(np.sqrt(np.float32(HD))), None, ALU.mult))
                    q3 = qf[:, b].rearrange("p (h d) -> p h d", d=HD)
                    quantise(q3, sq[:, b], qri[:, b])
                    for c in range(3):
                        last = nc.vector.tensor_copy(qp[:, b, :, c, :], q3)
                last.then_inc(s.q_parts_ready, 1)
                link(nc.vector.memset(vmax[:], 0.0))
                for i in range(NKT):
                    r = i % 2
                    dve.wait_ge(s.kv_in_psum, i + 1)
                    nc.vector.tensor_tensor(vf[:, i], k.bank(i % 4, P, D, D), bkv[:, D:], ALU.add).then_inc(s.kv_taken, 1)
                    nc.vector.tensor_tensor(kf[:, r], k.bank(i % 4, P, D), bkv[:, 0:D], ALU.add).then_inc(s.kv_taken, 1)
                    dve.wait_ge(s.kv_taken, 2 * (i + 1))
                    k3 = kf[:, r].rearrange("p (h d) -> p h d", d=HD)
                    r3 = kr[:, r].rearrange("p (h d) -> p h d", d=HD)
                    link(nc.vector.scalar_tensor_tensor(out=vabs[:, 0], in0=vf[:, i], scalar=-1.0, in1=vf[:, i], op0=ALU.mult, op1=ALU.max))
                    link(nc.vector.tensor_tensor(vmax[:], vmax[:], vabs[:, 0], ALU.max))
                    quantise(k3, ks[:, r], kri[:, r])
                    link(nc.vector.tensor_tensor(k3, k3, ks[:, r].unsqueeze(2).to_broadcast([P, nh, HD]), ALU.mult))
                    if i >= 2:
                        dve.wait_ge(s.kT_in_psum, i - 1)
                    link(nc.vector.tensor_copy(kp[:, r, :, 0, :], k3))
                    link(nc.vector.tensor_tensor(r3, k3, kp[:, r, :, 0, :], ALU.subtract))
                    link(nc.vector.tensor_copy(kp[:, r, :, 1, :], r3))
                    link(nc.vector.tensor_tensor(r3, r3, kp[:, r, :, 1, :], ALU.subtract))
                    nc.vector.tensor_copy(kp[:, r, :, 2, :], r3).then_inc(s.parts_ready, 1)
                dve.sem_inc(s.vmax_ready, 1)
                dve.wait_ge(s.vscale_ready, 1)
                link(nc.vector.tensor_scalar(vall[:], vall[:], 1.0 / 127.0, TINY, ALU.mult, ALU.max))
                link(nc.vector.reciprocal(vri[:], vall[:]))
                for g in range(4):
                    v3 = vf[:, 8 * g:8 * g + 8, :]
                    link(nc.vector.tensor_tensor(v3, v3, vri[:].unsqueeze(1).to_broadcast([P, 8, D]), ALU.mult))
                    link(nc.vector.tensor_scalar(vq[:, 8 * g:8 * g + 8, :], v3, ROUND, ROUND, ALU.add, ALU.subtract))
                dve.sem_inc(s.v_ready, 1)

                for u in range(B * nh + 1):
                    if u < B * nh:
                        b, h = divmod(u, nh)
                        for c in range(4):
                            dve.wait_ge(s.max_scores, 4 * u + c + 1)
                            nc.vector.reduce_max(mx[:, u % 2, c:c + 1], scores(c), AX.X).then_inc(s.max_taken, 1)
                        dve.wait_ge(s.max_taken, 4 * u + 4)
                        link(nc.vector.reduce_max(nb[:, u % 2, 0:1], mx[:, u % 2, :], AX.X))
                        link(nc.vector.tensor_tensor(nb[:, u % 2, 0:1], nb[:, u % 2, 0:1], sq[:, b, h:h + 1], ALU.mult))
                        nc.vector.tensor_scalar(nb[:, u % 2, 1:2], nb[:, u % 2, 0:1], -1.0, LN255, ALU.mult, ALU.add).then_inc(s.bias_ready, 1)
                    if u == 0:
                        continue
                    v = u - 1
                    b, h = divmod(v, nh)
                    for g in range(8):
                        n = 8 * v + g
                        dve.wait_ge(s.eT_in_psum, n + 1)
                        if n >= 2:
                            dve.wait_ge(s.pT_used, n - 1)
                        nc.vector.tensor_scalar(pt[:, n % 2, 0:4].rearrange("p a n -> p (a n)"), k.bank(4 + g % 2), ROUND, ROUND,
                                                ALU.add, ALU.subtract).then_inc(s.pT_ready, 1)
                    link(nc.vector.reduce_sum(rs[:, v % 2, 0:1], sums[:, v % 2, :], AX.X))
                    link(nc.vector.reciprocal(rs[:, v % 2, 1:2], rs[:, v % 2, 0:1]))
                    dve.wait_ge(s.pT_used, 8 * v + 8)
                    nc.vector.scalar_tensor_tensor(out=attn[:, b, h * HD:(h + 1) * HD], in0=k.bank(6 + v % 2, P, HD),
                                                   scalar=rs[:, v % 2, 1:2], in1=vall[:, h * HD:(h + 1) * HD],
                                                   op0=ALU.mult, op1=ALU.mult).then_inc(s.attn_ready, 1)
                for b in range(B):
                    link(nc.vector.tensor_tensor(k.x[:, b], k.x[:, b], bp[:], ALU.add))
                dve.wait_ge(s.out_in_psum, 1)
                for b in range(B):
                    nc.vector.tensor_tensor(k.x[:, b], k.x[:, b], k.bank(1, P, D, b * D), ALU.add)


def l0_attn(k):
    nc, A = k.nc, k.A
    with ExitStack() as ctx:
        def sb(name, shape, dt=F32):
            return k.sb("a0_" + name, shape, dt, ctx)
        w = [sb("w" + n, [P, DC, D]) for n in "ifgo"]
        gw = sb("gnorm", [P, DC])
        gate, v, sig_i = sb("gate", [P, DC, BT]), sb("v", [P, DC, BT]), sb("sig_i", [P, DC, BT])
        sig_g, o, o2 = sb("sig_g", [P, DC, BT]), sb("o", [P, DC, BT]), sb("o2", [P, DC, BT])
        rms = sb("rms", [P, 2, BT])
        flat = lambda t: t[:].rearrange("p c t -> p (c t)")

        def load(sp):
            for t, n in zip(w, "ifgo"):
                sp.dma_start(t[:], A["L0_attn_W" + n + "_T"].rearrange("(c p) n -> p c n", p=P)).then_inc(k.w_loaded[1], 16)
            sp.dma_start(gw[:], A["L0_attn_gnorm_w"].rearrange("(c p) -> p c", p=P), allow_slow_non_contiguous=True).then_inc(k.w_loaded[1], 16)
        layernorm(k, load)
        with signals(nc, k.pool, "dve_step proj_ready sig_ready scan_ready act_step ms_in_psum var_ready std_ready o_ready out_ready") as s, \
                nc.Block() as block:
            @block.tensor
            def _(pe):
                pe.wait_ge(k.w_loaded[1], 80)
                for j in (1, 0, 2):
                    for m in range(DC):
                        last = matmul_acc(nc, k.bank(j, P, BT, m * BT),
                                          [(w[j][:, c, m * P:(m + 1) * P], k.xt[:, c]) for c in range(DC)])
                    last.then_inc(s.proj_ready, 1)
                pe.wait_ge(s.act_step, 1)
                matmul_acc(nc, k.bank(3, P, BT), [(k.ones[:], o2[:, c]) for c in range(DC)]).then_inc(s.ms_in_psum, 1)
                pe.wait_ge(s.o_ready, 1)
                for b in range(B):
                    last = matmul_acc(nc, k.bank(4, P, D, b * D), [(o[:, c, b * T:(b + 1) * T], w[3][:, c]) for c in range(DC)])
                last.then_inc(s.out_ready, 1)

            @block.scalar
            def _(act):
                act.wait_ge(s.proj_ready, 1)
                nc.scalar.activation(flat(gate), k.bank(1), ACT.Sigmoid).then_inc(s.sig_ready, 1)
                nc.scalar.activation(flat(v), k.bank(1), ACT.Sigmoid, scale=-1.0).then_inc(s.sig_ready, 1)
                act.wait_ge(s.proj_ready, 2)
                nc.scalar.activation(flat(sig_i), k.bank(0), ACT.Sigmoid).then_inc(s.sig_ready, 1)
                act.wait_ge(s.proj_ready, 3)
                nc.scalar.activation(flat(sig_g), k.bank(2), ACT.Sigmoid).then_inc(s.sig_ready, 1)
                act.wait_ge(s.scan_ready, 4)
                nc.scalar.activation(flat(o2), flat(o), ACT.Square).then_inc(s.act_step, 1)
                act.wait_ge(s.var_ready, 1)
                nc.scalar.activation(rms[:, 1], rms[:, 0], ACT.Sqrt).then_inc(s.std_ready, 1)

            @block.vector
            def _(dve):
                link = chain(dve, s.dve_step)
                dve.wait_ge(s.sig_ready, 3)
                link(nc.vector.tensor_tensor(flat(sig_i), flat(sig_i), k.bank(0), ALU.mult))
                link(nc.vector.tensor_tensor(flat(v), flat(v), flat(sig_i), ALU.mult))
                for c in range(DC):
                    for b in range(B):
                        sl = slice(b * T, (b + 1) * T)
                        nc.vector.tensor_tensor_scan(o[:, c, sl], gate[:, c, sl], v[:, c, sl], 0.0, ALU.mult, ALU.add).then_inc(s.scan_ready, 1)
                dve.wait_ge(s.sig_ready, 4)
                link(nc.vector.tensor_tensor(flat(sig_g), flat(sig_g), k.bank(2), ALU.mult))
                for c in range(DC):
                    link(nc.vector.tensor_scalar(sig_g[:, c], sig_g[:, c], gw[:, c:c + 1], None, ALU.mult))
                dve.wait_ge(s.ms_in_psum, 1)
                nc.vector.tensor_scalar(rms[:, 0], k.bank(3, P, BT), 1.0 / D, LN_EPS, ALU.mult, ALU.add).then_inc(s.var_ready, 1)
                dve.wait_ge(s.std_ready, 1)
                link(nc.vector.reciprocal(rms[:, 0], rms[:, 1]))
                link(nc.vector.tensor_tensor(flat(o), flat(o), flat(sig_g), ALU.mult))
                nc.vector.tensor_tensor(o[:], o[:], rms[:, 0].unsqueeze(1).to_broadcast([P, DC, BT]), ALU.mult).then_inc(s.o_ready, 1)
                dve.wait_ge(s.out_ready, 1)
                xf = k.x[:].rearrange("p b d -> p (b d)")
                nc.vector.tensor_tensor(xf, xf, k.bank(4), ALU.add)


EXPERTS = 16
TOPK = 4
INNER = 176
IH = INNER // 2
CAP = 128
SHARED = 2
RING = 6


def l0_ffn(k):
    nc, A = k.nc, k.A
    ne = EXPERTS + SHARED
    with ExitStack() as ctx:
        def sb(name, shape, dt=F32):
            return k.sb("f0_" + name, shape, dt, ctx)
        wg = sb("router", [P, DC, EXPERTS])
        wgu = sb("w_gate_up", [P, RING, DC, 2, INNER])
        wd = sb("w_down", [IH, RING, 2, D])
        mid = sb("mid", [IH, 2, 2, BT])
        sig = sb("sig", [IH, 2, 2, BT])
        prob = sb("prob", [P, B, 24])
        marked = sb("marked", [P, B, 24])
        top = sb("top", [P, B, 8])
        sel = sb("selected", [P, B, EXPERTS])
        wt = sb("weights", [P, B, ne])
        sm = sb("small", [P, B, 4])
        acc = sb("acc", [P, B, D])

        def load(sp):
            sp.dma_start(wg[:], A["L0_ffn_gate_w_T"].rearrange("(c p) n -> p c n", p=P)).then_inc(k.w_loaded[2], 16)
        layernorm(k, load)
        with signals(nc, k.pool, "dve_step " + " ".join(f"w_loaded_{r}" for r in range(RING)) +
                     " gu_in_psum gu_taken mid_ready out_in_psum out_taken sig_ready logits_ready max_ready exp_ready sel_ready count_ready") as s, \
                nc.Block() as block:
            ring_loaded = [s.of[f"w_loaded_{r}"] for r in range(RING)]

            @block.sync
            def _(sp):
                for e in range(ne):
                    if e >= RING:
                        sp.wait_ge(s.out_in_psum, e - RING + 1)
                    sp.dma_start(wgu[:, e % RING], A["L0_ffn_gate_up"][e]).then_inc(ring_loaded[e % RING], 16)
                    sp.dma_start(wd[:, e % RING], A["L0_ffn_down"][e]).then_inc(ring_loaded[e % RING], 16)

            @block.tensor
            def _(pe):
                pe.wait_ge(k.w_loaded[2], 16)
                for b in range(B):
                    last = matmul_acc(nc, k.bank(7, P, EXPERTS, b * EXPERTS),
                                      [(k.xt[:, c, b * T:(b + 1) * T], wg[:, c]) for c in range(DC)])
                last.then_inc(s.logits_ready, 1)

                def down(e):
                    pe.wait_ge(s.mid_ready, e + 1)
                    if e >= 2:
                        pe.wait_ge(s.out_taken, B * (e - 1))
                    for b in range(B):
                        last = matmul_acc(nc, k.bank(4 + e % 2, P, D, b * D),
                                          [(mid[:, e % 2, m, b * T:(b + 1) * T], wd[:, e % RING, m]) for m in range(2)])
                    last.then_inc(s.out_in_psum, 1)
                for e in range(ne):
                    pe.wait_ge(ring_loaded[e % RING], 32 * (e // RING + 1))
                    if e >= 2:
                        pe.wait_ge(s.mid_ready, e - 1)
                    for j in range(2):
                        for m in range(2):
                            last = matmul_acc(nc, k.bank(2 * (e % 2) + j, IH, BT, m * BT),
                                              [(wgu[:, e % RING, c, j, m * IH:(m + 1) * IH], k.xt[:, c]) for c in range(DC)])
                    last.then_inc(s.gu_in_psum, 1)
                    if e == 1:
                        pe.wait_ge(s.sel_ready, 1)
                        nc.tensor.matmul(k.bank(6, P, EXPERTS), k.keep[:], sel[:, 0], start=True, stop=True)
                        matmul_acc(nc, k.bank(6, P, EXPERTS, EXPERTS), [(k.ones[:], sel[:, 0]), (k.keep[:], sel[:, 1])]).then_inc(s.count_ready, 1)
                    if e >= 1:
                        down(e - 1)
                down(ne - 1)

            @block.scalar
            def _(act):
                act.wait_ge(s.max_ready, B)
                for b in range(B):
                    nc.scalar.activation(prob[:, b, 0:EXPERTS], k.bank(7, P, EXPERTS, b * EXPERTS), ACT.Exp, bias=sm[:, b, 0:1],
                                         accum_out=sm[:, b, 1:2]).then_inc(s.exp_ready, 1)
                for e in range(ne):
                    act.wait_ge(s.gu_in_psum, e + 1)
                    if e >= 2:
                        act.wait_ge(s.mid_ready, e - 1)
                    nc.scalar.activation(sig[:, e % 2].rearrange("p a n -> p (a n)"), k.bank(2 * (e % 2), IH), ACT.Sigmoid).then_inc(s.sig_ready, 1)

            @block.vector
            def _(dve):
                link = chain(dve, s.dve_step)
                for b in range(B):
                    nc.vector.memset(wt[:, b, EXPERTS:ne], 1.0)
                    for j in range(4):
                        nc.vector.memset(prob[:, b, EXPERTS + j:EXPERTS + j + 1], -1.0 - j)
                    link(nc.vector.memset(prob[:, b, EXPERTS + 4:24], -9.0))
                dve.wait_ge(s.logits_ready, 1)
                for b in range(B):
                    link(nc.vector.reduce_max(sm[:, b, 2:3], k.bank(7, P, EXPERTS, b * EXPERTS), AX.X))
                    nc.vector.tensor_scalar(sm[:, b, 0:1], sm[:, b, 2:3], -1.0, None, ALU.mult).then_inc(s.max_ready, 1)
                dve.wait_ge(s.exp_ready, B)
                for b in range(B):
                    link(nc.vector.reciprocal(sm[:, b, 2:3], sm[:, b, 1:2]))
                    link(nc.vector.tensor_scalar(prob[:, b, 0:EXPERTS], prob[:, b, 0:EXPERTS], sm[:, b, 2:3], None, ALU.mult))
                    link(nc.vector.max(top[:, b], prob[:, b]))
                    for j in range(4):
                        nc.vector.memset(top[:, b, 4 + j:5 + j], -1.0 - j)
                    link(nc.vector.memset(sm[:, b, 3:4], 0.0))
                    link(nc.vector.match_replace(marked[:, b], top[:, b], prob[:, b], -5.0))
                    ins = nc.vector.tensor_scalar(sel[:, b], marked[:, b, 0:EXPERTS], -5.0, None, ALU.is_equal)
                    link(ins)
                dve.sem_inc(s.sel_ready, 1)
                for b in range(B):
                    link(nc.vector.tensor_tensor(wt[:, b, 0:EXPERTS], prob[:, b, 0:EXPERTS], sel[:, b], ALU.mult))
                    link(nc.vector.reduce_sum(sm[:, b, 2:3], wt[:, b, 0:EXPERTS], AX.X))
                    link(nc.vector.tensor_scalar(sm[:, b, 2:3], sm[:, b, 2:3], 1e-20, None, ALU.add))
                    link(nc.vector.reciprocal(sm[:, b, 3:4], sm[:, b, 2:3]))
                    link(nc.vector.tensor_scalar(wt[:, b, 0:EXPERTS], wt[:, b, 0:EXPERTS], sm[:, b, 3:4], None, ALU.mult))
                def capacity():
                    dve.wait_ge(s.count_ready, 1)
                    for b in range(B):
                        link(nc.vector.tensor_scalar(sel[:, b], k.bank(6, P, EXPERTS, b * EXPERTS), float(CAP), None, ALU.is_le))
                        link(nc.vector.tensor_tensor(wt[:, b, 0:EXPERTS], wt[:, b, 0:EXPERTS], sel[:, b], ALU.mult))

                def take(e):
                    dve.wait_ge(s.out_in_psum, e + 1)
                    for b in range(B):
                        if e >= 1:
                            dve.wait_ge(s.out_taken, B * (e - 1) + b + 1)
                        base = k.x if e == 0 else acc
                        out = k.x if e == ne - 1 else acc
                        nc.vector.scalar_tensor_tensor(out=out[:, b], in0=k.bank(4 + e % 2, P, D, b * D), scalar=wt[:, b, e:e + 1],
                                                       in1=base[:, b], op0=ALU.mult, op1=ALU.add).then_inc(s.out_taken, 1)
                for e in range(ne):
                    dve.wait_ge(s.sig_ready, e + 1)
                    sg = sig[:, e % 2].rearrange("p a n -> p (a n)")
                    link(nc.vector.tensor_tensor(sg, sg, k.bank(2 * (e % 2), IH), ALU.mult))
                    if e >= 2:
                        dve.wait_ge(s.out_in_psum, e - 1)
                    nc.vector.tensor_tensor(mid[:, e % 2].rearrange("p a n -> p (a n)"), sg, k.bank(2 * (e % 2) + 1, IH), ALU.mult).then_inc(s.mid_ready, 1)
                    if e == 1:
                        capacity()
                    if e >= 1:
                        take(e - 1)
                take(ne - 1)


def l1_xattn(k):
    nc, A = k.nc, k.A
    nt = S2 // P
    with ExitStack() as ctx:
        def sb(name, shape, dt=F32):
            return k.sb("x1_" + name, shape, dt, ctx)
        val = sb("ctx_tokens", [P, B, nt, D])
        mask8 = sb("mask8", [P, B, S2], mybir.dt.uint8)
        mask = sb("mask", [P, B, S2])
        bias = sb("mask_bias", [P, B, S2])
        sc = sb("scores", [P, B, S2])
        pt = sb("probsT", [P, B, nt, P])
        sm = sb("small", [P, B, 8])

        def load(sp):
            sp.dma_start(mask8[:], A["mask_BxS2_bk0"].rearrange("(a b) s -> a b s", a=1).to_broadcast([P, B, S2])).then_inc(k.w_loaded[3], 16)
            for b in range(B):
                sp.dma_start(val[:, b], A["ctx_2048"][b].rearrange("(n p) d -> p n d", p=P)).then_inc(k.w_loaded[3], 16)
        layernorm(k, load)
        with signals(nc, k.pool, "dve_step scores_ready masked_ready exp_ready tr_ready tr_taken out_ready max_ready mask_ready") as s, \
                nc.Block() as block:
            @block.tensor
            def _(pe):
                for loaded in k.ctx_loaded:
                    pe.wait_ge(loaded, 16)
                for b in range(B):
                    for j in range(4):
                        a = b * S2 + j * 512
                        matmul_acc(nc, k.bank(4 * b + j), [(k.xt[:, c, b * T:(b + 1) * T], k.ctxt[:, c, a:a + 512]) for c in range(DC)]
                                   ).then_inc(s.scores_ready, 1)
                for b in range(B):
                    pe.wait_ge(s.exp_ready, b + 1)
                    for g in range(4):
                        n = 4 * b + g
                        if n >= 2:
                            pe.wait_ge(s.tr_taken, n - 1)
                        for j in range(4):
                            i = 4 * g + j
                            last = nc.tensor.transpose(k.bank(n % 2, P, P, j * P), sc[:, b, i * P:(i + 1) * P], k.ident[:])
                        last.then_inc(s.tr_ready, 1)
                    pe.wait_ge(k.w_loaded[3], 48)
                    for i in range(nt):
                        if i % 4 == 0:
                            pe.wait_ge(s.tr_taken, 4 * b + i // 4 + 1)
                        last = nc.tensor.matmul(k.bank(2 + b, P, D), pt[:, b, i], val[:, b, i], start=(i == 0), stop=(i == nt - 1))
                    last.then_inc(s.out_ready, 1)

            @block.scalar
            def _(act):
                for b in range(B):
                    act.wait_ge(s.max_ready, b + 1)
                    nc.scalar.activation(sc[:, b], sc[:, b], ACT.Exp, bias=sm[:, b, 0:1], accum_out=sm[:, b, 1:2]).then_inc(s.exp_ready, 1)

            @block.gpsimd
            def _(pool):
                pool.wait_ge(k.w_loaded[3], 48)
                nc.gpsimd.tensor_copy(mask[:], mask8[:]).then_inc(s.mask_ready, 1)
                pool.wait_ge(s.mask_ready, 1)
                nc.gpsimd.tensor_scalar(bias[:], mask[:], -NEG, NEG, ALU.mult, ALU.add).then_inc(s.mask_ready, 1)

            @block.vector
            def _(dve):
                link = chain(dve, s.dve_step)
                dve.wait_ge(s.mask_ready, 2)
                for b in range(B):
                    for j in range(4):
                        dve.wait_ge(s.scores_ready, 4 * b + j + 1)
                        sl = slice(j * 512, (j + 1) * 512)
                        nc.vector.scalar_tensor_tensor(out=sc[:, b, sl], in0=k.bank(4 * b + j), scalar=1.0 / float(np.sqrt(D)),
                                                       in1=mask[:, b, sl], op0=ALU.mult, op1=ALU.mult).then_inc(s.masked_ready, 1)
                    dve.wait_ge(s.masked_ready, 4 * (b + 1))
                    link(nc.vector.tensor_tensor(sc[:, b], sc[:, b], bias[:, b], ALU.add))
                    link(nc.vector.reduce_max(sm[:, b, 2:3], sc[:, b], AX.X))
                    nc.vector.tensor_scalar(sm[:, b, 0:1], sm[:, b, 2:3], -1.0, None, ALU.mult).then_inc(s.max_ready, 1)
                    link(nc.vector.reduce_max(sm[:, b, 3:4], mask[:, b], AX.X))
                for b in range(B):
                    dve.wait_ge(s.exp_ready, b + 1)
                    link(nc.vector.reciprocal(sm[:, b, 4:5], sm[:, b, 1:2]))
                    link(nc.vector.tensor_tensor(sm[:, b, 5:6], sm[:, b, 4:5], sm[:, b, 3:4], ALU.mult))
                    for g in range(4):
                        n = 4 * b + g
                        dve.wait_ge(s.tr_ready, n + 1)
                        nc.vector.tensor_copy(pt[:, b, 4 * g:4 * g + 4].rearrange("p a n -> p (a n)"), k.bank(n % 2)).then_inc(s.tr_taken, 1)
                for b in range(B):
                    dve.wait_ge(s.out_ready, b + 1)
                    nc.vector.scalar_tensor_tensor(out=k.x[:, b], in0=k.bank(2 + b, P, D), scalar=sm[:, b, 5:6], in1=k.x[:, b],
                                                   op0=ALU.mult, op1=ALU.add)


def l1_attn(k):
    nc, A = k.nc, k.A
    with ExitStack() as ctx:
        def sb(name, shape, dt=F32):
            return k.sb("a1_" + name, shape, dt, ctx)
        wqkv, wo = sb("w_qkv", [P, DC, 3 * D]), sb("w_out", [P, DC, D])
        dec = sb("decay", [P, DC, 2])
        low, ex = sb("low", [P, 2, DC * BT]), sb("ex", [P, 2, DC * BT])
        q, kk, kv = sb("q", [P, DC, BT]), sb("k", [P, DC, BT]), sb("kv", [P, DC, BT])
        rkv, rk = sb("run_kv", [P, DC, BT]), sb("run_k", [P, DC, BT])
        flat = lambda t: t[:].rearrange("p c t -> p (c t)")

        def load(sp):
            sp.dma_start(dec[:, :, 0:1], A["L1_decay_ch"].rearrange("(c p a) -> p c a", p=P, a=1), allow_slow_non_contiguous=True).then_inc(k.w_loaded[4], 16)
            sp.dma_start(wqkv[:], A["L1_attn_w_qkv"].rearrange("(c p) n -> p c n", p=P)).then_inc(k.w_loaded[4], 16)
            sp.dma_start(wo[:], A["L1_attn_w_out"].rearrange("(c p) n -> p c n", p=P)).then_inc(k.w_loaded[4], 16)
        layernorm(k, load)
        with signals(nc, k.pool, "dve_step proj_ready low_ready exp_ready dec_ready scanned den_in_psum den_ready o_ready out_ready fm_ready") as s, \
                nc.Block() as block:
            @block.tensor
            def _(pe):
                pe.wait_ge(k.w_loaded[4], 48)
                for j in (1, 0, 2):
                    for m in range(DC):
                        a = j * D + m * P
                        last = matmul_acc(nc, k.bank(j, P, BT, m * BT), [(wqkv[:, c, a:a + P], k.xt[:, c]) for c in range(DC)])
                    last.then_inc(s.proj_ready, 1)
                pe.wait_ge(s.den_ready, 1)
                for m in range(DC):
                    last = nc.tensor.matmul(k.bank(3, P, BT, m * BT), k.blocks[:], rk[:, m], start=True, stop=True)
                last.then_inc(s.den_in_psum, 1)
                pe.wait_ge(s.o_ready, 1)
                for b in range(B):
                    last = matmul_acc(nc, k.bank(4, P, D, b * D), [(rkv[:, c, b * T:(b + 1) * T], wo[:, c]) for c in range(DC)])
                last.then_inc(s.out_ready, 1)

            @block.scalar
            def _(act):
                act.wait_ge(k.w_loaded[4], 48)
                nc.scalar.activation(dec[:, :, 1], dec[:, :, 0], ACT.Sigmoid).then_inc(s.dec_ready, 1)
                for j in range(2):
                    act.wait_ge(s.low_ready, j + 1)
                    nc.scalar.activation(ex[:, j], low[:, j], ACT.Exp).then_inc(s.exp_ready, 1)

            @block.vector
            def _(dve):
                link = chain(dve, s.dve_step)
                for j, bank in ((0, 1), (1, 0)):
                    dve.wait_ge(s.proj_ready, j + 1)
                    nc.vector.tensor_scalar(low[:, j], k.bank(bank), 0.0, None, ALU.min).then_inc(s.low_ready, 1)
                for j, bank, dst in ((0, 1, kk), (1, 0, q)):
                    dve.wait_ge(s.exp_ready, j + 1)
                    link(nc.vector.scalar_tensor_tensor(out=flat(dst), in0=k.bank(bank), scalar=0.0, in1=ex[:, j],
                                                        op0=ALU.max, op1=ALU.add))
                dve.wait_ge(s.proj_ready, 3)
                link(nc.vector.tensor_tensor(flat(kv), flat(kk), k.bank(2), ALU.mult))
                dve.wait_ge(s.dec_ready, 1)
                for src, dst in ((kk, rk), (kv, rkv)):
                    for c in range(DC):
                        for b in range(B):
                            sl = slice(b * T, (b + 1) * T)
                            nc.vector.tensor_tensor_scan(dst[:, c, sl], dec[:, c, 1:2].to_broadcast([P, T]), src[:, c, sl], 0.0,
                                                         ALU.mult, ALU.add).then_inc(s.scanned, 1)
                dve.wait_ge(s.scanned, 8)
                nc.vector.tensor_tensor(flat(rk), flat(rk), flat(q), ALU.mult).then_inc(s.den_ready, 1)
                link(nc.vector.tensor_tensor(flat(rkv), flat(rkv), flat(q), ALU.mult))
                dve.wait_ge(s.den_in_psum, 1)
                link(nc.vector.tensor_scalar(flat(kk), k.bank(3), 1e-6, None, ALU.max))
                link(nc.vector.reciprocal(flat(kv), flat(kk)))
                nc.vector.tensor_tensor(flat(rkv), flat(rkv), flat(kv), ALU.mult).then_inc(s.o_ready, 1)
                dve.wait_ge(s.out_ready, 1)
                xf = k.x[:].rearrange("p b d -> p (b d)")
                nc.vector.tensor_tensor(xf, xf, k.bank(4), ALU.add)


L2_EPS = 1e-12
SLOTS = 128
HID = 64


def l1_ffn(k):
    nc, A = k.nc, k.A
    ne = EXPERTS
    ns = ne * SLOTS
    with ExitStack() as ctx:
        def sb(name, shape, dt=F32):
            return k.sb("f1_" + name, shape, dt, ctx)
        mu = sb("mu", [P, DC, ns])
        w1, w2 = sb("w1", [P, DC, ne, HID]), sb("w2", [HID, ne, D])
        b1 = sb("b1", [HID, ne])
        b2 = sb("b2", [P, 2, D])
        gam, bet, sca = sb("gamma", [P, D]), sb("beta", [P, D]), sb("scale", [P, 1])
        xl = sb("x_ln", [P, B, D])
        xs = sb("x_l2", [P, B, D])
        xst = sb("x_l2_T", [P, DC, BT])
        sq, rn = sb("sq", [P, 2, 512]), sb("rn", [P, 2, 512])
        comb = sb("combine", [P, B, ns])
        disp = sb("disp", [P, 2, BT])
        dtk = sb("disp_tok", [P, 2, BT])
        ct = sb("combT", [P, 2, BT])
        slot = sb("slotT", [P, 2, DC, BT])
        ht, so = sb("hT", [HID, 2, BT]), sb("slot_out", [P, 2, B, D])
        sm = sb("small", [P, B, 12])
        dm = sb("disp_small", [P, 2, B, 4])

        def load(sp):
            for t, n in ((gam, "gamma"), (bet, "beta")):
                sp.dma_start(t[:], A["L1_ffn_" + n].rearrange("(a n) -> a n", a=1).to_broadcast([P, D])).then_inc(k.w_loaded[5], 16)
            sp.dma_start(sca[:], A["L1_ffn_scale"].rearrange("(a n) -> a n", a=1).to_broadcast([P, 1])).then_inc(k.w_loaded[5], 16)
            sp.dma_start(b1[:], A["L1_ffn_b1_T"]).then_inc(k.w_loaded[5], 16)
            sp.dma_start(mu[:], A["L1_ffn_mu"].rearrange("(c p) e s -> p c (e s)", p=P)).then_inc(k.w_loaded[5], 16)
            for c in range(DC):
                sp.dma_start(w1[:, c], A["L1_ffn_W1"][:, c * P:(c + 1) * P].rearrange("e p h -> p e h")).then_inc(k.w_loaded[5], 16)
            sp.dma_start(w2[:], A["L1_ffn_W2"].rearrange("e h d -> h e d")).then_inc(k.w_loaded[5], 16)
        layernorm(k, load)
        names = ("dve_step sq_ready ss_in_psum ss_taken std_ready mu_ready n_ready nstd_ready xs_ready xT_in_psum xT_ready "
                 "logits_ready logits_taken cmax_ready cexp_ready dlog_ready dmax_ready dexp_ready disp_ready "
                 "t_in_psum t_taken slot_in_psum slot_taken h_in_psum h_taken so_in_psum so_taken out_ready b2_loaded0 b2_loaded1 var_ready l2_ready")
        with signals(nc, k.pool, names) as s, nc.Block() as block:
            @block.sync
            def _(sp):
                for e in range(ne):
                    if e >= 2:
                        sp.wait_ge(s.so_taken, B * (e - 1))
                    sp.dma_start(b2[:, e % 2], A["L1_ffn_b2"][e:e + 1].to_broadcast([P, D])).then_inc((s.b2_loaded0, s.b2_loaded1)[e % 2], 16)

            @block.tensor
            def _(pe):
                for j in range(4):
                    pe.wait_ge(s.sq_ready, DC * (j + 1))
                    matmul_acc(nc, k.bank(j), [(k.ones[:], comb[:, c, j * 512:(j + 1) * 512]) for c in range(DC)]).then_inc(s.ss_in_psum, 1)
                pe.wait_ge(s.xs_ready, 1)
                for b in range(B):
                    for c in range(DC):
                        last = nc.tensor.transpose(k.bank(4, P, T, c * BT + b * T), xs[:, b, c * P:(c + 1) * P], k.ident[:])
                last.then_inc(s.xT_in_psum, 1)
                pe.wait_ge(s.xT_ready, 1)
                pe.wait_ge(s.mu_ready, 4)
                for b in range(B):
                    if b:
                        pe.wait_ge(s.cexp_ready, 1)
                    for j in range(4):
                        last = matmul_acc(nc, k.bank(j), [(xst[:, c, b * T:(b + 1) * T], mu[:, c, j * 512:(j + 1) * 512]) for c in range(DC)])
                    last.then_inc(s.logits_ready, 1)
                pe.wait_ge(s.cexp_ready, B)

                def dispatch_logits(e):
                    if e >= 1:
                        pe.wait_ge(s.dexp_ready, B * e)
                    matmul_acc(nc, k.bank(0, P, BT), [(mu[:, c, e * SLOTS:(e + 1) * SLOTS], xst[:, c]) for c in range(DC)]).then_inc(s.dlog_ready, 1)
                dispatch_logits(0)
                for e in range(ne):
                    if e + 1 < ne:
                        dispatch_logits(e + 1)
                    pe.wait_ge(s.disp_ready, e + 1)
                    if e >= 1:
                        pe.wait_ge(s.t_taken, e)
                    for b in range(B):
                        nc.tensor.transpose(k.bank(1, P, P, b * T), disp[:, e % 2, b * T:(b + 1) * T], k.ident[:])
                    for b in range(B):
                        last = nc.tensor.transpose(k.bank(1, P, P, BT + b * T), comb[:, b, e * SLOTS:(e + 1) * SLOTS], k.ident[:])
                    last.then_inc(s.t_in_psum, 1)
                    pe.wait_ge(s.t_taken, e + 1)
                    if e >= 1:
                        pe.wait_ge(s.slot_taken, e)
                    for c in range(DC):
                        for b in range(B):
                            last = nc.tensor.matmul(k.bank(2, P, T, c * BT + b * T), xl[:, b, c * P:(c + 1) * P],
                                                    dtk[:, e % 2, b * T:(b + 1) * T], start=True, stop=True)
                    last.then_inc(s.slot_in_psum, 1)
                    pe.wait_ge(s.slot_taken, e + 1)
                    if e >= 1:
                        pe.wait_ge(s.h_taken, e)
                    matmul_acc(nc, k.bank(3, HID, BT), [(w1[:, c, e], slot[:, e % 2, c]) for c in range(DC)]).then_inc(s.h_in_psum, 1)
                    pe.wait_ge(s.h_taken, e + 1)
                    if e >= 1:
                        pe.wait_ge(s.so_taken, B * e)
                    for b in range(B):
                        last = nc.tensor.matmul(k.bank(4, P, D, b * D), ht[:, e % 2, b * T:(b + 1) * T], w2[:, e], start=True, stop=True)
                    last.then_inc(s.so_in_psum, 1)
                    pe.wait_ge(s.so_taken, B * (e + 1))
                    for b in range(B):
                        last = nc.tensor.matmul(k.bank(5 + b, P, D), ct[:, e % 2, b * T:(b + 1) * T], so[:, e % 2, b],
                                                start=(e == 0), stop=(e == ne - 1))
                last.then_inc(s.out_ready, 1)

            @block.scalar
            def _(act):
                act.wait_ge(k.w_loaded[5], 128)
                for j in range(4):
                    for c in range(DC):
                        nc.scalar.activation(comb[:, c, j * 512:(j + 1) * 512], mu[:, c, j * 512:(j + 1) * 512], ACT.Square).then_inc(s.sq_ready, 1)
                for j in range(4):
                    act.wait_ge(s.ss_in_psum, j + 1)
                    if j >= 2:
                        act.wait_ge(s.ss_taken, j - 1)
                    nc.scalar.activation(sq[:, j % 2], k.bank(j), ACT.Sqrt).then_inc(s.std_ready, 1)
                act.wait_ge(s.var_ready, B)
                nc.scalar.activation(sm[:, :, 1], sm[:, :, 0], ACT.Sqrt).then_inc(s.nstd_ready, 1)
                act.wait_ge(s.n_ready, B)
                nc.scalar.activation(sm[:, :, 7], sm[:, :, 6], ACT.Sqrt).then_inc(s.l2_ready, 1)
                act.wait_ge(s.xT_in_psum, 1)
                nc.scalar.copy(xst[:].rearrange("p c t -> p (c t)"), k.bank(4)).then_inc(s.xT_ready, 1)
                for b in range(B):
                    act.wait_ge(s.cmax_ready, b + 1)
                    nc.scalar.activation(comb[:, b], k.ps[:, 0:4].rearrange("p a n -> p (a n)"), ACT.Exp, bias=sm[:, b, 4:5],
                                         accum_out=sm[:, b, 5:6]).then_inc(s.cexp_ready, 1)
                for e in range(ne):
                    act.wait_ge(s.dmax_ready, B * (e + 1))
                    if e >= 2:
                        act.wait_ge(s.t_in_psum, e - 1)
                    for b in range(B):
                        nc.scalar.activation(disp[:, e % 2, b * T:(b + 1) * T], k.bank(0, P, T, b * T), ACT.Exp,
                                             bias=dm[:, e % 2, b, 1:2], accum_out=dm[:, e % 2, b, 2:3]).then_inc(s.dexp_ready, 1)
                    act.wait_ge(s.h_in_psum, e + 1)
                    if e >= 2:
                        act.wait_ge(s.so_in_psum, e - 1)
                    nc.scalar.activation(ht[:, e % 2], k.bank(3, HID, BT), ACT.Gelu, bias=b1[:, e:e + 1]).then_inc(s.h_taken, 1)

            @block.vector
            def _(dve):
                link = chain(dve, s.dve_step)
                dve.wait_ge(k.w_loaded[5], 128)
                for b in range(B):
                    link(nc.vector.bn_stats(k.stat[:, b, :], k.xn[:, b]))
                    link(nc.vector.bn_aggr(k.mv[:, b, :], k.stat[:, b, :]))
                    nc.vector.tensor_scalar(sm[:, b, 0:1], k.mv[:, b, 1:2], LN_EPS, None, ALU.add).then_inc(s.var_ready, 1)
                for j in range(4):
                    dve.wait_ge(s.std_ready, j + 1)
                    link(nc.vector.tensor_scalar(rn[:, 0], sq[:, j % 2], L2_EPS, None, ALU.max))
                    nc.vector.reciprocal(rn[:, 1], rn[:, 0]).then_inc(s.ss_taken, 1)
                    dve.wait_ge(s.ss_taken, j + 1)
                    for c in range(DC):
                        sl = mu[:, c, j * 512:(j + 1) * 512]
                        link(nc.vector.tensor_tensor(sl, sl, rn[:, 1], ALU.mult))
                    dve.sem_inc(s.mu_ready, 1)
                dve.wait_ge(s.nstd_ready, 1)
                for b in range(B):
                    link(nc.vector.reciprocal(sm[:, b, 2:3], sm[:, b, 1:2]))
                    link(nc.vector.tensor_scalar(xl[:, b], k.xn[:, b], k.mv[:, b, 0:1], sm[:, b, 2:3], ALU.subtract, ALU.mult))
                    link(nc.vector.tensor_tensor(xl[:, b], xl[:, b], gam[:], ALU.mult))
                    link(nc.vector.tensor_tensor(xl[:, b], xl[:, b], bet[:], ALU.add))
                    link(nc.vector.tensor_tensor(xs[:, b], xl[:, b], xl[:, b], ALU.mult))
                    nc.vector.reduce_sum(sm[:, b, 6:7], xs[:, b], AX.X).then_inc(s.n_ready, 1)
                dve.wait_ge(s.l2_ready, 1)
                for b in range(B):
                    link(nc.vector.tensor_scalar(sm[:, b, 8:9], sm[:, b, 7:8], L2_EPS, None, ALU.max))
                    link(nc.vector.reciprocal(sm[:, b, 9:10], sm[:, b, 8:9]))
                    link(nc.vector.tensor_scalar(xs[:, b], xl[:, b], sm[:, b, 9:10], sca[:, 0:1], ALU.mult, ALU.mult))
                dve.sem_inc(s.xs_ready, 1)
                for b in range(B):
                    dve.wait_ge(s.logits_ready, b + 1)
                    link(nc.vector.reduce_max(sm[:, b, 10:11], k.ps[:, 0:4].rearrange("p a n -> p (a n)"), AX.X))
                    nc.vector.tensor_scalar(sm[:, b, 4:5], sm[:, b, 10:11], -1.0, None, ALU.mult).then_inc(s.cmax_ready, 1)

                def dispatch_max(e):
                    dve.wait_ge(s.dlog_ready, e + 1)
                    r = e % 2
                    link(nc.vector.tensor_reduce(dm[:, r, :, 0], k.bank(0, P, BT).rearrange("p (b t) -> p b t", b=B), AX.X, ALU.max))
                    for b in range(B):
                        nc.vector.tensor_scalar(dm[:, r, b, 1:2], dm[:, r, b, 0:1], -1.0, None, ALU.mult).then_inc(s.dmax_ready, 1)

                def dispatch_norm(e):
                    r = e % 2
                    dve.wait_ge(s.dexp_ready, B * (e + 1))
                    link(nc.vector.reciprocal(dm[:, r, :, 3], dm[:, r, :, 2]))
                    d3 = disp[:, r].rearrange("p (b t) -> p b t", b=B)
                    nc.vector.tensor_tensor(d3, d3, dm[:, r, :, 3].unsqueeze(2).to_broadcast([P, B, T]), ALU.mult).then_inc(s.disp_ready, 1)
                dispatch_max(0)
                for e in range(ne):
                    r = e % 2
                    dispatch_norm(e)
                    if e + 1 < ne:
                        dispatch_max(e + 1)
                    dve.wait_ge(s.t_in_psum, e + 1)
                    nc.vector.tensor_copy(dtk[:, r], k.bank(1, P, BT))
                    link(nc.vector.tensor_copy(ct[:, r], k.bank(1, P, BT, BT)))
                    dve.sem_inc(s.t_taken, 1)
                    dve.wait_ge(s.slot_in_psum, e + 1)
                    nc.vector.tensor_copy(slot[:, r].rearrange("p c t -> p (c t)"), k.bank(2)).then_inc(s.slot_taken, 1)
                    dve.wait_ge(s.so_in_psum, e + 1)
                    dve.wait_ge((s.b2_loaded0, s.b2_loaded1)[r], 16 * (e // 2 + 1))
                    for b in range(B):
                        nc.vector.tensor_tensor(so[:, r, b], k.bank(4, P, D, b * D), b2[:, r], ALU.add).then_inc(s.so_taken, 1)
                for b in range(B):
                    link(nc.vector.reciprocal(sm[:, b, 11:12], sm[:, b, 5:6]))
                dve.wait_ge(s.out_ready, 1)
                for b in range(B):
                    nc.vector.scalar_tensor_tensor(out=k.x[:, b], in0=k.bank(5 + b, P, D), scalar=sm[:, b, 11:12], in1=k.x[:, b],
                                                   op0=ALU.mult, op1=ALU.add)


def l2_xattn(k):
    nc, A = k.nc, k.A
    nt = S2 // P
    with ExitStack() as ctx:
        def sb(name, shape, dt=F32):
            return k.sb("x2_" + name, shape, dt, ctx)
        wq, wg, wo = sb("wq", [P, DC, D]), sb("wg", [P, DC, D]), sb("wo", [P, DC, D])
        wkv = sb("wkv", [P, DC, 2 * D])
        bg = sb("bg", [P, DC])
        q, gate, z = sb("q", [P, DC, BT]), sb("gate", [P, DC, BT]), sb("z", [P, DC, BT])
        low, ex = sb("low", [P, 3, 512]), sb("ex", [P, 3, 512])
        kf = sb("k_feat", [P, 4, D])
        va = sb("v_ones", [P, 4, DC, P + 1])
        kvb, kb = sb("kv_heads", [P, DC, B, P]), sb("ksum_heads", [P, DC, B, P])
        flat = lambda t: t[:].rearrange("p c t -> p (c t)")

        def load(sp):
            for t, n in ((wkv, "Wkv"), (wq, "Wq"), (wg, "Wg"), (wo, "Wo")):
                sp.dma_start(t[:], A["L2_xattn_" + n + "_T"].rearrange("(c p) n -> p c n", p=P)).then_inc(k.w_loaded[6], 16)
            sp.dma_start(bg[:], A["L2_xattn_bg"].rearrange("(c p) -> p c", p=P), allow_slow_non_contiguous=True).then_inc(k.w_loaded[6], 16)
        layernorm(k, load)
        names = ("dve_step q_in_psum gate_in_psum kv_in_psum low_ready exp_ready kf_ready v_taken ones_ready sum_taken "
                 "attn_in_psum o_ready out_ready gate_ready tile_used")
        with signals(nc, k.pool, names) as s, nc.Block() as block:
            @block.tensor
            def _(pe):
                pe.wait_ge(k.w_loaded[6], 80)
                for loaded in k.ctx_loaded:
                    pe.wait_ge(loaded, 16)
                for w, bank, sem in ((wq, 0, s.q_in_psum), (wg, 1, s.gate_in_psum)):
                    for m in range(DC):
                        last = matmul_acc(nc, k.bank(bank, P, BT, m * BT), [(w[:, c, m * P:(m + 1) * P], k.xt[:, c]) for c in range(DC)])
                    last.then_inc(sem, 1)
                pe.wait_ge(s.ones_ready, 1)

                def summary(i):
                    pe.wait_ge(s.kf_ready, i + 1)
                    pe.wait_ge(s.v_taken, i + 1)
                    if i == nt:
                        pe.wait_ge(s.sum_taken, 1)
                    for m in range(DC):
                        last = nc.tensor.matmul(k.bank(6 + m, P, P + 1), kf[:, i % 4, m * P:(m + 1) * P], va[:, i % 4, m],
                                                start=(i % nt == 0), stop=(i % nt == nt - 1))
                    last.then_inc(s.tile_used, 1)
                for i in range(NKT):
                    if i >= 4:
                        pe.wait_ge(s.kf_ready, i - 3)
                        pe.wait_ge(s.v_taken, i - 3)
                    matmul_acc(nc, k.bank(2 + i % 4), [(k.ctxt[:, c, i * P:(i + 1) * P], wkv[:, c]) for c in range(DC)]).then_inc(s.kv_in_psum, 1)
                    if i >= 2:
                        summary(i - 2)
                summary(NKT - 2)
                summary(NKT - 1)
                pe.wait_ge(s.sum_taken, 2)
                pe.wait_ge(s.gate_ready, 2)
                for b in range(B):
                    for m in range(DC):
                        nc.tensor.matmul(k.bank(0, P, T, m * BT + b * T), kvb[:, m, b], q[:, m, b * T:(b + 1) * T], start=True, stop=True)
                        last = nc.tensor.matmul(k.bank(1, P, T, m * BT + b * T), kb[:, m, b], q[:, m, b * T:(b + 1) * T], start=True, stop=True)
                last.then_inc(s.attn_in_psum, 1)
                pe.wait_ge(s.o_ready, 1)
                for b in range(B):
                    last = matmul_acc(nc, k.bank(2, P, D, b * D), [(z[:, c, b * T:(b + 1) * T], wo[:, c]) for c in range(DC)])
                last.then_inc(s.out_ready, 1)

            @block.scalar
            def _(act):
                act.wait_ge(k.w_loaded[6], 80)
                act.wait_ge(s.gate_in_psum, 1)
                for m in range(DC):
                    nc.scalar.activation(gate[:, m], k.bank(1, P, BT, m * BT), ACT.Sigmoid, bias=bg[:, m:m + 1]).then_inc(s.gate_ready, 1)
                act.wait_ge(s.low_ready, 1)
                nc.scalar.activation(ex[:, 2], low[:, 2], ACT.Exp).then_inc(s.exp_ready, 1)
                act.wait_ge(s.ones_ready, 1)

                def take_v(i):
                    act.wait_ge(s.kf_ready, i + 1)
                    if i >= 4:
                        act.wait_ge(s.tile_used, i - 3)
                    nc.scalar.copy(va[:, i % 4, :, 0:P], k.bank(2 + i % 4, P, D, D).rearrange("p (m n) -> p m n", m=DC)).then_inc(s.v_taken, 1)
                for i in range(NKT):
                    act.wait_ge(s.low_ready, i + 2)
                    nc.scalar.activation(ex[:, i % 2, 0:D], low[:, i % 2, 0:D], ACT.Exp).then_inc(s.exp_ready, 1)
                    if i >= 1:
                        take_v(i - 1)
                take_v(NKT - 1)

            @block.vector
            def _(dve):
                link = chain(dve, s.dve_step)
                nc.vector.memset(va[:, :, :, P:P + 1], 1.0).then_inc(s.ones_ready, 1)
                dve.wait_ge(s.q_in_psum, 1)
                nc.vector.tensor_scalar(low[:, 2], k.bank(0), 0.0, None, ALU.min).then_inc(s.low_ready, 1)
                dve.wait_ge(s.exp_ready, 1)
                link(nc.vector.scalar_tensor_tensor(out=flat(q), in0=k.bank(0), scalar=0.0, in1=ex[:, 2], op0=ALU.max, op1=ALU.add))

                def feature(i):
                    dve.wait_ge(s.exp_ready, i + 2)
                    if i >= 4:
                        dve.wait_ge(s.tile_used, i - 3)
                    nc.vector.scalar_tensor_tensor(out=kf[:, i % 4], in0=k.bank(2 + i % 4, P, D), scalar=0.0, in1=ex[:, i % 2, 0:D],
                                                   op0=ALU.max, op1=ALU.add).then_inc(s.kf_ready, 1)

                def take_summary(b):
                    dve.wait_ge(s.tile_used, nt * (b + 1))
                    for m in range(DC):
                        link(nc.vector.tensor_tensor(kvb[:, m, b], k.bank(6 + m, P, P), k.blocks[:], ALU.mult))
                        link(nc.vector.tensor_scalar(kb[:, m, b], k.blocks[:], k.bank(6 + m, P, 1, P), None, ALU.mult))
                    dve.sem_inc(s.sum_taken, 1)
                for i in range(NKT):
                    dve.wait_ge(s.kv_in_psum, i + 1)
                    nc.vector.tensor_scalar(low[:, i % 2, 0:D], k.bank(2 + i % 4, P, D), 0.0, None, ALU.min).then_inc(s.low_ready, 1)
                    if i >= 1:
                        feature(i - 1)
                    if i == nt:
                        take_summary(0)
                feature(NKT - 1)
                take_summary(1)
                dve.wait_ge(s.attn_in_psum, 1)
                link(nc.vector.tensor_scalar(low[:, 0], k.bank(1), 1e-6, None, ALU.add))
                link(nc.vector.reciprocal(low[:, 1], low[:, 0]))
                link(nc.vector.tensor_tensor(flat(z), low[:, 1], k.bank(0), ALU.mult))
                dve.wait_ge(s.gate_ready, 2)
                nc.vector.tensor_tensor(flat(z), flat(z), flat(gate), ALU.mult).then_inc(s.o_ready, 1)
                dve.wait_ge(s.out_ready, 1)
                xf = k.x[:].rearrange("p b d -> p (b d)")
                nc.vector.tensor_tensor(xf, xf, k.bank(2), ALU.add)


def l2_attn(k):
    nc, A = k.nc, k.A
    nh = HEADS
    PAD = 32
    GH = P // PAD
    NU = B * nh // GH
    with ExitStack() as ctx:
        def sb(name, shape, dt=F32):
            return k.sb("a2_" + name, shape, dt, ctx)
        w = [sb("w" + n, [P, DC, D]) for n in "qkvo"]
        bias = [sb("b" + n, [P, D]) for n in "qkvo"]
        cos, sin = sb("cos", [P, HD]), sb("sin", [P, HD])
        qk = sb("qk", [P, 2, B, D])
        v = sb("v", [P, B, D])
        t1, t2 = sb("t1", [P, D]), sb("t2", [P, D])
        pad = sb("padded", [P, 2, B, nh, PAD])
        qkt = sb("qkT", [P, 2, GH, BT])
        cb = sb("causal", [P, P])
        sc, et = sb("scores", [P, 2, GH, T]), sb("eT", [P, 2, GH, T])
        sm = sb("small", [P, 2, GH, 2])
        rs = sb("rsum", [P, B, nh])
        attn, att = sb("attn", [P, B, D]), sb("attnT", [P, DC, BT])

        def load(sp):
            for t, n in zip(w, "qkvo"):
                sp.dma_start(t[:], A["L2_attn_W" + n + "_T"].rearrange("(c p) n -> p c n", p=P)).then_inc(k.w_loaded[7], 16)
            for t, n in zip(bias, "qkvo"):
                sp.dma_start(t[:], A["L2_attn_b" + n].rearrange("(a n) -> a n", a=1).to_broadcast([P, D])).then_inc(k.w_loaded[7], 16)
            sp.dma_start(cos[:], A["L2_cos"]).then_inc(k.w_loaded[7], 16)
            sp.dma_start(sin[:], A["L2_sin"]).then_inc(k.w_loaded[7], 16)
        layernorm(k, load)
        names = ("dve_step proj_ready padded_ready zeroed t_in_psum t_taken scores_in_psum centred_ready exp_ready et_in_psum et_ready "
                 "v_ready pv_ready attn_ready attnT_in_psum attnT_ready out_ready pool_step")
        with signals(nc, k.pool, names) as s, nc.Block() as block:
            @block.gpsimd
            def _(pool):
                pool.memset(pad[:], 0.0).then_inc(s.zeroed, 1)
                pool.memset(cb[:], 0.0).then_inc(s.pool_step, 1)
                pool.wait_ge(s.pool_step, 1)
                nc.gpsimd.affine_select(out=cb[:], in_=cb[:], compare_op=ALU.is_ge, fill=NEG, base=0, pattern=[[-1, P]],
                                        channel_multiplier=1).then_inc(s.zeroed, 1)

            @block.tensor
            def _(pe):
                pe.wait_ge(k.w_loaded[7], 160)
                for j in range(3):
                    for b in range(B):
                        last = matmul_acc(nc, k.bank(j, P, D, b * D), [(k.xt[:, c, b * T:(b + 1) * T], w[j][:, c]) for c in range(DC)])
                    last.then_inc(s.proj_ready, 1)
                for j in range(2):
                    for b in range(B):
                        pe.wait_ge(s.padded_ready, 2 * j + b + 1)
                        for g in range(GH):
                            last = nc.tensor.transpose(k.bank(3 + 2 * j + b, P, P, g * P),
                                                       pad[:, j, b, GH * g:GH * (g + 1)].rearrange("p h d -> p (h d)"), k.ident[:])
                        last.then_inc(s.t_in_psum, 1)
                pe.wait_ge(s.t_taken, 4)
                pe.wait_ge(s.v_ready, B)

                def scores(u):
                    b, g = divmod(u, GH)
                    if u >= 1:
                        pe.wait_ge(s.centred_ready, u)
                    for j in range(GH):
                        r = slice(PAD * j, PAD * (j + 1))
                        last = nc.tensor.matmul(k.bank(j, P, T), qkt[r, 0, g, b * T:(b + 1) * T], qkt[r, 1, g, b * T:(b + 1) * T],
                                                start=True, stop=True)
                    last.then_inc(s.scores_in_psum, 1)
                scores(0)
                for u in range(NU):
                    if u + 1 < NU:
                        scores(u + 1)
                    b, g = divmod(u, GH)
                    pe.wait_ge(s.exp_ready, u + 1)
                    if u >= 2:
                        pe.wait_ge(s.et_ready, u - 1)
                    for j in range(GH):
                        last = nc.tensor.transpose(k.bank(4 + u % 2, P, T, j * T), sc[:, u % 2, j], k.ident[:])
                    last.then_inc(s.et_in_psum, 1)
                    pe.wait_ge(s.et_ready, u + 1)
                    for j in range(GH):
                        a = (GH * g + j) * HD
                        last = nc.tensor.matmul(k.bank(7, P, HD, b * D + a), et[:, u % 2, j], v[:, b, a:a + HD], start=True, stop=True)
                    last.then_inc(s.pv_ready, 1)
                for b in range(B):
                    pe.wait_ge(s.attn_ready, b + 1)
                    for c in range(DC):
                        last = nc.tensor.transpose(k.bank(3, P, T, c * BT + b * T), attn[:, b, c * P:(c + 1) * P], k.ident[:])
                last.then_inc(s.attnT_in_psum, 1)
                pe.wait_ge(s.attnT_ready, 1)
                for b in range(B):
                    last = matmul_acc(nc, k.bank(6, P, D, b * D), [(att[:, c, b * T:(b + 1) * T], w[3][:, c]) for c in range(DC)])
                last.then_inc(s.out_ready, 1)

            @block.scalar
            def _(act):
                for j in range(2):
                    for b in range(B):
                        act.wait_ge(s.t_in_psum, 2 * j + b + 1)
                        nc.scalar.copy(qkt[:, j, :, b * T:(b + 1) * T], k.bank(3 + 2 * j + b).rearrange("p (g n) -> p g n", g=GH)).then_inc(s.t_taken, 1)
                for u in range(NU):
                    act.wait_ge(s.centred_ready, u + 1)
                    nc.scalar.activation(sc[:, u % 2], sc[:, u % 2], ACT.Exp).then_inc(s.exp_ready, 1)
                    act.wait_ge(s.et_in_psum, u + 1)
                    if u >= 2:
                        act.wait_ge(s.pv_ready, u - 1)
                    nc.scalar.copy(et[:, u % 2].rearrange("p g t -> p (g t)"), k.bank(4 + u % 2)).then_inc(s.et_ready, 1)
                act.wait_ge(s.attnT_in_psum, 1)
                nc.scalar.copy(att[:].rearrange("p c t -> p (c t)"), k.bank(3)).then_inc(s.attnT_ready, 1)

            @block.vector
            def _(dve):
                link = chain(dve, s.dve_step)
                dve.wait_ge(k.w_loaded[7], 160)
                dve.wait_ge(s.zeroed, 2)
                half = HD // 2
                for j in range(2):
                    dve.wait_ge(s.proj_ready, j + 1)
                    for b in range(B):
                        link(nc.vector.tensor_tensor(qk[:, j, b], k.bank(j, P, D, b * D), bias[j][:], ALU.add))
                        x3 = qk[:, j, b].rearrange("p (h d) -> p h d", d=HD)
                        a3, b3 = (t[:].rearrange("p (h d) -> p h d", d=HD) for t in (t1, t2))
                        link(nc.vector.tensor_tensor(a3, x3, cos[:].unsqueeze(1).to_broadcast([P, nh, HD]), ALU.mult))
                        link(nc.vector.tensor_tensor(b3[:, :, 0:half], x3[:, :, half:HD], sin[:, 0:half].unsqueeze(1).to_broadcast([P, nh, half]), ALU.mult))
                        link(nc.vector.tensor_tensor(b3[:, :, half:HD], x3[:, :, 0:half], sin[:, half:HD].unsqueeze(1).to_broadcast([P, nh, half]), ALU.mult))
                        nc.vector.tensor_tensor(pad[:, j, b, :, 0:HD], a3, b3, ALU.add).then_inc(s.padded_ready, 1)
                        dve.wait_ge(s.padded_ready, 2 * j + b + 1)
                dve.wait_ge(s.proj_ready, 3)
                for b in range(B):
                    nc.vector.tensor_tensor(v[:, b], k.bank(2, P, D, b * D), bias[2][:], ALU.add).then_inc(s.v_ready, 1)
                for u in range(NU):
                    b, g = divmod(u, GH)
                    r = u % 2
                    dve.wait_ge(s.scores_in_psum, u + 1)
                    if u >= 2:
                        dve.wait_ge(s.et_in_psum, u - 1)
                    link(nc.vector.scalar_tensor_tensor(out=sc[:, r], in0=k.ps[:, 0:GH, 0:T], scalar=1.0 / float(np.sqrt(HD)),
                                                        in1=cb[:].unsqueeze(1).to_broadcast([P, GH, T]), op0=ALU.mult, op1=ALU.add))
                    link(nc.vector.reduce_max(sm[:, r, :, 0], sc[:, r], AX.X))
                    nc.vector.tensor_tensor(sc[:, r], sc[:, r], sm[:, r, :, 0].unsqueeze(2).to_broadcast([P, GH, T]), ALU.subtract).then_inc(s.centred_ready, 1)
                    dve.wait_ge(s.exp_ready, u + 1)
                    link(nc.vector.reduce_sum(sm[:, r, :, 1], sc[:, r], AX.X))
                    link(nc.vector.reciprocal(rs[:, b, GH * g:GH * (g + 1)], sm[:, r, :, 1]))
                    if g == GH - 1:
                        dve.wait_ge(s.pv_ready, u + 1)
                        nc.vector.tensor_tensor(attn[:, b].rearrange("p (h d) -> p h d", d=HD), k.bank(7, P, D, b * D).rearrange("p (h d) -> p h d", d=HD),
                                                rs[:, b].unsqueeze(2).to_broadcast([P, nh, HD]), ALU.mult).then_inc(s.attn_ready, 1)
                for b in range(B):
                    link(nc.vector.tensor_tensor(k.x[:, b], k.x[:, b], bias[3][:], ALU.add))
                dve.wait_ge(s.out_ready, 1)
                xf = k.x[:].rearrange("p b d -> p (b d)")
                nc.vector.tensor_tensor(xf, xf, k.bank(6), ALU.add)


LORAS = 8
RANK = 16


def l2_ffn(k):
    nc, A = k.nc, k.A
    ne = LORAS
    with ExitStack() as ctx:
        def sb(name, shape, dt=F32):
            return k.sb("f2_" + name, shape, dt, ctx)
        w, wa, wgt = sb("w", [P, DC, D]), sb("lora_a", [P, DC, P]), sb("gate_w", [P, DC, ne])
        wb = sb("lora_b", [P, D])
        bias, gb = sb("bias", [P, D]), sb("gate_b", [P, ne])
        lg, mk = sb("logits", [P, B, 16]), sb("marked", [P, B, 16])
        top, sm = sb("top", [P, B, 8]), sb("small", [P, B, 8])
        g = sb("gates", [P, B, ne])
        xa, xat = sb("xa", [P, B, P]), sb("xaT", [P, BT])

        def load(sp):
            for t, n in ((w, "L2_ffn_W_T"), (wa, "L2_ffn_lora_A_T"), (wgt, "L2_ffn_gate_w_T")):
                sp.dma_start(t[:], A[n].rearrange("(c p) n -> p c n", p=P)).then_inc(k.w_loaded[8], 16)
            sp.dma_start(wb[:], A["L2_ffn_lora_B_T"]).then_inc(k.w_loaded[8], 16)
            sp.dma_start(bias[:], A["L2_ffn_b"].rearrange("(a n) -> a n", a=1).to_broadcast([P, D])).then_inc(k.w_loaded[8], 16)
            sp.dma_start(gb[:], A["L2_ffn_gate_b"].rearrange("(a n) -> a n", a=1).to_broadcast([P, ne])).then_inc(k.w_loaded[8], 16)
        layernorm(k, load)
        with signals(nc, k.pool, "dve_step logits_ready xa_in_psum neg_ready exp_ready xa_ready xaT_in_psum xaT_ready out_ready") as s, \
                nc.Block() as block:
            @block.tensor
            def _(pe):
                pe.wait_ge(k.w_loaded[8], 96)
                for b in range(B):
                    last = matmul_acc(nc, k.bank(0, P, ne, b * ne), [(k.xt[:, c, b * T:(b + 1) * T], wgt[:, c]) for c in range(DC)])
                last.then_inc(s.logits_ready, 1)
                for b in range(B):
                    last = matmul_acc(nc, k.bank(1, P, P, b * P), [(k.xt[:, c, b * T:(b + 1) * T], wa[:, c]) for c in range(DC)])
                last.then_inc(s.xa_in_psum, 1)
                pe.wait_ge(s.xa_ready, B)
                for b in range(B):
                    last = nc.tensor.transpose(k.bank(2, P, P, b * T), xa[:, b], k.ident[:])
                last.then_inc(s.xaT_in_psum, 1)
                pe.wait_ge(s.xaT_ready, 1)
                for b in range(B):
                    sl = slice(b * T, (b + 1) * T)
                    last = matmul_acc(nc, k.bank(3, P, D, b * D), [(k.xt[:, c, sl], w[:, c]) for c in range(DC)] + [(xat[:, sl], wb[:])])
                last.then_inc(s.out_ready, 1)

            @block.scalar
            def _(act):
                act.wait_ge(s.neg_ready, B)
                for b in range(B):
                    nc.scalar.activation(g[:, b], lg[:, b, 0:ne], ACT.Exp, bias=sm[:, b, 0:1]).then_inc(s.exp_ready, 1)
                act.wait_ge(s.xaT_in_psum, 1)
                nc.scalar.copy(xat[:], k.bank(2, P, BT)).then_inc(s.xaT_ready, 1)

            @block.vector
            def _(dve):
                link = chain(dve, s.dve_step)
                dve.wait_ge(k.w_loaded[8], 96)
                for b in range(B):
                    for j in range(ne):
                        last = nc.vector.memset(lg[:, b, ne + j:ne + j + 1], NEG * (j + 1))
                link(last)
                dve.wait_ge(s.logits_ready, 1)
                for b in range(B):
                    link(nc.vector.tensor_tensor(lg[:, b, 0:ne], k.bank(0, P, ne, b * ne), gb[:], ALU.add))
                    link(nc.vector.max(top[:, b], lg[:, b]))
                    nc.vector.tensor_scalar(sm[:, b, 0:1], top[:, b, 0:1], -1.0, None, ALU.mult).then_inc(s.neg_ready, 1)
                    dve.wait_ge(s.neg_ready, b + 1)
                    for j in range(6):
                        last = nc.vector.memset(top[:, b, 2 + j:3 + j], NEG * (j + 1))
                    link(last)
                    link(nc.vector.match_replace(mk[:, b], top[:, b], lg[:, b], 100 * NEG))
                    link(nc.vector.tensor_scalar(mk[:, b, 0:ne], mk[:, b, 0:ne], 100 * NEG, None, ALU.is_equal))
                dve.wait_ge(s.exp_ready, B)
                for b in range(B):
                    link(nc.vector.tensor_tensor(g[:, b], g[:, b], mk[:, b, 0:ne], ALU.mult))
                    link(nc.vector.reduce_sum(sm[:, b, 1:2], g[:, b], AX.X))
                    link(nc.vector.reciprocal(sm[:, b, 2:3], sm[:, b, 1:2]))
                    link(nc.vector.tensor_scalar(g[:, b], g[:, b], sm[:, b, 2:3], None, ALU.mult))
                dve.wait_ge(s.xa_in_psum, 1)
                for b in range(B):
                    nc.vector.tensor_tensor(xa[:, b].rearrange("p (e r) -> p e r", r=RANK), k.bank(1, P, P, b * P).rearrange("p (e r) -> p e r", r=RANK),
                                            g[:, b].unsqueeze(2).to_broadcast([P, ne, RANK]), ALU.mult).then_inc(s.xa_ready, 1)
                for b in range(B):
                    link(nc.vector.tensor_tensor(k.x[:, b], k.x[:, b], bias[:], ALU.add))
                dve.wait_ge(s.out_ready, 1)
                xf = k.x[:].rearrange("p b d -> p (b d)")
                nc.vector.tensor_tensor(xf, xf, k.bank(3), ALU.add)


TWO_PI = 2 * np.pi
TP1 = 6.28125
TP2 = int((TWO_PI - TP1) * 2 ** 21) / 2 ** 21
TP3 = float(np.float32(TWO_PI - TP1 - TP2))
PI_IN = 3.1415925


def reduce_angle(nc, link, ang, turns):
    link(nc.vector.tensor_scalar(turns, ang, float(1 / TWO_PI), ROUND, ALU.mult, ALU.add))
    link(nc.vector.tensor_scalar(turns, turns, ROUND, None, ALU.subtract))
    for part in (TP1, TP2, TP3):
        link(nc.vector.scalar_tensor_tensor(out=ang, in0=turns, scalar=-part, in1=ang, op0=ALU.mult, op1=ALU.add))
    link(nc.vector.tensor_scalar(ang, ang, PI_IN, -PI_IN, ALU.min, ALU.max))


H3 = 16
KVH = 4
HD3 = 128
HALF = HD3 // 2
RMS_EPS = 1e-6
KT3 = S2 // P + 1


def l3_xattn(k):
    nc, A = k.nc, k.A
    NQ = H3 // KVH
    NI = NQ + KT3
    NK = KT3 * P
    NG = (KT3 + 3) // 4
    with ExitStack() as ctx:
        def sb(name, shape, dt=F32):
            return k.sb("x3_" + name, shape, dt, ctx)
        wq, wk, wv = sb("wq", [P, DC, H3 * HD3]), sb("wk", [P, DC, KVH * HD3]), sb("wv", [P, DC, KVH * HD3])
        wo = sb("wo", [P, H3, D])
        nw = sb("norm_w", [P, 2, HD3])
        invf = sb("inv_freq", [P, HALF])
        posi, posf = sb("pos_i", [P, B, KT3], I32), sb("pos_f", [P, B, KT3])
        tc, ts = sb("tab_cos", [P, KT3 + 1, HD3]), sb("tab_sin", [P, KT3 + 1, HD3])
        t1, t2 = sb("t1", [P, 4, 4, HD3]), sb("t2", [P, 2, 4, HD3])
        st = sb("rms", [P, 4, 3, 4])
        kt, vt = sb("kT", [P, KVH, NK]), sb("v", [P, KT3, KVH * HD3])
        qt = sb("qT", [P, H3, T])
        ex = sb("exps", [P, 2, NK])
        ang, turn, sn, cs = (ex[:].rearrange("p a (c t f) -> p (a c) t f", c=2, f=HALF)[:, j] for j in range(4))
        et = t2
        sm = sb("small", [P, 2, 4])
        on = k.xn[:].rearrange("p a n -> p (a n)")[:, 0:2 * HD3].rearrange("p (a n) -> p a n", a=2)
        ot = t1[:].rearrange("p a h n -> p (a h) n")

        def load(sp):
            for t, n in ((wk, "Wk"), (wv, "Wv"), (wq, "Wq"), (wo, "Wo")):
                sp.dma_start(t[:], A["L3_xattn_" + n + "_T"].rearrange("(c p) n -> p c n", p=P)).then_inc(k.w_loaded[9], 16)
            for j, n in enumerate(("q_norm_w", "k_norm_w")):
                sp.dma_start(nw[:, j], A["L3_xattn_" + n].rearrange("(a n) -> a n", a=1).to_broadcast([P, HD3])).then_inc(k.w_loaded[9], 16)
            sp.dma_start(invf[:], A["L3_inv_freq"].rearrange("(a n) -> a n", a=1).to_broadcast([P, HALF])).then_inc(k.w_loaded[9], 16)
            for b in range(B):
                sp.dma_start(posi[:, b, 0:KT3 - 1], A["pos_BxS2"][b].rearrange("(n p) -> p n", p=P), allow_slow_non_contiguous=True).then_inc(k.w_loaded[9], 16)
                sp.dma_start(posi[:, b, KT3 - 1:KT3], A["itok_BxS_4096_4607"][b].rearrange("(n p) -> p n", p=P), allow_slow_non_contiguous=True).then_inc(k.w_loaded[9], 16)
        layernorm(k, load)
        NW = 11 * 16
        names = ("dve_step ang_ready trig_ready tab_ready proj_in_psum v_in_psum v_taken mults_done turned sq_done var_ready std_ready rstd_ready "
                 "normed t_in_psum t_taken scores_in_psum neg_ready exp_done et_in_psum et_ready et_used pv_in_psum on_ready "
                 "ot_in_psum ot_taken out_ready out_taken")
        with signals(nc, k.pool, names) as s, nc.Block() as block:
            def source(b, i):
                if i < NQ:
                    return [(k.xt[:, c, b * T:(b + 1) * T], wq[:, c, i * 512:(i + 1) * 512]) for c in range(DC)]
                return [(key_src(b, i - NQ, c), wk[:, c]) for c in range(DC)]

            def key_src(b, j, c):
                if j == KT3 - 1:
                    return k.xt[:, c, b * T:(b + 1) * T]
                return k.ctxt[:, c, b * S2 + j * P:b * S2 + (j + 1) * P]

            @block.tensor
            def _(pe):
                pe.wait_ge(k.w_loaded[9], NW)
                for loaded in k.ctx_loaded:
                    pe.wait_ge(loaded, 16)
                for b in range(B):
                    def turn_back(i):
                        n = b * NI + i
                        pe.wait_ge(s.normed, n + 1)
                        if n >= 2:
                            pe.wait_ge(s.t_taken, n - 1)
                        for h in range(4):
                            last = nc.tensor.transpose(k.bank(4 + n % 2, P, P, h * P), t1[:, n % 4, h], k.ident[:])
                        last.then_inc(s.t_in_psum, 1)
                    for i in range(NI):
                        n = b * NI + i
                        if n >= 2:
                            pe.wait_ge(s.sq_done, n - 1)
                        matmul_acc(nc, k.bank(n % 2), source(b, i)).then_inc(s.proj_in_psum, 1)
                        if i >= NQ:
                            m = b * KT3 + i - NQ
                            if m >= 2:
                                pe.wait_ge(s.v_taken, m - 1)
                            matmul_acc(nc, k.bank(2 + m % 2), [(key_src(b, i - NQ, c), wv[:, c]) for c in range(DC)]).then_inc(s.v_in_psum, 1)
                        if i >= 3:
                            turn_back(i - 3)
                    for i in range(NI - 3, NI):
                        turn_back(i)
                    pe.wait_ge(s.t_taken, (b + 1) * NI)
                    pe.wait_ge(s.v_taken, (b + 1) * KT3)

                    def scores(h):
                        n = b * H3 + h
                        if n >= 1:
                            pe.wait_ge(s.exp_done, n)
                        for a in range(0, NK, 512):
                            w = min(512, NK - a)
                            last = nc.tensor.matmul(k.bank(a // 512, P, w), qt[:, h], kt[:, h // NQ, a:a + w], start=True, stop=True)
                        last.then_inc(s.scores_in_psum, 1)

                    def values(h):
                        n = b * H3 + h
                        pe.wait_ge(s.exp_done, n + 1)

                        def pv(g):
                            pe.wait_ge(s.et_ready, n * NG + g + 1)
                            for j in range(4 * g, min(4 * g + 4, KT3)):
                                last = nc.tensor.matmul(k.bank(7, P, HD3), et[:, (n * NG + g) % 2, j % 4], vt[:, j, (h // NQ) * HD3:(h // NQ + 1) * HD3],
                                                        start=(j == 0), stop=(j == KT3 - 1))
                            last.then_inc(s.et_used, 1)
                        if n >= 1:
                            pe.wait_ge(s.on_ready, n)
                        for g in range(NG):
                            q = n * NG + g
                            if q >= 2:
                                pe.wait_ge(s.et_ready, q - 1)
                            elif q == 0:
                                pass
                            for j in range(4 * g, min(4 * g + 4, KT3)):
                                last = nc.tensor.transpose(k.bank(5 + q % 2, P, P, (j % 4) * P), ex[:, n % 2, j * P:(j + 1) * P], k.ident[:])
                            last.then_inc(s.et_in_psum, 1)
                            if g >= 1:
                                pv(g - 1)
                        pv(NG - 1)

                    def turn_out(h):
                        n = b * H3 + h
                        pe.wait_ge(s.on_ready, n + 1)
                        nc.tensor.transpose(k.bank(7, P, P, 256), on[:, n % 2], k.ident[:]).then_inc(s.ot_in_psum, 1)
                        pe.wait_ge(s.ot_taken, n + 1)
                    scores(0)
                    for h in range(H3):
                        if h + 1 < H3:
                            scores(h + 1)
                        if h >= 1:
                            turn_out(h - 1)
                        values(h)
                    turn_out(H3 - 1)
                    if b:
                        pe.wait_ge(s.out_taken, b)
                    matmul_acc(nc, k.bank(6, P, D), [(ot[:, h], wo[:, h]) for h in range(H3)]).then_inc(s.out_ready, 1)
                    if b == 0:
                        pe.wait_ge(s.out_taken, 1)

            @block.gpsimd
            def _(pool):
                def norm(n):
                    pool.wait_ge(s.rstd_ready, n + 1)
                    pool.wait_ge(s.turned, n + 1)
                    r = n % 4
                    nc.gpsimd.tensor_tensor(t1[:, r], t1[:, r], st[:, r, 2].unsqueeze(2).to_broadcast([P, 4, HD3]), ALU.mult).then_inc(s.normed, 1)
                for n in range(B * NI):
                    pool.wait_ge(s.mults_done, n + 1)
                    nc.gpsimd.tensor_tensor(t1[:, n % 4], t1[:, n % 4], t2[:, n % 2], ALU.add).then_inc(s.turned, 1)
                    if n % NI >= 2:
                        norm(n - 2)
                    if n % NI == NI - 1:
                        norm(n - 1)
                        norm(n)

            @block.scalar
            def _(act):
                for b in range(B):
                    act.wait_ge(s.ang_ready, 2 * b + 1)
                    flat = lambda t: t.rearrange("p a n -> p (a n)")
                    nc.scalar.activation(flat(sn), flat(ang), ACT.Sin).then_inc(s.trig_ready, 1)
                    act.wait_ge(s.ang_ready, 2 * b + 2)
                    nc.scalar.activation(flat(cs), flat(turn), ACT.Sin).then_inc(s.trig_ready, 1)

                    def take(i):
                        n = b * NI + i
                        act.wait_ge(s.t_in_psum, n + 1)
                        src = k.bank(4 + n % 2).rearrange("p (h n) -> p h n", h=4)
                        dst = qt[:, 4 * i:4 * i + 4] if i < NQ else kt[:, :, (i - NQ) * P:(i - NQ + 1) * P]
                        nc.scalar.copy(dst, src).then_inc(s.t_taken, 1)

                    def root(i):
                        n = b * NI + i
                        act.wait_ge(s.var_ready, n + 1)
                        nc.scalar.activation(st[:, n % 4, 1], st[:, n % 4, 0], ACT.Sqrt).then_inc(s.std_ready, 1)
                    for i in range(NI):
                        n = b * NI + i
                        act.wait_ge(s.mults_done, n + 1)
                        if n >= 4:
                            act.wait_ge(s.normed, n - 3)
                        for h in range(4):
                            last = nc.scalar.activation(k.bank(n % 2, P, HD3, h * HD3), k.bank(n % 2, P, HD3, h * HD3), ACT.Square, accum_out=st[:, n % 4, 2, h:h + 1])
                        last.then_inc(s.sq_done, 1)
                        if i >= NQ:
                            m = b * KT3 + i - NQ
                            act.wait_ge(s.v_in_psum, m + 1)
                            nc.scalar.copy(vt[:, i - NQ], k.bank(2 + m % 2)).then_inc(s.v_taken, 1)
                        if i >= 1:
                            root(i - 1)
                        if i >= 4:
                            take(i - 4)
                    root(NI - 1)
                    for i in range(NI - 4, NI):
                        take(i)
                    for h in range(H3):
                        n = b * H3 + h
                        act.wait_ge(s.neg_ready, n + 1)
                        if n >= 2:
                            act.wait_ge(s.et_in_psum, NG * (n - 1))
                        nc.scalar.activation(ex[:, n % 2], k.ps[:, 0:5].rearrange("p a n -> p (a n)")[:, 0:NK], ACT.Exp, bias=sm[:, n % 2, 1:2],
                                             scale=1.0 / float(np.sqrt(HD3)), accum_out=sm[:, n % 2, 2:3]).then_inc(s.exp_done, 1)
                        if h >= 1:
                            act.wait_ge(s.ot_in_psum, n)
                            nc.scalar.copy(ot[:, h - 1], k.bank(7, P, P, 256)).then_inc(s.ot_taken, 1)
                    act.wait_ge(s.ot_in_psum, (b + 1) * H3)
                    nc.scalar.copy(ot[:, H3 - 1], k.bank(7, P, P, 256)).then_inc(s.ot_taken, 1)

            @block.vector
            def _(dve):
                link = chain(dve, s.dve_step)
                dve.wait_ge(k.w_loaded[9], NW)
                link(nc.vector.tensor_copy(posf[:], posi[:]))
                for b in range(B):
                    flat = lambda t: t.rearrange("p a n -> p (a n)")
                    link(nc.vector.tensor_tensor(ang, invf[:].unsqueeze(1).to_broadcast([P, KT3, HALF]),
                                                 posf[:, b].unsqueeze(2).to_broadcast([P, KT3, HALF]), ALU.mult))
                    reduce_angle(nc, link, flat(ang), flat(turn))
                    link(nc.vector.scalar_tensor_tensor(out=flat(turn), in0=flat(ang), scalar=-1.0, in1=flat(ang), op0=ALU.mult, op1=ALU.max))
                    dve.sem_inc(s.ang_ready, 1)
                    link(nc.vector.tensor_scalar(flat(turn), flat(turn), -1.0, float(np.pi / 2), ALU.mult, ALU.add))
                    dve.sem_inc(s.ang_ready, 1)
                    dve.wait_ge(s.trig_ready, 2 * b + 2)
                    for lo, n, j, a in ((0, KT3, 1, 0), (KT3, 1, 0, KT3 - 1)):
                        cc, ss = cs[:, a:a + n], sn[:, a:a + n]
                        for hf in range(2):
                            o = slice(hf * HALF, (hf + 1) * HALF)
                            other = slice((1 - hf) * HALF, (2 - hf) * HALF)
                            link(nc.vector.tensor_tensor(tc[:, lo:lo + n, o], cc, nw[:, j, o].unsqueeze(1).to_broadcast([P, n, HALF]), ALU.mult))
                            link(nc.vector.tensor_tensor(ts[:, lo:lo + n, o], ss, nw[:, j, other].unsqueeze(1).to_broadcast([P, n, HALF]), ALU.mult))
                        link(nc.vector.tensor_scalar(ts[:, lo:lo + n, 0:HALF], ts[:, lo:lo + n, 0:HALF], -1.0, None, ALU.mult))

                    def variance(i):
                        n = b * NI + i
                        dve.wait_ge(s.sq_done, n + 1)
                        nc.vector.tensor_scalar(st[:, n % 4, 0], st[:, n % 4, 2], 1.0 / HD3, RMS_EPS, ALU.mult, ALU.add).then_inc(s.var_ready, 1)

                    def rstd(i):
                        n = b * NI + i
                        dve.wait_ge(s.std_ready, n + 1)
                        nc.vector.reciprocal(st[:, n % 4, 2], st[:, n % 4, 1]).then_inc(s.rstd_ready, 1)
                    for i in range(NI):
                        n = b * NI + i
                        e = KT3 if i < NQ else i - NQ
                        dve.wait_ge(s.proj_in_psum, n + 1)
                        if n >= 4:
                            dve.wait_ge(s.t_in_psum, n - 3)
                        if n >= 2:
                            dve.wait_ge(s.turned, n - 1)
                        src = k.bank(n % 2).rearrange("p (h n) -> p h n", h=4)
                        link(nc.vector.tensor_tensor(t1[:, n % 4], src, tc[:, e:e + 1].to_broadcast([P, 4, HD3]), ALU.mult))
                        for hf in range(2):
                            o = slice(hf * HALF, (hf + 1) * HALF)
                            other = slice((1 - hf) * HALF, (2 - hf) * HALF)
                            last = nc.vector.tensor_tensor(t2[:, n % 2, :, o], src[:, :, other], ts[:, e:e + 1, o].to_broadcast([P, 4, HALF]), ALU.mult)
                            if hf == 0:
                                link(last)
                        last.then_inc(s.mults_done, 1)
                        if i >= 1:
                            variance(i - 1)
                        if i >= 2:
                            rstd(i - 2)
                    variance(NI - 1)
                    rstd(NI - 2)
                    rstd(NI - 1)
                    for h in range(H3 + 1):
                        n = b * H3 + h
                        if h < H3:
                            dve.wait_ge(s.scores_in_psum, n + 1)
                            link(nc.vector.reduce_max(sm[:, n % 2, 0:1], k.ps[:, 0:5].rearrange("p a n -> p (a n)")[:, 0:NK], AX.X))
                            nc.vector.tensor_scalar(sm[:, n % 2, 1:2], sm[:, n % 2, 0:1], -1.0 / float(np.sqrt(HD3)), None, ALU.mult).then_inc(s.neg_ready, 1)
                        if h == 0:
                            continue
                        m = n - 1
                        for g in range(NG):
                            q = m * NG + g
                            w = min(4, KT3 - 4 * g) * P
                            dve.wait_ge(s.et_in_psum, q + 1)
                            if q >= 2:
                                dve.wait_ge(s.et_used, q - 1)
                            nc.vector.tensor_copy(et[:, q % 2].rearrange("p a n -> p (a n)")[:, 0:w], k.bank(5 + q % 2, P, w)).then_inc(s.et_ready, 1)
                        link(nc.vector.reciprocal(sm[:, m % 2, 3:4], sm[:, m % 2, 2:3]))
                        dve.wait_ge(s.et_used, (m + 1) * NG)
                        nc.vector.tensor_scalar(on[:, m % 2], k.bank(7, P, HD3), sm[:, m % 2, 3:4], None, ALU.mult).then_inc(s.on_ready, 1)
                    dve.wait_ge(s.out_ready, b + 1)
                    nc.vector.tensor_tensor(k.x[:, b], k.x[:, b], k.bank(6, P, D), ALU.add).then_inc(s.out_taken, 1)


H4 = 64
N4 = 128
P4 = 8
DIN = H4 * P4
HG = 4


def l3_attn(k):
    nc, A = k.nc, k.A
    NTH = 8
    NG4 = H4 // HG
    NU = NG4 * B
    RB = 3
    W = HG * N4
    with ExitStack() as ctx:
        def sb(name, shape, dt=F32):
            return k.sb("a3_" + name, shape, dt, ctx)
        wx, wz = sb("wx", [P, DC, DIN]), sb("wz", [P, DC, DIN])
        wdl = sb("w_dt_lam", [P, DC, 2 * H4])
        wout = sb("w_out", [P, DIN // P, D])
        ring = sb("w_ring", [P, RB, 2, DC, W])
        bring = sb("bias_ring", [P, RB, 2, W])
        nw = sb("norm_w", [P, 2, N4])
        al = sb("a_log", [P, H4])
        xh, sz, y = sb("x_heads", [P, B, DIN]), sb("silu_z", [P, B, DIN]), sb("y", [P, B, DIN])
        dtr, dt, lam = sb("dt_raw", [P, 3, B, H4]), sb("dt", [P, B, H4]), sb("lam", [P, B, H4])
        la, gd, vv, ww = (sb(n, [P, B, H4]) for n in ("log_a", "g_diag", "v_next", "w_past"))
        after, strict, shift = sb("after", [P, P]), sb("strict", [P, P]), sb("shift", [P, P])
        cs = sb("cs", [P, B, H4, N4 // 2])
        sn = k.ctxt[:].rearrange("p c s -> p (c s)").rearrange("p (b h n) -> p b h n", b=B, h=H4)
        t1 = sb("t1", [P, 2, 2, HG, 2, N4 // 2])
        r1 = sb("r1", [P, 2, 2, HG, 2, N4 // 2])
        r2 = sb("r2", [P, 2, HG, 2, N4 // 2])
        junk = sb("junk", [P, 2, W], BF16)
        bct = sb("bcT", [P, 2, 2, W])
        dr, ff, ee = sb("decay_rhs", [P, 2, W]), sb("f", [P, 2, W]), sb("e", [P, 3, W])
        st = sb("rms", [P, 2, 4, 2 * HG])
        yt = t1[:].rearrange("p a b h c n -> p (a b h c n)")[:, 0:DIN // P * BT].rearrange("p (c t) -> p c t", t=BT)
        thdt = r1[:].rearrange("p a b h c n -> p (a b h c n)")[:, 0:1024].rearrange("p (a n) -> p a n", a=2)
        turn = r2[:].rearrange("p a h c n -> p (a h c n)")[:, 0:512]

        def load(sp):
            def put(dst, src):
                sp.dma_start(dst, src).then_inc(k.w_loaded[10], 16)
            put(wdl[:], A["L3_attn_Wdtlam_T"].rearrange("(c p) n -> p c n", p=P))
            put(wx[:], A["L3_attn_Wx_T"].rearrange("(c p) n -> p c n", p=P))
            put(wz[:], A["L3_attn_Wz_T"].rearrange("(c p) n -> p c n", p=P))
            put(wout[:], A["L3_attn_Wout_T"].rearrange("(c p) n -> p c n", p=P))
            put(al[:], A["L3_attn_A_log"].rearrange("(a n) -> a n", a=1).to_broadcast([P, H4]))
            for j, n in enumerate("BC"):
                put(nw[:, j], A[f"L3_attn_{n}n_w_perm"].rearrange("(a n) -> a n", a=1).to_broadcast([P, N4]))
        layernorm(k, load)
        NW = 7 * 16
        names = ("dve_step pool_step masks_ready slot_loaded0 slot_loaded1 slot_loaded2 w_used bias_used xz_in_psum dl_in_psum dlT_taken "
                 "negabs_ready e_ready e1_ready ln_ready lam_ready xz_taken la_ready sh_ready sh_in_psum ww_ready "
                 "th_in_psum thdt_ready cum_in_psum cum_taken ang_ready cos_ready trig_done bc_in_psum sq_done var_ready std_ready "
                 "normed biased roped")
        names2 = ("added dr_ready fs_ready f_ready d_in_psum exp_done bcT_in_psum bcT_ready")
        with signals(nc, k.pool, names + " " + names2 + " g_in_psum") as s, \
                nc.semaphore("mg_ready") as mg_ready, nc.semaphore("y_in_psum") as y_in_psum, \
                nc.semaphore("y_taken") as y_taken, nc.semaphore("yz_ready") as yz_ready, \
                nc.semaphore("yT_in_psum") as yT_in_psum, nc.semaphore("yT_ready") as yT_ready, \
                nc.semaphore("y_out") as y_out, nc.Block() as block:
            slot = (s.slot_loaded0, s.slot_loaded1, s.slot_loaded2)
            need, total = [], [0] * RB
            for i in range(NTH + NG4):
                total[i % RB] += 16 if i < NTH else 64
                need.append(total[i % RB])

            @block.sync
            def _(sp):
                for i in range(NTH + NG4):
                    r = i % RB
                    if i >= RB:
                        sp.wait_ge(s.w_used, i - RB + 1)
                    if i < NTH:
                        sp.dma_start(ring[:, r, 0], A["L3_attn_Wth_T"].rearrange("(c p) n -> p c n", p=P)[:, :, i * 512:(i + 1) * 512]).then_inc(slot[r], 16)
                        continue
                    g = i - NTH
                    if g >= RB:
                        sp.wait_ge(s.bias_used, 2 * (g - RB + 1) * 2)
                    for j, n in enumerate("BC"):
                        sp.dma_start(ring[:, r, j], A[f"L3_attn_W{n}_T"].rearrange("(c p) n -> p c n", p=P)[:, :, g * W:(g + 1) * W]).then_inc(slot[r], 16)
                        sp.dma_start(bring[:, r, j], A[f"L3_attn_{n}_bias_perm"].rearrange("(a n) -> a n", a=1)[:, g * W:(g + 1) * W].to_broadcast([P, W])).then_inc(slot[r], 16)

            @block.tensor
            def _(pe):
                pe.wait_ge(k.w_loaded[10], NW)
                for b in range(B):
                    sl = slice(b * T, (b + 1) * T)
                    last = matmul_acc(nc, k.bank(4, P, 2 * H4, b * 2 * H4), [(k.xt[:, c, sl], wdl[:, c]) for c in range(DC)])
                last.then_inc(s.dl_in_psum, 1)
                for b in range(B):
                    sl = slice(b * T, (b + 1) * T)
                    for j, w in enumerate((wx, wz)):
                        last = matmul_acc(nc, k.bank(2 * j + b), [(k.xt[:, c, sl], w[:, c]) for c in range(DC)])
                last.then_inc(s.xz_in_psum, 1)
                pe.wait_ge(s.masks_ready, 3)
                pe.wait_ge(s.sh_ready, 1)
                nc.tensor.matmul(k.bank(5, P, B * H4), shift[:], vv[:].rearrange("p b h -> p (b h)"), start=True, stop=True).then_inc(s.sh_in_psum, 1)
                pe.wait_ge(s.xz_taken, 4)
                for m in range(NTH * B + 1):
                    if m < NTH * B:
                        i, b = divmod(m, B)
                        if b == 0:
                            pe.wait_ge(slot[i % RB], need[i])
                        if m >= 2:
                            pe.wait_ge(s.thdt_ready, m - 1)
                        last = matmul_acc(nc, k.bank(m % 2), [(k.xt[:, c, b * T:(b + 1) * T], ring[:, i % RB, 0, c]) for c in range(DC)])
                        last.then_inc(s.th_in_psum, 1)
                        if b == B - 1:
                            pe.wait_ge(s.th_in_psum, m + 1)
                            pe.sem_inc(s.w_used, 1)
                    if m >= 1:
                        q = m - 1
                        pe.wait_ge(s.thdt_ready, q + 1)
                        if q >= 2:
                            pe.wait_ge(s.cum_taken, q - 1)
                        nc.tensor.matmul(k.bank(2 + q % 2), k.keep[:], thdt[:, q % 2], start=True, stop=True).then_inc(s.cum_in_psum, 1)
                pe.wait_ge(s.cum_taken, NTH * B)

                for n in range(NU + 3):
                    if n < NU:
                        g, b = divmod(n, B)
                        i = NTH + g
                        if b == 0:
                            pe.wait_ge(slot[i % RB], need[i])
                        if n >= 1:
                            pe.wait_ge(s.normed, n)
                        for j in range(2):
                            last = matmul_acc(nc, k.bank(1 + j), [(k.xt[:, c, b * T:(b + 1) * T], ring[:, i % RB, j, c]) for c in range(DC)])
                        last.then_inc(s.bc_in_psum, 1)
                        if b == B - 1:
                            pe.wait_ge(s.bc_in_psum, n + 1)
                            pe.sem_inc(s.w_used, 1)
                    if 1 <= n < NU + 1:
                        m = n - 1
                        pe.wait_ge(s.dr_ready, m + 1)
                        if m >= 1:
                            pe.wait_ge(s.exp_done, m)
                        nc.tensor.matmul(k.bank(4), after[:], dr[:, m % 2], start=True, stop=True).then_inc(s.d_in_psum, 1)
                    if 2 <= n < NU + 2:
                        m = n - 2
                        pe.wait_ge(s.added, m + 1)
                        if m >= 1:
                            pe.wait_ge(s.bcT_ready, 2 * m)
                        for j in range(2):
                            for h in range(HG):
                                last = nc.tensor.transpose(k.bank((3, 5)[j], P, P, h * P), r1[:, m % 2, j, h].rearrange("p c n -> p (c n)"), k.ident[:])
                            last.then_inc(s.bcT_in_psum, 1)
                        pe.wait_ge(s.bcT_ready, 2 * (m + 1))
                        if m >= 1:
                            pe.wait_ge(mg_ready, m)
                        for h in range(HG):
                            sl = slice(h * P, (h + 1) * P)
                            last = nc.tensor.matmul(k.bank(6, P, P, h * P), bct[:, m % 2, 0, sl], bct[:, m % 2, 1, sl], start=True, stop=True)
                        last.then_inc(s.g_in_psum, 1)
                    if n >= 3:
                        m = n - 3
                        g, b = divmod(m, B)
                        pe.wait_ge(mg_ready, m + 1)
                        if m >= 1:
                            pe.wait_ge(y_taken, m)
                        for h in range(HG):
                            hh = g * HG + h
                            last = nc.tensor.matmul(k.bank(7, P, P4, h * P4), ee[:, m % 3, h * P:(h + 1) * P], xh[:, b, hh * P4:(hh + 1) * P4], start=True, stop=True)
                        last.then_inc(y_in_psum, 1)
                for b in range(B):
                    pe.wait_ge(yz_ready, b + 1)
                    for c in range(DIN // P):
                        last = nc.tensor.transpose(k.bank(b, P, T, c * T), y[:, b, c * P:(c + 1) * P], k.ident[:])
                    last.then_inc(yT_in_psum, 1)
                pe.wait_ge(yT_ready, B)
                for b in range(B):
                    last = matmul_acc(nc, k.bank(2, P, D, b * D), [(yt[:, c, b * T:(b + 1) * T], wout[:, c]) for c in range(DIN // P)])
                last.then_inc(y_out, 1)

            @block.scalar
            def _(act):
                fl = lambda t: t.rearrange("p b h -> p (b h)")
                act.wait_ge(k.w_loaded[10], NW)
                nc.scalar.activation(al[:], al[:], ACT.Exp).then_inc(s.e_ready, 1)
                act.wait_ge(s.negabs_ready, 1)
                nc.scalar.activation(fl(dtr[:, 1]), fl(dtr[:, 1]), ACT.Exp).then_inc(s.e_ready, 1)
                act.wait_ge(s.e1_ready, 1)
                nc.scalar.activation(fl(dtr[:, 2]), fl(dtr[:, 2]), ACT.Ln).then_inc(s.ln_ready, 1)
                nc.scalar.activation(lam[:], k.bank(4, P, B * 2 * H4).rearrange("p (b a h) -> p b a h", b=B, a=2)[:, :, 1], ACT.Sigmoid).then_inc(s.lam_ready, 1)
                act.wait_ge(s.xz_in_psum, 1)
                for b in range(B):
                    nc.scalar.activation(sz[:, b], k.bank(2 + b), ACT.Sigmoid).then_inc(s.lam_ready, 1)
                    nc.scalar.copy(xh[:, b], k.bank(b)).then_inc(s.xz_taken, 1)
                for q in range(NTH * B):
                    i, b = divmod(q, B)
                    sl = slice(i * 8, (i + 1) * 8)
                    act.wait_ge(s.ang_ready, q + 1)
                    a = sn[:, b, sl].rearrange("p h n -> p (h n)")
                    nc.scalar.activation(a, a, ACT.Sin).then_inc(s.trig_done, 1)
                    a = cs[:, b, sl].rearrange("p h n -> p (h n)")
                    nc.scalar.activation(a, a, ACT.Sin).then_inc(s.trig_done, 1)
                for n in range(NU + 2):
                    if n < NU:
                        r = n % 2
                        act.wait_ge(s.bc_in_psum, n + 1)
                        if n >= 1:
                            act.wait_ge(s.sq_done, n)
                        for j in range(2):
                            for h in range(HG):
                                last = nc.scalar.activation(junk[:, j, h * N4:(h + 1) * N4], k.bank(1 + j, P, N4, h * N4), ACT.Square,
                                                            accum_out=st[:, r, 0, j * HG + h:j * HG + h + 1])
                        last.then_inc(s.sq_done, 1)
                        act.wait_ge(s.var_ready, n + 1)
                        nc.scalar.activation(st[:, r, 2], st[:, r, 1], ACT.Sqrt).then_inc(s.std_ready, 1)
                    if 1 <= n < NU + 1:
                        m = n - 1
                        act.wait_ge(s.d_in_psum, m + 1)
                        if m >= 3:
                            act.wait_ge(y_in_psum, m - 2)
                        nc.scalar.activation(ee[:, m % 3], k.bank(4), ACT.Exp).then_inc(s.exp_done, 1)
                    if n >= 2:
                        m = n - 2
                        if m >= 2:
                            act.wait_ge(s.g_in_psum, m - 1)
                        for j in range(2):
                            act.wait_ge(s.bcT_in_psum, 2 * m + j + 1)
                            nc.scalar.copy(bct[:, m % 2, j], k.bank((3, 5)[j])).then_inc(s.bcT_ready, 1)
                for b in range(B):
                    act.wait_ge(yT_in_psum, b + 1)
                    nc.scalar.copy(yt[:, :, b * T:(b + 1) * T], k.bank(b).rearrange("p (c t) -> p c t", t=T)).then_inc(yT_ready, 1)

            @block.gpsimd
            def _(pool):
                nc.gpsimd.affine_select(out=after[:], in_=k.ones[:], compare_op=ALU.is_gt, fill=0.0, base=0, pattern=[[-1, P]],
                                        channel_multiplier=1).then_inc(s.masks_ready, 1)
                nc.gpsimd.affine_select(out=strict[:], in_=k.ones[:], compare_op=ALU.is_gt, fill=0.0, base=0, pattern=[[1, P]],
                                        channel_multiplier=-1).then_inc(s.masks_ready, 1)
                nc.gpsimd.affine_select(out=shift[:], in_=k.ones[:], compare_op=ALU.is_equal, fill=0.0, base=-1, pattern=[[-1, P]],
                                        channel_multiplier=1).then_inc(s.masks_ready, 1)
                pool.wait_ge(s.masks_ready, 3)
                pool.wait_ge(s.ww_ready, 1)
                for n in range(NU + 1):
                    if n >= 1:
                        m = n - 1
                        g, b = divmod(m, B)
                        if m >= 2:
                            pool.wait_ge(mg_ready, m - 1)
                        for h in range(HG):
                            hh = g * HG + h
                            last = nc.gpsimd.tensor_scalar(ff[:, m % 2, h * P:(h + 1) * P], strict[:], ww[:, b, hh:hh + 1], 1.0, ALU.mult, ALU.mult)
                        last.then_inc(s.fs_ready, 1)
                    if n < NU:
                        g, b = divmod(n, B)
                        i = NTH + g
                        pool.wait_ge(slot[i % RB], need[i])
                        pool.wait_ge(s.normed, n + 1)
                        for j in range(2):
                            a = t1[:, n % 2, j].rearrange("p h c n -> p (h c n)")
                            last = nc.gpsimd.tensor_tensor(a, a, bring[:, i % RB, j], ALU.add).then_inc(s.bias_used, 1)
                    if n >= 1:
                        m = n - 1
                        pool.wait_ge(s.roped, m + 1)
                        for j in range(2):
                            for hf, op in ((0, ALU.subtract), (1, ALU.add)):
                                a = r1[:, m % 2, j, :, hf]
                                last = nc.gpsimd.tensor_tensor(a, a, r2[:, j, :, hf], op)
                        last.then_inc(s.added, 1)

            @block.vector
            def _(dve):
                link = chain(dve, s.dve_step)
                fl = lambda t: t.rearrange("p b h -> p (b h)")
                dve.wait_ge(s.dl_in_psum, 1)
                dl = k.bank(4, P, B * 2 * H4).rearrange("p (b a h) -> p b a h", b=B, a=2)
                link(nc.vector.tensor_copy(dtr[:, 0], dl[:, :, 0]))
                nc.vector.scalar_tensor_tensor(out=fl(dtr[:, 1]), in0=fl(dtr[:, 0]), scalar=-1.0, in1=fl(dtr[:, 0]), op0=ALU.mult, op1=ALU.min).then_inc(s.negabs_ready, 1)
                dve.wait_ge(s.e_ready, 2)
                nc.vector.tensor_scalar(fl(dtr[:, 2]), fl(dtr[:, 1]), 1.0, None, ALU.add).then_inc(s.e1_ready, 1)
                dve.wait_ge(s.ln_ready, 1)
                link(nc.vector.scalar_tensor_tensor(out=fl(dt[:]), in0=fl(dtr[:, 0]), scalar=0.0, in1=fl(dtr[:, 2]), op0=ALU.max, op1=ALU.add))
                for b in range(B):
                    link(nc.vector.scalar_tensor_tensor(out=la[:, b], in0=dt[:, b], scalar=-1.0, in1=al[:], op0=ALU.mult, op1=ALU.mult))
                dve.wait_ge(s.lam_ready, 1)
                link(nc.vector.tensor_tensor(fl(gd[:]), fl(lam[:]), fl(dt[:]), ALU.mult))
                nc.vector.tensor_tensor(fl(vv[:]), fl(dt[:]), fl(gd[:]), ALU.subtract).then_inc(s.sh_ready, 1)
                dve.wait_ge(s.sh_in_psum, 1)
                nc.vector.tensor_tensor(fl(ww[:]), fl(gd[:]), k.bank(5, P, B * H4), ALU.add).then_inc(s.ww_ready, 1)
                dve.wait_ge(s.lam_ready, 1 + B)
                for b in range(B):
                    nc.vector.tensor_tensor(sz[:, b], sz[:, b], k.bank(2 + b), ALU.mult).then_inc(s.xz_taken, 1)

                def angles(q):
                    i, b = divmod(q, B)
                    sl = slice(i * 8, (i + 1) * 8)
                    a = sn[:, b, sl].rearrange("p h n -> p (h n)")
                    c = cs[:, b, sl].rearrange("p h n -> p (h n)")
                    dve.wait_ge(s.cum_in_psum, q + 1)
                    nc.vector.tensor_copy(a, k.bank(2 + q % 2)).then_inc(s.cum_taken, 1)
                    dve.wait_ge(s.cum_taken, q + 1)
                    reduce_angle(nc, link, a, turn)
                    link(nc.vector.scalar_tensor_tensor(out=c, in0=a, scalar=-1.0, in1=a, op0=ALU.mult, op1=ALU.max))
                    nc.vector.tensor_scalar(c, c, -1.0, float(np.pi / 2), ALU.mult, ALU.add).then_inc(s.ang_ready, 1)
                for q in range(NTH * B + 1):
                    if q < NTH * B:
                        i, b = divmod(q, B)
                        dve.wait_ge(s.th_in_psum, q + 1)
                        if q >= 2:
                            dve.wait_ge(s.cum_in_psum, q - 1)
                        nc.vector.tensor_tensor(thdt[:, q % 2].rearrange("p (h n) -> p h n", h=8), k.bank(q % 2).rearrange("p (h n) -> p h n", h=8),
                                                dt[:, b, i * 8:(i + 1) * 8].unsqueeze(2).to_broadcast([P, 8, N4 // 2]), ALU.mult).then_inc(s.thdt_ready, 1)
                    if q >= 1:
                        angles(q - 1)
                dve.wait_ge(s.trig_done, 2 * NTH * B)

                for n in range(NU + 3):
                    r = n % 2
                    if n < NU:
                        dve.wait_ge(s.sq_done, n + 1)
                        nc.vector.tensor_scalar(st[:, r, 1], st[:, r, 0], 1.0 / N4, RMS_EPS, ALU.mult, ALU.add).then_inc(s.var_ready, 1)
                    if 1 <= n < NU + 1:
                        m = n - 1
                        g, b = divmod(m, B)
                        if m >= 2:
                            dve.wait_ge(s.d_in_psum, m - 1)
                        for h in range(HG):
                            hh = g * HG + h
                            last = nc.vector.tensor_scalar(dr[:, m % 2, h * P:(h + 1) * P], k.keep[:], la[:, b, hh:hh + 1], None, ALU.mult)
                        last.then_inc(s.dr_ready, 1)
                        dve.wait_ge(s.fs_ready, m + 1)
                        for h in range(HG):
                            hh = g * HG + h
                            fh = ff[:, m % 2, h * P:(h + 1) * P]
                            last = nc.vector.scalar_tensor_tensor(out=fh, in0=k.ident[:], scalar=gd[:, b, hh:hh + 1], in1=fh, op0=ALU.mult, op1=ALU.add)
                        last.then_inc(s.f_ready, 1)
                    if n < NU:
                        dve.wait_ge(s.std_ready, n + 1)
                        if n >= 2:
                            dve.wait_ge(s.roped, n - 1)
                        link(nc.vector.reciprocal(st[:, r, 3], st[:, r, 2]))
                        for j in range(2):
                            for h in range(HG):
                                last = nc.vector.scalar_tensor_tensor(out=t1[:, r, j, h].rearrange("p c n -> p (c n)"), in0=k.bank(1 + j, P, N4, h * N4),
                                                                      scalar=st[:, r, 3, j * HG + h:j * HG + h + 1], in1=nw[:, j], op0=ALU.mult, op1=ALU.mult)
                        last.then_inc(s.normed, 1)
                    if 1 <= n < NU + 1:
                        m = n - 1
                        g, b = divmod(m, B)
                        dve.wait_ge(s.bias_used, 2 * (m + 1))
                        if m >= 2:
                            dve.wait_ge(s.bcT_in_psum, 2 * (m - 1))
                        if m >= 1:
                            dve.wait_ge(s.added, m)
                        cc = cs[:, b, g * HG:(g + 1) * HG]
                        ss = sn[:, b, g * HG:(g + 1) * HG]
                        for j in range(2):
                            nc.vector.tensor_tensor(r1[:, m % 2, j], t1[:, m % 2, j], cc.unsqueeze(2).to_broadcast([P, HG, 2, N4 // 2]), ALU.mult)
                            for hf in range(2):
                                last = nc.vector.tensor_tensor(r2[:, j, :, hf], t1[:, m % 2, j, :, 1 - hf], ss, ALU.mult)
                        last.then_inc(s.roped, 1)
                    if 2 <= n < NU + 2:
                        m = n - 2
                        g, b = divmod(m, B)
                        dve.wait_ge(s.exp_done, m + 1)
                        dve.wait_ge(s.f_ready, m + 1)
                        link(nc.vector.tensor_tensor(ee[:, m % 3], ee[:, m % 3], ff[:, m % 2], ALU.mult))
                        dve.wait_ge(s.g_in_psum, m + 1)
                        nc.vector.tensor_tensor(ee[:, m % 3], ee[:, m % 3], k.bank(6), ALU.mult).then_inc(mg_ready, 1)
                    if n >= 3:
                        m = n - 3
                        g, b = divmod(m, B)
                        dve.wait_ge(y_in_psum, m + 1)
                        nc.vector.tensor_copy(y[:, b, g * HG * P4:(g + 1) * HG * P4], k.bank(7, P, HG * P4)).then_inc(y_taken, 1)
                dve.wait_ge(y_taken, NU)
                for b in range(B):
                    nc.vector.tensor_tensor(y[:, b], y[:, b], sz[:, b], ALU.mult).then_inc(yz_ready, 1)
                dve.wait_ge(y_out, 1)
                xf = k.x[:].rearrange("p b d -> p (b d)")
                nc.vector.tensor_tensor(xf, xf, k.bank(2), ALU.add)


MLP = 2048
MATS = ("gate", "up", "down")
CW = 512


def l3_ffn(k):
    nc, A = k.nc, k.A
    NC = MLP // CW
    NS = NC * 3 * 2
    NT = MLP // P
    TPC = CW // P
    with ExitStack() as ctx:
        def sb(name, shape, dt=F32):
            return k.sb("f3_" + name, shape, dt, ctx)
        packed = sb("packed", [P, 3, MLP], I32)
        scale = sb("scales", [P, 3, MLP])
        xeo = sb("x_even_odd_T", [P, 2, BT])
        wd = sb("weights", [P, 3, 2, 2, CW])
        mg, sg = sb("magnitude", [P, 2, CW], I32), sb("sign_bit", [P, 2, CW], I32)
        m4, m6, ss = sb("max4", [P, 2, CW]), sb("max6", [P, 2, CW]), sb("signed_scale", [P, 2, CW])
        act_g, inter = sb("gelu", [P, 2, BT]), sb("inter", [P, 3, BT])

        def load(sp):
            for c in range(NC):
                sl = slice(c * CW, (c + 1) * CW)
                for j in range(3):
                    sp.dma_start(packed[:, j, sl], A["L3_ffn_packed_T"][j, :, sl]).then_inc(k.p_loaded[c], 16)
                    sp.dma_start(scale[:, j, sl], A["L3_ffn_scales_T"][j, :, sl].unsqueeze(1).to_broadcast([8, 16, CW])).then_inc(k.p_loaded[c], 16)
        layernorm(k, load)
        names = ("dve_step bits_ready pool_step scale_ready w_ready xT_in_psum xT_ready gu_in_psum gelu_ready inter_ready down_done")
        with signals(nc, k.pool, names) as s, nc.Block() as block:
            @block.tensor
            def _(pe):
                for e in range(2):
                    for b in range(B):
                        last = nc.tensor.transpose(k.bank(5, P, T, e * BT + b * T), k.xn[:, b, e::2], k.ident[:])
                last.then_inc(s.xT_in_psum, 1)
                pe.wait_ge(s.xT_ready, 1)

                def down(i):
                    c, j, par = i // TPC, (i % TPC) // 2, i % 2
                    pe.wait_ge(s.inter_ready, i + 1)
                    pe.wait_ge(s.w_ready, 6 * c + 6)
                    for b in range(B):
                        last = nc.tensor.matmul(k.bank(6 + b, P, D), inter[:, i % 3, b * T:(b + 1) * T], wd[:, 2, c % 2, par, j * D:(j + 1) * D],
                                                start=(i == 0), stop=(i == NT - 1))
                    last.then_inc(s.down_done, 1)
                for i in range(NT):
                    c = i // TPC
                    pe.wait_ge(s.w_ready, 6 * c + 4)
                    if i >= 4:
                        pe.wait_ge(s.inter_ready, i - 3)
                    sl = slice((i % TPC) * P, (i % TPC + 1) * P)
                    for j in range(2):
                        last = matmul_acc(nc, k.bank(i % 4, P, BT, j * BT), [(wd[:, j, c % 2, e, sl], xeo[:, e]) for e in range(2)])
                    last.then_inc(s.gu_in_psum, 1)
                    if i >= 1:
                        down(i - 1)
                down(NT - 1)

            @block.scalar
            def _(act):
                act.wait_ge(s.xT_in_psum, 1)
                nc.scalar.copy(xeo[:].rearrange("p c t -> p (c t)"), k.bank(5)).then_inc(s.xT_ready, 1)
                for i in range(NT):
                    act.wait_ge(s.gu_in_psum, i + 1)
                    if i >= 2:
                        act.wait_ge(s.inter_ready, i - 1)
                    nc.scalar.activation(act_g[:, i % 2], k.bank(i % 4, P, BT), ACT.Gelu_apprx_tanh).then_inc(s.gelu_ready, 1)

            @block.gpsimd
            def _(pool):
                for v in range(NS):
                    r = v % 2
                    c, j = divmod(v // 2, 3)
                    pool.wait_ge(k.p_loaded[c], 96)
                    pool.wait_ge(s.bits_ready, v + 1)
                    if v >= 2:
                        pool.wait_ge(s.w_ready, v - 1)
                    nc.gpsimd.tensor_scalar(ss[:, r], sg[:, r], -1.0, 0.5, ALU.mult, ALU.add).then_inc(s.pool_step, 1)
                    nc.gpsimd.tensor_scalar(m4[:, r], mg[:, r], 7.0, 4.0, ALU.min, ALU.max)
                    nc.gpsimd.tensor_scalar(m6[:, r], mg[:, r], 7.0, 6.0, ALU.min, ALU.max)
                    pool.wait_ge(s.pool_step, v + 1)
                    nc.gpsimd.tensor_tensor(ss[:, r], ss[:, r], scale[:, j, c * CW:(c + 1) * CW], ALU.mult).then_inc(s.scale_ready, 1)

            @block.vector
            def _(dve):
                link = chain(dve, s.dve_step)

                def bits(v):
                    r = v % 2
                    c, j = divmod(v // 2, 3)
                    dve.wait_ge(k.p_loaded[c], 96)
                    if v >= 2:
                        dve.wait_ge(s.scale_ready, v - 1)
                    w = packed[:, j, c * CW:(c + 1) * CW]
                    nc.vector.tensor_scalar(mg[:, r], w, 4 * (v % 2), 7, ALU.logical_shift_right, ALU.bitwise_and)
                    nc.vector.tensor_scalar(sg[:, r], w, 4 * (v % 2) + 3, 1, ALU.logical_shift_right, ALU.bitwise_and).then_inc(s.bits_ready, 1)

                def weights(v):
                    r = v % 2
                    c, j = divmod(v // 2, 3)
                    dve.wait_ge(s.scale_ready, v + 1)
                    if c >= 2:
                        dve.wait_ge(s.down_done, TPC * (c - 1))
                    link(nc.vector.scalar_tensor_tensor(out=m4[:, r], in0=m6[:, r], scalar=2.0, in1=m4[:, r], op0=ALU.mult, op1=ALU.add))
                    link(nc.vector.scalar_tensor_tensor(out=m4[:, r], in0=mg[:, r], scalar=-16.0, in1=m4[:, r], op0=ALU.add, op1=ALU.add))
                    nc.vector.tensor_tensor(wd[:, j, c % 2, v % 2], m4[:, r], ss[:, r], ALU.mult).then_inc(s.w_ready, 1)

                def product(i):
                    dve.wait_ge(s.gelu_ready, i + 1)
                    if i >= 3:
                        dve.wait_ge(s.down_done, i - 2)
                    nc.vector.tensor_tensor(inter[:, i % 3], act_g[:, i % 2], k.bank(i % 4, P, BT, BT), ALU.mult).then_inc(s.inter_ready, 1)
                bits(0)
                for v in range(NS):
                    if v + 1 < NS:
                        bits(v + 1)
                    weights(v)
                    c, q = divmod(v, 6)
                    if c >= 1 and q < TPC:
                        product(TPC * (c - 1) + q)
                for q in range(TPC):
                    product(NT - TPC + q)
                dve.wait_ge(s.down_done, NT)
                for b in range(B):
                    nc.vector.tensor_tensor(k.x[:, b], k.x[:, b], k.bank(6 + b, P, D), ALU.add)


def layouts(i):
    c = np.ascontiguousarray
    d = {n: c(a) for n, a in i.items()}
    d["ctxT"] = c(i["ctx_2048"].reshape(KEYS, D).T)
    for n in "ifgo":
        d["L0_attn_W" + n + "_T"] = c(i["L0_attn_W" + n].T)
    d["L0_ffn_gate_w_T"] = c(i["L0_ffn_gate_w"].T)

    def experts(a, b):
        return np.concatenate([a, b.reshape(D, SHARED, INNER).transpose(1, 0, 2)])
    g, u = experts(i["L0_ffn_w_gate"], i["L0_ffn_sw_gate"]), experts(i["L0_ffn_w_up"], i["L0_ffn_sw_up"])
    d["L0_ffn_gate_up"] = c(np.stack([g, u], 2).reshape(EXPERTS + SHARED, DC, P, 2, INNER).transpose(0, 2, 1, 3, 4))
    dn = np.concatenate([i["L0_ffn_w_down"], i["L0_ffn_sw_down"].reshape(SHARED, INNER, D)])
    d["L0_ffn_down"] = c(dn.reshape(EXPERTS + SHARED, 2, IH, D).transpose(0, 2, 1, 3))
    d["L1_decay_ch"] = np.repeat(i["L1_attn_decay_param"], HD)
    d["L1_ffn_b1_T"] = c(i["L1_ffn_b1"].T)
    for n in ("Wq", "Wg", "Wkv", "Wo"):
        d["L2_xattn_" + n + "_T"] = c(i["L2_xattn_" + n].T)
    for n in "qkvo":
        d["L2_attn_W" + n + "_T"] = c(i["L2_attn_W" + n].T)
    ang = np.arange(1, T + 1, dtype=np.float64)[:, None] * 10000.0 ** (-2.0 * np.arange(HD // 2) / HD)[None]
    d["L2_cos"] = np.concatenate([np.cos(ang), np.cos(ang)], 1).astype(np.float32)
    d["L2_sin"] = np.concatenate([-np.sin(ang), np.sin(ang)], 1).astype(np.float32)
    d["L2_ffn_W_T"] = c(i["L2_ffn_W"].T)
    d["L2_ffn_lora_A_T"] = c(i["L2_ffn_lora_A"].reshape(P, D).T)
    d["L2_ffn_lora_B_T"] = c(i["L2_ffn_lora_B"].transpose(0, 2, 1).reshape(P, D))
    d["L2_ffn_gate_w_T"] = c(i["L2_ffn_gate_w"].T)
    for n in ("Wq", "Wk", "Wv", "Wo"):
        d["L3_xattn_" + n + "_T"] = c(i["L3_xattn_" + n].T)
    d["L3_inv_freq"] = (np.float32(1) / np.float32(10000.0) ** (np.arange(0, HD3, 2, dtype=np.float32) / np.float32(HD3))).astype(np.float32)
    even_first = np.concatenate([np.arange(0, N4, 2), np.arange(1, N4, 2)])
    for n in "BC":
        d[f"L3_attn_W{n}_T"] = c(i["L3_attn_W" + n].reshape(H4, N4, D)[:, even_first].reshape(H4 * N4, D).T)
        d[f"L3_attn_{n}_bias_perm"] = c(i[f"L3_attn_{n}_bias"][:, even_first]).reshape(-1)
        d[f"L3_attn_{n}n_w_perm"] = c(i[f"L3_attn_{n}n_w"][even_first])
    for n in ("Wx", "Wz", "Wth", "Wout"):
        d[f"L3_attn_{n}_T"] = c(i["L3_attn_" + n].T)
    d["L3_attn_Wdtlam_T"] = c(np.concatenate([i["L3_attn_Wdt"], i["L3_attn_Wlam"]]).T)
    def by_parity(w):
        return w.reshape(MLP // 256, P, 2, -1).transpose(3, 0, 2, 1).reshape(-1, MLP)
    down = i["L3_ffn_down_W_packed"].T.reshape(8, P, D).transpose(1, 0, 2).reshape(P, MLP)
    d["L3_ffn_packed_T"] = c(np.stack([by_parity(i["L3_ffn_gate_W_packed"]), by_parity(i["L3_ffn_up_W_packed"]), down]))
    down = i["L3_ffn_down_scales"].T.reshape(8, 8, D).transpose(1, 0, 2).reshape(8, MLP)
    d["L3_ffn_scales_T"] = c(np.stack([by_parity(i["L3_ffn_gate_scales"]), by_parity(i["L3_ffn_up_scales"]), down]))
    return d


STAGES = (l0_xattn, l0_attn, l0_ffn, l1_xattn, l1_attn, l1_ffn, l2_xattn, l2_attn, l2_ffn, l3_xattn, l3_attn, l3_ffn)

READ = ("x", "ctxT", "L0_xattn_Wq", "L0_xattn_Wkv", "L0_xattn_Wp", "L0_xattn_bq", "L0_xattn_bkv", "L0_xattn_bp",
        "L0_attn_Wi_T", "L0_attn_Wf_T", "L0_attn_Wg_T", "L0_attn_Wo_T", "L0_attn_gnorm_w", "L0_ffn_gate_w_T",
        "L0_ffn_gate_up", "L0_ffn_down", "mask_BxS2_bk0", "ctx_2048", "L1_decay_ch", "L1_attn_w_qkv",
        "L1_attn_w_out", "L1_ffn_gamma", "L1_ffn_beta", "L1_ffn_scale", "L1_ffn_b1_T", "L1_ffn_mu", "L1_ffn_W1",
        "L1_ffn_W2", "L1_ffn_b2", "L2_xattn_Wkv_T", "L2_xattn_Wq_T", "L2_xattn_Wg_T", "L2_xattn_Wo_T", "L2_xattn_bg",
        "L2_attn_Wq_T", "L2_attn_Wk_T", "L2_attn_Wv_T", "L2_attn_Wo_T", "L2_attn_bq", "L2_attn_bk", "L2_attn_bv",
        "L2_attn_bo", "L2_cos", "L2_sin", "L2_ffn_W_T", "L2_ffn_lora_A_T", "L2_ffn_gate_w_T", "L2_ffn_lora_B_T",
        "L2_ffn_b", "L2_ffn_gate_b", "L3_xattn_Wk_T", "L3_xattn_Wv_T", "L3_xattn_Wq_T", "L3_xattn_Wo_T",
        "L3_xattn_q_norm_w", "L3_xattn_k_norm_w", "L3_inv_freq", "pos_BxS2", "itok_BxS_4096_4607",
        "L3_attn_Wdtlam_T", "L3_attn_Wx_T", "L3_attn_Wz_T", "L3_attn_Wout_T", "L3_attn_A_log", "L3_attn_Bn_w_perm",
        "L3_attn_Cn_w_perm", "L3_attn_Wth_T", "L3_attn_WB_T", "L3_attn_B_bias_perm", "L3_attn_WC_T",
        "L3_attn_C_bias_perm", "L3_ffn_packed_T", "L3_ffn_scales_T")


def build(nc, A, out):
    with ExitStack() as ctx:
        k = Core(nc, ctx, A)
        constants(k, A["x"])
        for stage in STAGES:
            stage(k)
        with nc.semaphore("stored") as stored, nc.Block() as block:
            @block.sync
            def _(sp):
                sp.dma_start(out.rearrange("b t d -> t b d"), k.x[:]).then_inc(stored, 16)
                sp.wait_ge(stored, 16)


def kernel(**inputs):
    import concourse.bacc as bacc
    from concourse.bass_utils import run_bass_kernel_spmd

    arrays = layouts({name: np.asarray(a) for name, a in inputs.items()})
    nc = bacc.Bacc("TRN2", target_bir_lowering=False, num_devices=1)
    A = {name: nc.dram_tensor("in_" + name, arrays[name].shape, mybir.dt.from_np(arrays[name].dtype), kind="ExternalInput").ap()
         for name in READ}
    out = nc.dram_tensor("out_x", (B, T, D), F32, kind="ExternalOutput").ap()
    build(nc, A, out)
    result = run_bass_kernel_spmd(nc, [{"in_" + name: arrays[name] for name in READ}], core_ids=[0])
    return result.results[0]["out_x"]
```

```python
from contextlib import ExitStack, contextmanager

import numpy as np
import concourse.bass as bass
from concourse import mybir

ALU = mybir.AluOpType
ACT = mybir.ActivationFunctionType
AX = mybir.AxisListType
F32 = mybir.dt.float32
BF16 = mybir.dt.bfloat16
I32 = mybir.dt.int32

P = 128
B = 2
T = 128
D = 256
DC = D // P
BT = B * T
S2 = 2048
KEYS = B * S2
NKT = KEYS // P
LN_EPS = 1e-5
ROUND = float(3 * 2 ** 22)
NEG = -1e30


class Signals:

    def __init__(self, names, pool):
        self.of = dict(zip(names, pool))

    def __getattr__(self, name):
        return self.of[name]


class Pool(list):
    used = 0


@contextmanager
def signals(nc, pool, names):
    names = names.split()
    assert len(names) <= len(pool), len(names)
    assert pool.used == 0
    yield Signals(names, pool)
    pool.used = len(names)


def chain(engine, sem):
    count = [0]

    def link(ins):
        count[0] += 1
        ins.then_inc(sem, 1)
        engine.wait_ge(sem, count[0])
    return link


LN_NAMES = "dve_step var_ready std_ready xn_ready xt_in_psum".split()


class Core:

    def __init__(self, nc, ctx, A):
        self.nc, self.A, self.ctx = nc, A, ctx
        self.n = 0
        self.x = self.sb("x_res", [P, B, D])
        self.xn = self.sb("x_normed", [P, B, D])
        self.xt = self.sb("x_normed_T", [P, DC, BT])
        self.ident = self.sb("ident", [P, P])
        self.ones = self.sb("ones", [P, P])
        self.blocks = self.sb("head_blocks", [P, P])
        self.keep = self.sb("upper_incl", [P, P])
        self.ctxt = self.sb("ctx_T", [P, DC, KEYS])
        self.ctx_loaded = [ctx.enter_context(nc.semaphore(f"ctx_loaded_{i}")) for i in range(4)]
        self.stat = self.sb("ln_stats", [P, B, 6])
        self.mv = self.sb("ln_mean_var", [P, B, 2])
        self.rstd = self.sb("ln_rstd", [P, B, 2])
        self.ps = ctx.enter_context(nc.psum_tensor("banks", [P, 8, 512], F32))
        self.w_loaded = [ctx.enter_context(nc.semaphore(f"weights_loaded_{i}")) for i in range(12)]
        self.p_loaded = [ctx.enter_context(nc.semaphore(f"packed_loaded_{i}")) for i in range(4)]
        self.mu_loaded = ctx.enter_context(nc.semaphore("mu_loaded"))
        self.out_w_loaded = ctx.enter_context(nc.semaphore("first_out_weights_loaded"))
        self.mask_loaded = ctx.enter_context(nc.semaphore("mask_loaded"))
        self.dt_w_loaded = ctx.enter_context(nc.semaphore("dt_weights_loaded"))
        self.pos_loaded = ctx.enter_context(nc.semaphore("positions_loaded"))
        self.wo_loaded = ctx.enter_context(nc.semaphore("out_weights_loaded"))
        self.pool = Pool(ctx.enter_context(nc.semaphore(f"signal_{i}")) for i in range(44))
        self.ln = Signals(LN_NAMES, [ctx.enter_context(nc.semaphore("ln_" + n)) for n in LN_NAMES])

    def sb(self, name, shape, dt=F32, ctx=None):
        return (ctx or self.ctx).enter_context(self.nc.sbuf_tensor(name, shape, dt))

    def bank(self, i, p=P, n=512, a=0):
        return self.ps[0:p, i, a:a + n]


def load_context(k, sp):
    ctx_dram = k.A["ctxT"].rearrange("(c p) s -> p c s", p=P)
    for i in range(4):
        part = slice(i * KEYS // 4, (i + 1) * KEYS // 4)
        sp.dma_start(k.ctxt[:, :, part], ctx_dram[:, :, part]).then_inc(k.ctx_loaded[i], 16)


def constants(k, x_in, load=None):
    nc = k.nc
    with signals(nc, k.pool, "x_loaded filled") as s, nc.Block() as block:
        @block.sync
        def _(sp):
            sp.dma_start(k.x[:], x_in.rearrange("b t d -> t b d")).then_inc(s.x_loaded, 16)
            if load:
                load(k, sp)
            sp.wait_ge(s.x_loaded, 16)

        @block.gpsimd
        def _(pool):
            nc.gpsimd.memset(k.ones[:], 1.0).then_inc(s.filled, 1)
            pool.wait_ge(s.filled, 1)
            nc.gpsimd.affine_select(out=k.ident[:], in_=k.ones[:], compare_op=ALU.is_equal, fill=0.0,
                                    base=0, pattern=[[-1, P]], channel_multiplier=1)
            nc.gpsimd.affine_select(out=k.keep[:], in_=k.ones[:], compare_op=ALU.is_ge, fill=0.0,
                                    base=0, pattern=[[1, P]], channel_multiplier=-1)
            heads = k.blocks[:].rearrange("p (h d) -> p h d", d=16)
            nc.gpsimd.affine_select(out=heads, in_=k.ones[:].rearrange("p (h d) -> p h d", d=16), compare_op=ALU.is_ge, fill=0.0,
                                    base=0, pattern=[[-16, P // 16], [0, 16]], channel_multiplier=1).then_inc(s.filled, 1)
            pool.wait_ge(s.filled, 2)
            nc.gpsimd.affine_select(out=heads, in_=heads, compare_op=ALU.is_ge, fill=0.0,
                                    base=15, pattern=[[16, P // 16], [0, 16]], channel_multiplier=-1)


def layernorm(k, load=None, n_loads=0):
    nc = k.nc
    s, n = k.ln, k.n
    k.n += 1
    with nc.Block() as block:
        @block.sync
        def _(sp):
            if load:
                load(sp)
            for sem in k.pool[:k.pool.used]:
                sp.sem_clear(sem)
            k.pool.used = 0

        @block.vector
        def _(dve):
            link = chain(dve, s.dve_step)
            for b in range(B):
                nc.vector.bn_stats(k.stat[:, b, :], k.x[:, b, :]).then_inc(s.dve_step, 1)
            dve.wait_ge(s.dve_step, 5 * n + 2)
            for b in range(B):
                nc.vector.bn_aggr(k.mv[:, b, :], k.stat[:, b, :]).then_inc(s.dve_step, 1)
            dve.wait_ge(s.dve_step, 5 * n + 4)
            nc.vector.tensor_scalar(k.rstd[:, :, 0], k.mv[:, :, 1], LN_EPS, None, ALU.add).then_inc(s.var_ready, 1)
            dve.wait_ge(s.std_ready, n + 1)
            nc.vector.reciprocal(k.rstd[:, :, 0], k.rstd[:, :, 1]).then_inc(s.dve_step, 1)
            dve.wait_ge(s.dve_step, 5 * n + 5)
            for b in range(B):
                nc.vector.tensor_scalar(k.xn[:, b, :], k.x[:, b, :], k.mv[:, b, 0:1], k.rstd[:, b, 0:1],
                                        ALU.subtract, ALU.mult).then_inc(s.xn_ready, 1)

        @block.scalar
        def _(act):
            act.wait_ge(s.var_ready, n + 1)
            nc.scalar.activation(k.rstd[:, :, 1], k.rstd[:, :, 0], ACT.Sqrt).then_inc(s.std_ready, 1)
            act.wait_ge(s.xt_in_psum, n + 1)
            nc.scalar.copy(k.xt[:].rearrange("p c t -> p (c t)"), k.bank(0))

        @block.tensor
        def _(pe):
            for b in range(B):
                pe.wait_ge(s.xn_ready, B * n + b + 1)
                for c in range(DC):
                    last = nc.tensor.transpose(k.bank(0, P, T, c * BT + b * T),
                                               k.xn[:, b, c * P:(c + 1) * P], k.ident[:])
            last.then_inc(s.xt_in_psum, 1)


def matmul_acc(nc, out, pairs):
    for i, (lhsT, rhs) in enumerate(pairs):
        last = nc.tensor.matmul(out, lhsT, rhs, start=(i == 0), stop=(i == len(pairs) - 1))
    return last


HEADS = 16
HD = D // HEADS
LN255 = float(np.log(255.0))
TINY = 1e-8


def l0_xattn(k):
    nc, A = k.nc, k.A
    nh = HEADS
    NP = NKT // 2
    NQC = 4
    CK = KEYS // NQC
    CB = CK // P
    with ExitStack() as ctx:
        def sb(name, shape, dt=F32):
            return k.sb("x0_" + name, shape, dt, ctx)
        wq, wkv, wp = sb("wq", [P, DC, D]), sb("wkv", [P, DC, 2 * D]), sb("wp", [P, DC, D])
        bq, bkv, bp = sb("bq", [P, D]), sb("bkv", [1, 2 * D]), sb("bp", [P, D])
        vf = sb("v_full", [P, NKT, D])
        vq = sb("v_int", [P, NKT, D], BF16)
        kt = sb("kT_parts", [P, nh // 2, KEYS], BF16)
        qt = sb("qT_int", [P, nh // 2, BT], BF16)
        kp = sb("k_parts", [P, 4, 2, nh, 4, HD], BF16)
        qp = kp[:, 2]
        kf, kr, kl = sb("k_full", [P, 3, 2, nh, HD]), sb("k_rest", [P, 2, 2, nh, HD]), sb("k_last", [P, 2, 2, nh, HD])
        ks, kri = sb("k_scale", [P, 2 * nh]), sb("k_rscale", [P, 2 * nh])
        sq, qri = sb("q_scale", [P, B, nh]), sb("q_rscale", [P, B, nh])
        qf = sb("q_full", [P, B, D])
        vmax, vall, vri = sb("v_max", [P, D]), sb("v_scale", [P, D]), sb("v_rscale", [P, D])
        identb = sb("identb", [P, P], BF16)
        mx, nb = sb("row_max8", [P, 2, 8]), sb("neg_max", [P, 2, 2])
        sums = sb("row_sum4", [P, B * nh, 4])
        rs = sb("row_sum", [P, B, nh])
        ot = kp[:].rearrange("p r a h c d -> p (r a h c d)").bitcast(F32).rearrange("p (u t) -> p u t", t=P)
        attn = sb("attn", [P, B, D])
        att = qf[:].rearrange("p b d -> p (b d)").rearrange("p (c t) -> p c t", t=BT)
        vflat = vf[:].rearrange("p a n -> p (a n)")
        ex = vflat[:, 0:3 * CK].rearrange("p (r n) -> p r n", r=3)
        eb = vflat[:, 3 * CK:3 * CK + 3 * CK // 2].bitcast(BF16).rearrange("p (r n) -> p r n", r=3)
        pt = vflat[:, 5 * CK:5 * CK + 3 * CK // 2].bitcast(BF16).rearrange("p (r a n) -> p r a n", r=3, n=P)

        def load(sp):
            sp.dma_start(bkv[:], A["L0_xattn_bkv"].rearrange("(a n) -> a n", a=1)).then_inc(k.w_loaded[0], 16)
            for dst, src in ((wkv, A["L0_xattn_Wkv"]), (wq, A["L0_xattn_Wq"])):
                sp.dma_start(dst[:], src.rearrange("(c p) n -> p c n", p=P)).then_inc(k.w_loaded[0], 16)
            sp.dma_start(bq[:], A["L0_xattn_bq"].rearrange("(a n) -> a n", a=1).to_broadcast([P, D])).then_inc(k.w_loaded[0], 16)
            load_context(k, sp)
            sp.dma_start(wp[:], A["L0_xattn_Wp"].rearrange("(c p) n -> p c n", p=P)).then_inc(k.out_w_loaded, 16)
            sp.dma_start(bp[:], A["L0_xattn_bp"].rearrange("(a n) -> a n", a=1).to_broadcast([P, D])).then_inc(k.out_w_loaded, 16)
        layernorm(k, load)

        names = ("dve_step k_in_psum v_in_psum k_taken v_taken kf_ready hi_ready mid_ready rest_ready last_ready "
                 "parts_ready kT_in_psum kT_taken q_in_psum q_parts_ready qT_in_psum qT_taken vmax_ready vscale_ready v_ready "
                 "max_scores max_taken bias_ready exp_scores exp_done rounded eT_in_psum pT_ready pT_used attn_ready oT_ready o_in_psum "
                 "attnT_in_psum attnT_ready out_in_psum zeroed")
        MAXES = (2, 2, 2, 2)
        MBANK = (0, 1, 7)
        NU = B * nh
        NCH = NU * NQC
        def part(j, c):
            return kp[:, (0, 1, 3)[j % 3], :, :, c]
        with signals(nc, k.pool, names) as s, nc.Block() as block:
            @block.tensor
            def _(pe):
                pe.wait_ge(k.w_loaded[0], 64)
                for b in range(B):
                    last = matmul_acc(nc, k.bank(7, P, D, b * D), [(k.xt[:, c, b * T:(b + 1) * T], wq[:, c]) for c in range(DC)])
                last.then_inc(s.q_in_psum, 1)

                def project(j):
                    if j % 4 == 0:
                        pe.wait_ge(k.ctx_loaded[j // 4], 16)
                    for half, taken, arrived in ((0, s.k_taken, s.k_in_psum), (1, s.v_taken, s.v_in_psum)):
                        if j >= 2:
                            pe.wait_ge(taken, j - 1)
                        for i in range(2):
                            a = (2 * j + i) * P
                            cols = slice(half * D, (half + 1) * D)
                            last = matmul_acc(nc, k.bank(2 * half + j % 2, P, D, i * D),
                                              [(k.ctxt[:, c, a:a + P], wkv[:, c, cols]) for c in range(DC)] + [(k.ones[0:1, :], bkv[:, cols])])
                        last.then_inc(arrived, 1)

                def transpose_keys(j):
                    pe.wait_ge(s.parts_ready, j + 1)
                    for i in range(2):
                        if j >= 1:
                            pe.wait_ge(s.kT_taken, 2 * (j - 1) + i + 1)
                        tgt = k.ps[:, 4 + i, :].bitcast(BF16)
                        for h in range(nh // 2):
                            last = nc.tensor.transpose(tgt[:, h * P:(h + 1) * P],
                                                       kp[:, (0, 1, 3)[j % 3], i, 2 * h:2 * h + 2].rearrange("p a c d -> p (a c d)"), identb[:])
                        last.then_inc(s.kT_in_psum, 1)
                for j in range(NP + 3):
                    if j < NP:
                        project(j)
                    if j == 1:
                        pe.wait_ge(s.q_parts_ready, 1)
                        for b in range(B):
                            for h in range(nh // 2):
                                last = nc.tensor.transpose(k.ps[:, 6 + b, :].bitcast(BF16)[:, h * P:(h + 1) * P],
                                                           qp[:, b, 2 * h:2 * h + 2].rearrange("p a c d -> p (a c d)"), identb[:])
                        last.then_inc(s.qT_in_psum, 1)
                    if j >= 3:
                        transpose_keys(j - 3)

                def scores(u, bank, a):
                    b, h = divmod(u, nh)
                    lo = 64 * (h % 2)
                    return nc.tensor.matmul(k.bank(bank), qt[lo:lo + 64, h // 2, b * T:(b + 1) * T], kt[lo:lo + 64, h // 2, a:a + 512],
                                            start=True, stop=True)

                def for_max(u, first, n):
                    for i in range(first, first + n):
                        m = 8 * u + i
                        if m >= 3:
                            pe.wait_ge(s.max_taken, m - 2)
                        scores(u, MBANK[m % 3], 512 * i).then_inc(s.max_scores, 1)

                def turn(q):
                    pe.wait_ge(s.rounded, q + 1)
                    if q >= 2:
                        pe.wait_ge(s.pT_ready, q - 1)
                    tgt = k.ps[:, 4 + q % 2, :].bitcast(BF16)
                    for i in range(CB):
                        last = nc.tensor.transpose(tgt[:, i * P:(i + 1) * P], eb[:, q % 3, i * P:(i + 1) * P], identb[:])
                    last.then_inc(s.eT_in_psum, 1)

                def values(q):
                    v, c = divmod(q, NQC)
                    h = v % nh
                    pe.wait_ge(s.pT_ready, q + 1)
                    if c == 0 and v >= 1:
                        pe.wait_ge(s.oT_ready, v)
                    for i in range(CB):
                        tile = CB * c + i
                        last = nc.tensor.matmul(k.bank(6, HD, P), vq[:, tile, h * HD:(h + 1) * HD], pt[:, q % 3, i],
                                                start=(tile == 0), stop=(tile == NKT - 1))
                    last.then_inc(s.pT_used, 1)

                pe.wait_ge(s.kT_taken, NKT)
                pe.wait_ge(s.qT_taken, 1)
                pe.wait_ge(s.v_ready, 1)
                for_max(0, 0, 8)
                for q in range(NCH + 3):
                    v, c = divmod(q, NQC)
                    if v + 1 < NU:
                        for_max(v + 1, sum(MAXES[:c]), MAXES[c])
                    if q < NCH:
                        if q >= 1:
                            pe.wait_ge(s.exp_done, q)
                        for i in range(2):
                            last = scores(v, 2 + i, c * CK + 512 * i)
                        last.then_inc(s.exp_scores, 1)
                    if 2 <= q < NCH + 2:
                        turn(q - 2)
                    if q >= 3:
                        values(q - 3)
                pe.wait_ge(s.oT_ready, NU)
                for u in range(NU):
                    last = nc.tensor.transpose(k.bank(0, P, HD, u * HD), ot[0:HD, u], k.ident[0:HD, 0:HD])
                last.then_inc(s.o_in_psum, 1)
                pe.wait_ge(s.attn_ready, B)
                for b in range(B):
                    for c in range(DC):
                        last = nc.tensor.transpose(k.bank(2, P, T, c * BT + b * T), attn[:, b, c * P:(c + 1) * P], k.ident[:])
                last.then_inc(s.attnT_in_psum, 1)
                pe.wait_ge(s.attnT_ready, 1)
                pe.wait_ge(k.out_w_loaded, 32)
                for b in range(B):
                    last = matmul_acc(nc, k.bank(1, P, D, b * D), [(att[:, c, b * T:(b + 1) * T], wp[:, c]) for c in range(DC)])
                last.then_inc(s.out_in_psum, 1)

            @block.gpsimd
            def _(pool):
                pool.memset(kp[:], 0.0)
                nc.gpsimd.tensor_copy(identb[:], k.ident[:]).then_inc(s.zeroed, 1)
                for j in range(NP + 1):
                    if j < NP:
                        pool.wait_ge(s.hi_ready, j + 1)
                        if j >= 2:
                            pool.wait_ge(s.mid_ready, j - 1)
                            pool.wait_ge(s.last_ready, j - 1)
                        nc.gpsimd.tensor_tensor(kr[:, j % 2], kf[:, j % 3], part(j, 0), ALU.subtract).then_inc(s.rest_ready, 1)
                    if j >= 1:
                        m = j - 1
                        pool.wait_ge(s.mid_ready, m + 1)
                        pool.wait_ge(s.rest_ready, m + 1)
                        if m >= 2:
                            pool.wait_ge(s.parts_ready, m - 1)
                        nc.gpsimd.tensor_tensor(kl[:, m % 2], kr[:, m % 2], part(m, 1), ALU.subtract).then_inc(s.last_ready, 1)
                pool.wait_ge(s.vmax_ready, 1)
                nc.gpsimd.partition_all_reduce(vall[:], vmax[:], P, bass.bass_isa.ReduceOp.max).then_inc(s.vscale_ready, 1)

            @block.scalar
            def _(act):
                act.wait_ge(s.zeroed, 1)

                def take_keys(j):
                    for i in range(2):
                        act.wait_ge(s.kT_in_psum, 2 * j + i + 1)
                        a = (2 * j + i) * P
                        nc.scalar.copy(kt[:, :, a:a + P], k.ps[:, 4 + i, :].bitcast(BF16).rearrange("p (h n) -> p h n", n=P)).then_inc(s.kT_taken, 1)
                for j in range(NP + 3):
                    if j < NP:
                        act.wait_ge(s.v_in_psum, j + 1)
                        nc.scalar.copy(vf[:, 2 * j:2 * j + 2].rearrange("p a n -> p (a n)"), k.bank(2 + j % 2)).then_inc(s.v_taken, 1)
                    if j == 2:
                        act.wait_ge(s.qT_in_psum, 1)
                        for b in range(B):
                            last = nc.scalar.copy(qt[:, :, b * T:(b + 1) * T],
                                                  k.ps[:, 6 + b, :].bitcast(BF16).rearrange("p (h n) -> p h n", n=P))
                        last.then_inc(s.qT_taken, 1)
                    if j < NP:
                        act.wait_ge(s.kf_ready, j + 1)
                        if j >= 3:
                            act.wait_ge(s.kT_in_psum, 2 * (j - 2))
                        nc.scalar.copy(part(j, 0), kf[:, j % 3]).then_inc(s.hi_ready, 1)
                    if 1 <= j < NP + 1:
                        m = j - 1
                        act.wait_ge(s.rest_ready, m + 1)
                        nc.scalar.copy(part(m, 1), kr[:, m % 2]).then_inc(s.mid_ready, 1)
                    if 2 <= j < NP + 2:
                        m = j - 2
                        act.wait_ge(s.last_ready, m + 1)
                        nc.scalar.copy(part(m, 2), kl[:, m % 2]).then_inc(s.parts_ready, 1)
                    if j >= 3:
                        take_keys(j - 3)
                act.wait_ge(s.v_ready, 1)
                for q in range(NCH + 2):
                    v, c = divmod(q, NQC)
                    b, h = divmod(v, nh)
                    if q < NCH:
                        if c == 0:
                            act.wait_ge(s.bias_ready, v + 1)
                        if q >= 3:
                            act.wait_ge(s.rounded, q - 2)
                        act.wait_ge(s.exp_scores, q + 1)
                        nc.scalar.activation(ex[:, q % 3], k.ps[:, 2:4, :].rearrange("p a n -> p (a n)"), ACT.Exp,
                                             bias=nb[:, v % 2, 1:2], scale=sq[:, b, h:h + 1],
                                             accum_out=sums[:, v, c:c + 1]).then_inc(s.exp_done, 1)
                    if q >= 2:
                        m = q - 2
                        act.wait_ge(s.eT_in_psum, m + 1)
                        if m >= 3:
                            act.wait_ge(s.pT_used, m - 2)
                        nc.scalar.copy(pt[:, m % 3].rearrange("p a n -> p (a n)"), k.ps[:, 4 + m % 2, :].bitcast(BF16)).then_inc(s.pT_ready, 1)
                act.wait_ge(s.attnT_in_psum, 1)
                nc.scalar.copy(qf[:].rearrange("p b d -> p (b d)"), k.bank(2)).then_inc(s.attnT_ready, 1)

            @block.vector
            def _(dve):
                link = chain(dve, s.dve_step)

                def quantise(full, src, scale, rscale, n):
                    link(nc.vector.tensor_reduce(scale, src, AX.X, ALU.max, apply_absolute_value=True))
                    link(nc.vector.tensor_scalar(scale, scale, 1.0 / 127.0, TINY, ALU.mult, ALU.max))
                    link(nc.vector.reciprocal(rscale, scale))
                    return nc.vector.tensor_tensor(full, src, rscale.unsqueeze(2).to_broadcast([P, n, HD]), ALU.mult)

                dve.wait_ge(s.q_in_psum, 1)
                dve.wait_ge(k.w_loaded[0], 64)
                dve.wait_ge(s.zeroed, 1)
                for b in range(B):
                    link(nc.vector.tensor_tensor(qf[:, b], k.bank(7, P, D, b * D), bq[:], ALU.add))
                    link(nc.vector.tensor_scalar(qf[:, b], qf[:, b], 1.0 / float(np.sqrt(np.float32(HD))), None, ALU.mult))
                    q3 = qf[:, b].rearrange("p (h d) -> p h d", d=HD)
                    link(quantise(q3, q3, sq[:, b], qri[:, b], nh))
                    link(nc.vector.tensor_scalar(qf[:, b], qf[:, b], ROUND, ROUND, ALU.add, ALU.subtract))
                    for c in range(3):
                        last = nc.vector.tensor_copy(qp[:, b, :, c, :], q3)
                last.then_inc(s.q_parts_ready, 1)
                link(nc.vector.memset(vmax[:], 0.0))

                def v_maxima(j):
                    dve.wait_ge(s.v_taken, j + 1)
                    link(nc.vector.tensor_reduce(vri[:], vf[:, 2 * j:2 * j + 2].rearrange("p t d -> p d t"), AX.X, ALU.max, apply_absolute_value=True))
                    link(nc.vector.tensor_tensor(vmax[:], vmax[:], vri[:], ALU.max))
                for j in range(NP):
                    dve.wait_ge(s.k_in_psum, j + 1)
                    if j >= 3:
                        dve.wait_ge(s.rest_ready, j - 2)
                    full = kf[:, j % 3].rearrange("p a h d -> p (a h) d")
                    quantise(full, k.bank(j % 2).rearrange("p (g d) -> p g d", d=HD), ks[:], kri[:], 2 * nh).then_inc(s.k_taken, 1)
                    dve.wait_ge(s.k_taken, j + 1)
                    link(nc.vector.tensor_scalar(full, full, ROUND, ROUND, ALU.add, ALU.subtract))
                    nc.vector.tensor_tensor(full, full, ks[:].unsqueeze(2).to_broadcast([P, 2 * nh, HD]), ALU.mult).then_inc(s.kf_ready, 1)
                    dve.wait_ge(s.kf_ready, j + 1)
                    v_maxima(j)
                dve.sem_inc(s.vmax_ready, 1)
                dve.wait_ge(s.vscale_ready, 1)
                link(nc.vector.tensor_scalar(vall[:], vall[:], 1.0 / 127.0, TINY, ALU.mult, ALU.max))
                link(nc.vector.reciprocal(vri[:], vall[:]))
                for g in range(4):
                    v3 = vf[:, 8 * g:8 * g + 8, :]
                    link(nc.vector.tensor_tensor(v3, v3, vri[:].unsqueeze(1).to_broadcast([P, 8, D]), ALU.mult))
                for g in range(4):
                    v3 = vf[:, 8 * g:8 * g + 8, :]
                    last = nc.vector.tensor_scalar(vq[:, 8 * g:8 * g + 8, :], v3, ROUND, ROUND, ALU.add, ALU.subtract)
                last.then_inc(s.v_ready, 1)

                def maxima(u, first, n):
                    b, h = divmod(u, nh)
                    for i in range(first, first + n):
                        m = 8 * u + i
                        dve.wait_ge(s.max_scores, m + 1)
                        nc.vector.reduce_max(mx[:, u % 2, i:i + 1], k.bank(MBANK[m % 3]), AX.X).then_inc(s.max_taken, 1)
                    if first + n == 8 and n:
                        dve.wait_ge(s.max_taken, 8 * u + 8)
                        link(nc.vector.reduce_max(nb[:, u % 2, 0:1], mx[:, u % 2, :], AX.X))
                        link(nc.vector.tensor_tensor(nb[:, u % 2, 0:1], nb[:, u % 2, 0:1], sq[:, b, h:h + 1], ALU.mult))
                        if u >= 2:
                            dve.wait_ge(s.exp_done, NQC * (u - 1))
                        nc.vector.tensor_scalar(nb[:, u % 2, 1:2], nb[:, u % 2, 0:1], -1.0, LN255, ALU.mult, ALU.add).then_inc(s.bias_ready, 1)

                def take_output(v):
                    dve.wait_ge(s.pT_used, NQC * (v + 1))
                    nc.vector.tensor_copy(ot[0:HD, v], k.bank(6, HD, P)).then_inc(s.oT_ready, 1)
                maxima(0, 0, 8)
                for q in range(NCH + 1):
                    v, c = divmod(q, NQC)
                    if q >= 1:
                        m = q - 1
                        dve.wait_ge(s.exp_done, m + 1)
                        if m >= 3:
                            dve.wait_ge(s.eT_in_psum, m - 2)
                        nc.vector.tensor_scalar(eb[:, m % 3], ex[:, m % 3], ROUND, ROUND, ALU.add, ALU.subtract).then_inc(s.rounded, 1)
                    if c == 3 and v >= 1:
                        take_output(v - 1)
                    if v + 1 < NU:
                        maxima(v + 1, sum(MAXES[:c]), MAXES[c])
                take_output(NU - 1)
                dve.wait_ge(k.out_w_loaded, 32)
                link(nc.vector.reduce_sum(rs[:].rearrange("p b h -> p (b h)"), sums[:], AX.X))
                link(nc.vector.reciprocal(rs[:], rs[:]))
                dve.wait_ge(s.o_in_psum, 1)
                for b in range(B):
                    link(nc.vector.tensor_tensor(attn[:, b].rearrange("p (h d) -> p h d", d=HD),
                                                 k.bank(0, P, D, b * D).rearrange("p (h d) -> p h d", d=HD),
                                                 rs[:, b].unsqueeze(2).to_broadcast([P, nh, HD]), ALU.mult))
                    nc.vector.tensor_tensor(attn[:, b], attn[:, b], vall[:], ALU.mult).then_inc(s.attn_ready, 1)
                for b in range(B):
                    link(nc.vector.tensor_tensor(k.x[:, b], k.x[:, b], bp[:], ALU.add))
                dve.wait_ge(s.out_in_psum, 1)
                for b in range(B):
                    nc.vector.tensor_tensor(k.x[:, b], k.x[:, b], k.bank(1, P, D, b * D), ALU.add)


def l0_attn(k):
    nc, A = k.nc, k.A
    with ExitStack() as ctx:
        def sb(name, shape, dt=F32):
            return k.sb("a0_" + name, shape, dt, ctx)
        w = [sb("w" + n, [P, DC, D]) for n in "ifgo"]
        gw = sb("gnorm", [P, DC])
        gate, v, sig_i = sb("gate", [P, DC, BT]), sb("v", [P, DC, BT]), sb("sig_i", [P, DC, BT])
        sig_g, o, o2 = sb("sig_g", [P, DC, BT]), sb("o", [P, DC, BT]), sb("o2", [P, DC, BT])
        rms = sb("rms", [P, 2, BT])
        flat = lambda t: t[:].rearrange("p c t -> p (c t)")

        def load(sp):
            for t, n in zip(w, "ifgo"):
                sp.dma_start(t[:], A["L0_attn_W" + n + "_T"].rearrange("(c p) n -> p c n", p=P)).then_inc(k.w_loaded[1], 16)
            sp.dma_start(gw[:], A["L0_attn_gnorm_w"].rearrange("(c p) -> p c", p=P), allow_slow_non_contiguous=True).then_inc(k.w_loaded[1], 16)
        layernorm(k, load)
        with signals(nc, k.pool, "dve_step proj_ready sig_ready scan_ready act_step ms_in_psum var_ready std_ready o_ready out_ready") as s, \
                nc.Block() as block:
            @block.tensor
            def _(pe):
                pe.wait_ge(k.w_loaded[1], 80)
                for j in (1, 0, 2):
                    for m in range(DC):
                        last = matmul_acc(nc, k.bank(j, P, BT, m * BT),
                                          [(w[j][:, c, m * P:(m + 1) * P], k.xt[:, c]) for c in range(DC)])
                    last.then_inc(s.proj_ready, 1)
                pe.wait_ge(s.act_step, 1)
                matmul_acc(nc, k.bank(3, P, BT), [(k.ones[:], o2[:, c]) for c in range(DC)]).then_inc(s.ms_in_psum, 1)
                pe.wait_ge(s.o_ready, 1)
                for b in range(B):
                    last = matmul_acc(nc, k.bank(4, P, D, b * D), [(o[:, c, b * T:(b + 1) * T], w[3][:, c]) for c in range(DC)])
                last.then_inc(s.out_ready, 1)

            @block.scalar
            def _(act):
                act.wait_ge(s.proj_ready, 1)
                nc.scalar.activation(flat(gate), k.bank(1), ACT.Sigmoid).then_inc(s.sig_ready, 1)
                nc.scalar.activation(flat(v), k.bank(1), ACT.Sigmoid, scale=-1.0).then_inc(s.sig_ready, 1)
                act.wait_ge(s.proj_ready, 2)
                nc.scalar.activation(flat(sig_i), k.bank(0), ACT.Sigmoid).then_inc(s.sig_ready, 1)
                act.wait_ge(s.proj_ready, 3)
                nc.scalar.activation(flat(sig_g), k.bank(2), ACT.Sigmoid).then_inc(s.sig_ready, 1)
                act.wait_ge(s.scan_ready, 4)
                nc.scalar.activation(flat(o2), flat(o), ACT.Square).then_inc(s.act_step, 1)
                act.wait_ge(s.var_ready, 1)
                nc.scalar.activation(rms[:, 1], rms[:, 0], ACT.Sqrt).then_inc(s.std_ready, 1)

            @block.vector
            def _(dve):
                link = chain(dve, s.dve_step)
                dve.wait_ge(s.sig_ready, 3)
                link(nc.vector.tensor_tensor(flat(sig_i), flat(sig_i), k.bank(0), ALU.mult))
                link(nc.vector.tensor_tensor(flat(v), flat(v), flat(sig_i), ALU.mult))
                for c in range(DC):
                    for b in range(B):
                        sl = slice(b * T, (b + 1) * T)
                        nc.vector.tensor_tensor_scan(o[:, c, sl], gate[:, c, sl], v[:, c, sl], 0.0, ALU.mult, ALU.add).then_inc(s.scan_ready, 1)
                dve.wait_ge(s.sig_ready, 4)
                link(nc.vector.tensor_tensor(flat(sig_g), flat(sig_g), k.bank(2), ALU.mult))
                for c in range(DC):
                    link(nc.vector.tensor_scalar(sig_g[:, c], sig_g[:, c], gw[:, c:c + 1], None, ALU.mult))
                dve.wait_ge(s.ms_in_psum, 1)
                nc.vector.tensor_scalar(rms[:, 0], k.bank(3, P, BT), 1.0 / D, LN_EPS, ALU.mult, ALU.add).then_inc(s.var_ready, 1)
                dve.wait_ge(s.std_ready, 1)
                link(nc.vector.reciprocal(rms[:, 0], rms[:, 1]))
                link(nc.vector.tensor_tensor(flat(o), flat(o), flat(sig_g), ALU.mult))
                nc.vector.tensor_tensor(o[:], o[:], rms[:, 0].unsqueeze(1).to_broadcast([P, DC, BT]), ALU.mult).then_inc(s.o_ready, 1)
                dve.wait_ge(s.out_ready, 1)
                xf = k.x[:].rearrange("p b d -> p (b d)")
                nc.vector.tensor_tensor(xf, xf, k.bank(4), ALU.add)


EXPERTS = 16
TOPK = 4
INNER = 176
IH = INNER // 2
CAP = 128
SHARED = 2
RING = 6


def l0_ffn(k):
    nc, A = k.nc, k.A
    ne = EXPERTS + SHARED
    with ExitStack() as ctx:
        def sb(name, shape, dt=F32):
            return k.sb("f0_" + name, shape, dt, ctx)
        wg = sb("router", [P, DC, EXPERTS])
        wgu = sb("w_gate_up", [P, RING, DC, 2, INNER])
        wd = sb("w_down", [IH, RING, 2, D])
        mid = sb("mid", [IH, 2, 2, BT])
        sig = sb("sig", [IH, 2, 2, BT])
        prob = sb("prob", [P, B, 24])
        marked = sb("marked", [P, B, 24])
        top = sb("top", [P, B, 8])
        sel = sb("selected", [P, B, EXPERTS])
        wt = sb("weights", [P, B, ne])
        sm = sb("small", [P, B, 4])
        acc = sb("acc", [P, B, D])

        def load(sp):
            sp.dma_start(wg[:], A["L0_ffn_gate_w_T"].rearrange("(c p) n -> p c n", p=P)).then_inc(k.w_loaded[2], 16)
        layernorm(k, load)
        with signals(nc, k.pool, "dve_step " + " ".join(f"w_loaded_{r}" for r in range(RING)) +
                     " gu_in_psum gu_taken mid_ready out_in_psum out_taken sig_ready logits_ready max_ready exp_ready sel_ready count_ready") as s, \
                nc.Block() as block:
            ring_loaded = [s.of[f"w_loaded_{r}"] for r in range(RING)]

            @block.sync
            def _(sp):
                for e in range(ne):
                    if e >= RING:
                        sp.wait_ge(s.out_in_psum, e - RING + 1)
                    sp.dma_start(wgu[:, e % RING], A["L0_ffn_gate_up"][e]).then_inc(ring_loaded[e % RING], 16)
                    sp.dma_start(wd[:, e % RING], A["L0_ffn_down"][e]).then_inc(ring_loaded[e % RING], 16)

            @block.tensor
            def _(pe):
                pe.wait_ge(k.w_loaded[2], 16)
                for b in range(B):
                    last = matmul_acc(nc, k.bank(7, P, EXPERTS, b * EXPERTS),
                                      [(k.xt[:, c, b * T:(b + 1) * T], wg[:, c]) for c in range(DC)])
                last.then_inc(s.logits_ready, 1)

                def down(e):
                    pe.wait_ge(s.mid_ready, e + 1)
                    if e >= 2:
                        pe.wait_ge(s.out_taken, B * (e - 1))
                    for b in range(B):
                        last = matmul_acc(nc, k.bank(4 + e % 2, P, D, b * D),
                                          [(mid[:, e % 2, m, b * T:(b + 1) * T], wd[:, e % RING, m]) for m in range(2)])
                    last.then_inc(s.out_in_psum, 1)
                for e in range(ne):
                    pe.wait_ge(ring_loaded[e % RING], 32 * (e // RING + 1))
                    if e >= 2:
                        pe.wait_ge(s.mid_ready, e - 1)
                    for j in range(2):
                        for m in range(2):
                            last = matmul_acc(nc, k.bank(2 * (e % 2) + j, IH, BT, m * BT),
                                              [(wgu[:, e % RING, c, j, m * IH:(m + 1) * IH], k.xt[:, c]) for c in range(DC)])
                    last.then_inc(s.gu_in_psum, 1)
                    if e == 1:
                        pe.wait_ge(s.sel_ready, 1)
                        nc.tensor.matmul(k.bank(6, P, EXPERTS), k.keep[:], sel[:, 0], start=True, stop=True)
                        matmul_acc(nc, k.bank(6, P, EXPERTS, EXPERTS), [(k.ones[:], sel[:, 0]), (k.keep[:], sel[:, 1])]).then_inc(s.count_ready, 1)
                    if e >= 1:
                        down(e - 1)
                down(ne - 1)

            @block.scalar
            def _(act):
                act.wait_ge(s.max_ready, B)
                for b in range(B):
                    nc.scalar.activation(prob[:, b, 0:EXPERTS], k.bank(7, P, EXPERTS, b * EXPERTS), ACT.Exp, bias=sm[:, b, 0:1],
                                         accum_out=sm[:, b, 1:2]).then_inc(s.exp_ready, 1)
                for e in range(ne):
                    act.wait_ge(s.gu_in_psum, e + 1)
                    if e >= 2:
                        act.wait_ge(s.mid_ready, e - 1)
                    nc.scalar.activation(sig[:, e % 2].rearrange("p a n -> p (a n)"), k.bank(2 * (e % 2), IH), ACT.Sigmoid).then_inc(s.sig_ready, 1)

            @block.vector
            def _(dve):
                link = chain(dve, s.dve_step)
                for b in range(B):
                    nc.vector.memset(wt[:, b, EXPERTS:ne], 1.0)
                    for j in range(4):
                        nc.vector.memset(prob[:, b, EXPERTS + j:EXPERTS + j + 1], -1.0 - j)
                    link(nc.vector.memset(prob[:, b, EXPERTS + 4:24], -9.0))
                dve.wait_ge(s.logits_ready, 1)
                for b in range(B):
                    link(nc.vector.reduce_max(sm[:, b, 2:3], k.bank(7, P, EXPERTS, b * EXPERTS), AX.X))
                    nc.vector.tensor_scalar(sm[:, b, 0:1], sm[:, b, 2:3], -1.0, None, ALU.mult).then_inc(s.max_ready, 1)
                dve.wait_ge(s.exp_ready, B)
                for b in range(B):
                    link(nc.vector.reciprocal(sm[:, b, 2:3], sm[:, b, 1:2]))
                    link(nc.vector.tensor_scalar(prob[:, b, 0:EXPERTS], prob[:, b, 0:EXPERTS], sm[:, b, 2:3], None, ALU.mult))
                    link(nc.vector.max(top[:, b], prob[:, b]))
                    for j in range(4):
                        nc.vector.memset(top[:, b, 4 + j:5 + j], -1.0 - j)
                    link(nc.vector.memset(sm[:, b, 3:4], 0.0))
                    link(nc.vector.match_replace(marked[:, b], top[:, b], prob[:, b], -5.0))
                    ins = nc.vector.tensor_scalar(sel[:, b], marked[:, b, 0:EXPERTS], -5.0, None, ALU.is_equal)
                    link(ins)
                dve.sem_inc(s.sel_ready, 1)
                for b in range(B):
                    link(nc.vector.tensor_tensor(wt[:, b, 0:EXPERTS], prob[:, b, 0:EXPERTS], sel[:, b], ALU.mult))
                    link(nc.vector.reduce_sum(sm[:, b, 2:3], wt[:, b, 0:EXPERTS], AX.X))
                    link(nc.vector.tensor_scalar(sm[:, b, 2:3], sm[:, b, 2:3], 1e-20, None, ALU.add))
                    link(nc.vector.reciprocal(sm[:, b, 3:4], sm[:, b, 2:3]))
                    link(nc.vector.tensor_scalar(wt[:, b, 0:EXPERTS], wt[:, b, 0:EXPERTS], sm[:, b, 3:4], None, ALU.mult))
                def capacity():
                    dve.wait_ge(s.count_ready, 1)
                    for b in range(B):
                        link(nc.vector.tensor_scalar(sel[:, b], k.bank(6, P, EXPERTS, b * EXPERTS), float(CAP), None, ALU.is_le))
                        link(nc.vector.tensor_tensor(wt[:, b, 0:EXPERTS], wt[:, b, 0:EXPERTS], sel[:, b], ALU.mult))

                def take(e):
                    dve.wait_ge(s.out_in_psum, e + 1)
                    for b in range(B):
                        if e >= 1:
                            dve.wait_ge(s.out_taken, B * (e - 1) + b + 1)
                        base = k.x if e == 0 else acc
                        out = k.x if e == ne - 1 else acc
                        nc.vector.scalar_tensor_tensor(out=out[:, b], in0=k.bank(4 + e % 2, P, D, b * D), scalar=wt[:, b, e:e + 1],
                                                       in1=base[:, b], op0=ALU.mult, op1=ALU.add).then_inc(s.out_taken, 1)
                for e in range(ne):
                    dve.wait_ge(s.sig_ready, e + 1)
                    sg = sig[:, e % 2].rearrange("p a n -> p (a n)")
                    link(nc.vector.tensor_tensor(sg, sg, k.bank(2 * (e % 2), IH), ALU.mult))
                    if e >= 2:
                        dve.wait_ge(s.out_in_psum, e - 1)
                    nc.vector.tensor_tensor(mid[:, e % 2].rearrange("p a n -> p (a n)"), sg, k.bank(2 * (e % 2) + 1, IH), ALU.mult).then_inc(s.mid_ready, 1)
                    if e == 1:
                        capacity()
                    if e >= 1:
                        take(e - 1)
                take(ne - 1)


def l1_xattn(k):
    nc, A = k.nc, k.A
    nt = S2 // P
    with ExitStack() as ctx:
        def sb(name, shape, dt=F32):
            return k.sb("x1_" + name, shape, dt, ctx)
        val = sb("ctx_tokens", [P, B, nt, D])
        mask8 = sb("mask8", [P, B, S2], mybir.dt.uint8)
        bias = sb("mask_bias", [P, B, S2])
        sc = sb("scores", [P, B, S2])
        pt = sb("probsT", [P, B, nt, P])
        sm = sb("small", [P, B, 8])

        def load(sp):
            sp.dma_start(mask8[:], A["mask_BxS2_bk0"].rearrange("(a b) s -> a b s", a=1).to_broadcast([P, B, S2])).then_inc(k.mask_loaded, 16)
            for b in range(B):
                sp.dma_start(val[:, b], A["ctx_2048"][b].rearrange("(n p) d -> p n d", p=P)).then_inc(k.w_loaded[3], 16)
        layernorm(k, load)
        with signals(nc, k.pool, "dve_step scores_ready masked_ready exp_ready tr_ready tr_taken out_ready max_ready") as s, \
                nc.Block() as block:
            @block.tensor
            def _(pe):
                for loaded in k.ctx_loaded:
                    pe.wait_ge(loaded, 16)
                for b in range(B):
                    for j in range(4):
                        a = b * S2 + j * 512
                        matmul_acc(nc, k.bank(4 * b + j), [(k.xt[:, c, b * T:(b + 1) * T], k.ctxt[:, c, a:a + 512]) for c in range(DC)]
                                   ).then_inc(s.scores_ready, 1)
                for b in range(B):
                    pe.wait_ge(s.exp_ready, b + 1)
                    for g in range(4):
                        n = 4 * b + g
                        if n >= 2:
                            pe.wait_ge(s.tr_taken, n - 1)
                        for j in range(4):
                            i = 4 * g + j
                            last = nc.tensor.transpose(k.bank(n % 2, P, P, j * P), sc[:, b, i * P:(i + 1) * P], k.ident[:])
                        last.then_inc(s.tr_ready, 1)
                    pe.wait_ge(k.w_loaded[3], 32)
                    for i in range(nt):
                        if i % 4 == 0:
                            pe.wait_ge(s.tr_taken, 4 * b + i // 4 + 1)
                        last = nc.tensor.matmul(k.bank(2 + b, P, D), pt[:, b, i], val[:, b, i], start=(i == 0), stop=(i == nt - 1))
                    last.then_inc(s.out_ready, 1)

            @block.scalar
            def _(act):
                for b in range(B):
                    act.wait_ge(s.max_ready, b + 1)
                    nc.scalar.activation(sc[:, b], sc[:, b], ACT.Exp, bias=sm[:, b, 0:1], accum_out=sm[:, b, 1:2]).then_inc(s.exp_ready, 1)

            @block.vector
            def _(dve):
                link = chain(dve, s.dve_step)
                dve.wait_ge(k.mask_loaded, 16)
                for b in range(B):
                    link(nc.vector.tensor_scalar(bias[:, b], mask8[:, b], -NEG, NEG, ALU.mult, ALU.add))
                for b in range(B):
                    for j in range(4):
                        dve.wait_ge(s.scores_ready, 4 * b + j + 1)
                        sl = slice(j * 512, (j + 1) * 512)
                        nc.vector.scalar_tensor_tensor(out=sc[:, b, sl], in0=k.bank(4 * b + j), scalar=1.0 / float(np.sqrt(D)),
                                                       in1=mask8[:, b, sl], op0=ALU.mult, op1=ALU.mult).then_inc(s.masked_ready, 1)
                    dve.wait_ge(s.masked_ready, 4 * (b + 1))
                    link(nc.vector.tensor_tensor(sc[:, b], sc[:, b], bias[:, b], ALU.add))
                    link(nc.vector.reduce_max(sm[:, b, 2:3], sc[:, b], AX.X))
                    nc.vector.tensor_scalar(sm[:, b, 0:1], sm[:, b, 2:3], -1.0, None, ALU.mult).then_inc(s.max_ready, 1)
                    link(nc.vector.reduce_max(sm[:, b, 3:4], mask8[:, b], AX.X))
                for b in range(B):
                    dve.wait_ge(s.exp_ready, b + 1)
                    link(nc.vector.reciprocal(sm[:, b, 4:5], sm[:, b, 1:2]))
                    link(nc.vector.tensor_tensor(sm[:, b, 5:6], sm[:, b, 4:5], sm[:, b, 3:4], ALU.mult))
                    for g in range(4):
                        n = 4 * b + g
                        dve.wait_ge(s.tr_ready, n + 1)
                        nc.vector.tensor_copy(pt[:, b, 4 * g:4 * g + 4].rearrange("p a n -> p (a n)"), k.bank(n % 2)).then_inc(s.tr_taken, 1)
                for b in range(B):
                    dve.wait_ge(s.out_ready, b + 1)
                    nc.vector.scalar_tensor_tensor(out=k.x[:, b], in0=k.bank(2 + b, P, D), scalar=sm[:, b, 5:6], in1=k.x[:, b],
                                                   op0=ALU.mult, op1=ALU.add)


def l1_attn(k):
    nc, A = k.nc, k.A
    with ExitStack() as ctx:
        def sb(name, shape, dt=F32):
            return k.sb("a1_" + name, shape, dt, ctx)
        wqkv, wo = sb("w_qkv", [P, DC, 3 * D]), sb("w_out", [P, DC, D])
        dec = sb("decay", [P, DC, 2])
        low, ex = sb("low", [P, 2, DC * BT]), sb("ex", [P, 2, DC * BT])
        q, kk, kv = sb("q", [P, DC, BT]), sb("k", [P, DC, BT]), sb("kv", [P, DC, BT])
        rkv, rk = sb("run_kv", [P, DC, BT]), sb("run_k", [P, DC, BT])
        flat = lambda t: t[:].rearrange("p c t -> p (c t)")

        def load(sp):
            sp.dma_start(dec[:, :, 0:1], A["L1_decay_ch"].rearrange("(c p a) -> p c a", p=P, a=1), allow_slow_non_contiguous=True).then_inc(k.w_loaded[4], 16)
            sp.dma_start(wqkv[:], A["L1_attn_w_qkv"].rearrange("(c p) n -> p c n", p=P)).then_inc(k.w_loaded[4], 16)
            sp.dma_start(wo[:], A["L1_attn_w_out"].rearrange("(c p) n -> p c n", p=P)).then_inc(k.w_loaded[4], 16)
        layernorm(k, load)
        with signals(nc, k.pool, "dve_step proj_ready low_ready exp_ready dec_ready scanned den_in_psum den_ready o_ready out_ready fm_ready") as s, \
                nc.Block() as block:
            @block.tensor
            def _(pe):
                pe.wait_ge(k.w_loaded[4], 48)
                for j in (1, 0, 2):
                    for m in range(DC):
                        a = j * D + m * P
                        last = matmul_acc(nc, k.bank(j, P, BT, m * BT), [(wqkv[:, c, a:a + P], k.xt[:, c]) for c in range(DC)])
                    last.then_inc(s.proj_ready, 1)
                pe.wait_ge(s.den_ready, 1)
                for m in range(DC):
                    last = nc.tensor.matmul(k.bank(3, P, BT, m * BT), k.blocks[:], rk[:, m], start=True, stop=True)
                last.then_inc(s.den_in_psum, 1)
                pe.wait_ge(s.o_ready, 1)
                for b in range(B):
                    last = matmul_acc(nc, k.bank(4, P, D, b * D), [(rkv[:, c, b * T:(b + 1) * T], wo[:, c]) for c in range(DC)])
                last.then_inc(s.out_ready, 1)

            @block.scalar
            def _(act):
                act.wait_ge(k.w_loaded[4], 48)
                nc.scalar.activation(dec[:, :, 1], dec[:, :, 0], ACT.Sigmoid).then_inc(s.dec_ready, 1)
                for j in range(2):
                    act.wait_ge(s.low_ready, j + 1)
                    nc.scalar.activation(ex[:, j], low[:, j], ACT.Exp).then_inc(s.exp_ready, 1)

            @block.vector
            def _(dve):
                link = chain(dve, s.dve_step)
                for j, bank in ((0, 1), (1, 0)):
                    dve.wait_ge(s.proj_ready, j + 1)
                    nc.vector.tensor_scalar(low[:, j], k.bank(bank), 0.0, None, ALU.min).then_inc(s.low_ready, 1)
                for j, bank, dst in ((0, 1, kk), (1, 0, q)):
                    dve.wait_ge(s.exp_ready, j + 1)
                    link(nc.vector.scalar_tensor_tensor(out=flat(dst), in0=k.bank(bank), scalar=0.0, in1=ex[:, j],
                                                        op0=ALU.max, op1=ALU.add))
                dve.wait_ge(s.proj_ready, 3)
                link(nc.vector.tensor_tensor(flat(kv), flat(kk), k.bank(2), ALU.mult))
                dve.wait_ge(s.dec_ready, 1)
                for src, dst in ((kk, rk), (kv, rkv)):
                    for c in range(DC):
                        for b in range(B):
                            sl = slice(b * T, (b + 1) * T)
                            nc.vector.tensor_tensor_scan(dst[:, c, sl], dec[:, c, 1:2].to_broadcast([P, T]), src[:, c, sl], 0.0,
                                                         ALU.mult, ALU.add).then_inc(s.scanned, 1)
                dve.wait_ge(s.scanned, 8)
                nc.vector.tensor_tensor(flat(rk), flat(rk), flat(q), ALU.mult).then_inc(s.den_ready, 1)
                link(nc.vector.tensor_tensor(flat(rkv), flat(rkv), flat(q), ALU.mult))
                dve.wait_ge(s.den_in_psum, 1)
                link(nc.vector.tensor_scalar(flat(kk), k.bank(3), 1e-6, None, ALU.max))
                link(nc.vector.reciprocal(flat(kv), flat(kk)))
                nc.vector.tensor_tensor(flat(rkv), flat(rkv), flat(kv), ALU.mult).then_inc(s.o_ready, 1)
                dve.wait_ge(s.out_ready, 1)
                xf = k.x[:].rearrange("p b d -> p (b d)")
                nc.vector.tensor_tensor(xf, xf, k.bank(4), ALU.add)


L2_EPS = 1e-12
SLOTS = 128
HID = 64


def l1_ffn(k):
    nc, A = k.nc, k.A
    ne = EXPERTS
    ns = ne * SLOTS
    CR = 6
    with ExitStack() as ctx:
        def sb(name, shape, dt=F32):
            return k.sb("f1_" + name, shape, dt, ctx)
        mu = sb("mu", [P, DC, ns])
        w1, w2 = sb("w1", [P, DC, ne, HID]), sb("w2", [HID, ne, D])
        b1 = sb("b1", [HID, ne])
        b2 = sb("b2", [P, 2, D])
        gam, bet, sca = sb("gamma", [P, D]), sb("beta", [P, D]), sb("scale", [P, 1])
        xl = sb("x_ln", [P, B, D])
        xs = sb("x_l2", [P, B, D])
        xst = sb("x_l2_T", [P, DC, BT])
        sq, rn = sb("sq", [P, 2, 512]), sb("rn", [P, 2, 512])
        comb = sb("combine", [P, B, ns])
        disp = sb("disp", [P, 2, BT])
        dtk = sb("disp_tok", [P, 2, BT])
        ct = sb("combT", [P, CR, BT])
        slot = sb("slotT", [P, 2, DC, BT])
        ht, so = sb("hT", [HID, 2, BT]), sb("slot_out", [P, 2, B, D])
        sm = sb("small", [P, B, 12])
        dm = sb("disp_small", [P, 2, B, 4])

        def load(sp):
            sp.dma_start(mu[:], A["L1_ffn_mu"].rearrange("(c p) e s -> p c (e s)", p=P)).then_inc(k.mu_loaded, 16)
            for t, n in ((gam, "gamma"), (bet, "beta")):
                sp.dma_start(t[:], A["L1_ffn_" + n].rearrange("(a n) -> a n", a=1).to_broadcast([P, D])).then_inc(k.w_loaded[5], 16)
            sp.dma_start(sca[:], A["L1_ffn_scale"].rearrange("(a n) -> a n", a=1).to_broadcast([P, 1])).then_inc(k.w_loaded[5], 16)
            sp.dma_start(b1[:], A["L1_ffn_b1_T"]).then_inc(k.w_loaded[5], 16)
            for c in range(DC):
                sp.dma_start(w1[:, c], A["L1_ffn_W1"][:, c * P:(c + 1) * P].rearrange("e p h -> p e h")).then_inc(k.w_loaded[5], 16)
            sp.dma_start(w2[:], A["L1_ffn_W2"].rearrange("e h d -> h e d")).then_inc(k.w_loaded[5], 16)
        layernorm(k, load)
        names = ("dve_step sq_ready ss_in_psum ss_taken std_ready mu_ready n_ready nstd_ready xs_ready xT_in_psum xT_ready "
                 "logits_ready logits_taken cmax_ready cexp_ready dlog_ready dmax_ready dexp_ready disp_ready "
                 "t_in_psum t_taken slot_in_psum slot_taken h_in_psum h_taken so_in_psum so_taken b2_loaded0 b2_loaded1 out_added var_ready l2_ready")
        with signals(nc, k.pool, names) as s, nc.Block() as block:
            @block.sync
            def _(sp):
                for e in range(ne):
                    if e >= 2:
                        sp.wait_ge(s.so_taken, B * (e - 1))
                    sp.dma_start(b2[:, e % 2], A["L1_ffn_b2"][e:e + 1].to_broadcast([P, D])).then_inc((s.b2_loaded0, s.b2_loaded1)[e % 2], 16)

            @block.tensor
            def _(pe):
                for j in range(4):
                    pe.wait_ge(s.sq_ready, DC * (j + 1))
                    matmul_acc(nc, k.bank(j), [(k.ones[:], comb[:, c, j * 512:(j + 1) * 512]) for c in range(DC)]).then_inc(s.ss_in_psum, 1)
                pe.wait_ge(s.xs_ready, 1)
                for b in range(B):
                    for c in range(DC):
                        last = nc.tensor.transpose(k.bank(4, P, T, c * BT + b * T), xs[:, b, c * P:(c + 1) * P], k.ident[:])
                last.then_inc(s.xT_in_psum, 1)
                pe.wait_ge(s.xT_ready, 1)
                pe.wait_ge(s.mu_ready, 4)
                for b in range(B):
                    if b:
                        pe.wait_ge(s.cexp_ready, 1)
                    for j in range(4):
                        last = matmul_acc(nc, k.bank(j), [(xst[:, c, b * T:(b + 1) * T], mu[:, c, j * 512:(j + 1) * 512]) for c in range(DC)])
                    last.then_inc(s.logits_ready, 1)
                pe.wait_ge(s.cexp_ready, B)

                pe.wait_ge(k.w_loaded[5], 112)

                def dispatch_logits(e):
                    if e >= 1:
                        pe.wait_ge(s.dexp_ready, B * e)
                    matmul_acc(nc, k.bank(0, P, BT), [(mu[:, c, e * SLOTS:(e + 1) * SLOTS], xst[:, c]) for c in range(DC)]).then_inc(s.dlog_ready, 1)

                def turn(e):
                    if e >= 1:
                        pe.wait_ge(s.t_taken, e)
                    for b in range(B):
                        nc.tensor.transpose(k.bank(1, P, P, BT + b * T), comb[:, b, e * SLOTS:(e + 1) * SLOTS], k.ident[:])
                    pe.wait_ge(s.disp_ready, e + 1)
                    for b in range(B):
                        last = nc.tensor.transpose(k.bank(1, P, P, b * T), disp[:, e % 2, b * T:(b + 1) * T], k.ident[:])
                    last.then_inc(s.t_in_psum, 1)

                def gather(e):
                    pe.wait_ge(s.t_taken, e + 1)
                    if e >= 1:
                        pe.wait_ge(s.slot_taken, e)
                    for c in range(DC):
                        for b in range(B):
                            last = nc.tensor.matmul(k.bank(2, P, T, c * BT + b * T), xl[:, b, c * P:(c + 1) * P],
                                                    dtk[:, e % 2, b * T:(b + 1) * T], start=True, stop=True)
                    last.then_inc(s.slot_in_psum, 1)

                def hidden(e):
                    pe.wait_ge(s.slot_taken, e + 1)
                    if e >= 1:
                        pe.wait_ge(s.h_taken, e)
                    matmul_acc(nc, k.bank(3, HID, BT), [(w1[:, c, e], slot[:, e % 2, c]) for c in range(DC)]).then_inc(s.h_in_psum, 1)

                def slot_out(e):
                    pe.wait_ge(s.h_taken, e + 1)
                    if e >= 1:
                        pe.wait_ge(s.so_taken, B * e)
                    for b in range(B):
                        last = nc.tensor.matmul(k.bank(4, P, D, b * D), ht[:, e % 2, b * T:(b + 1) * T], w2[:, e], start=True, stop=True)
                    last.then_inc(s.so_in_psum, 1)

                def combine(e):
                    pe.wait_ge(s.so_taken, B * (e + 1))
                    for b in range(B):
                        last = nc.tensor.matmul(k.bank(5 + b, P, D), ct[:, e % CR, b * T:(b + 1) * T], so[:, e % 2, b],
                                                start=(e == 0), stop=(e == ne - 1))
                    last.then_inc(s.out_added, 1)
                steps = (dispatch_logits, turn, gather, hidden, slot_out, combine)
                for i in range(ne + len(steps) - 1):
                    for lag, step in enumerate(steps):
                        if 0 <= i - lag < ne:
                            step(i - lag)

            @block.scalar
            def _(act):
                act.wait_ge(k.mu_loaded, 16)
                for j in range(4):
                    for c in range(DC):
                        nc.scalar.activation(comb[:, c, j * 512:(j + 1) * 512], mu[:, c, j * 512:(j + 1) * 512], ACT.Square).then_inc(s.sq_ready, 1)
                for j in range(4):
                    act.wait_ge(s.ss_in_psum, j + 1)
                    if j >= 2:
                        act.wait_ge(s.ss_taken, j - 1)
                    nc.scalar.activation(sq[:, j % 2], k.bank(j), ACT.Sqrt).then_inc(s.std_ready, 1)
                act.wait_ge(s.var_ready, B)
                nc.scalar.activation(sm[:, :, 1], sm[:, :, 0], ACT.Sqrt).then_inc(s.nstd_ready, 1)
                act.wait_ge(s.n_ready, B)
                nc.scalar.activation(sm[:, :, 7], sm[:, :, 6], ACT.Sqrt).then_inc(s.l2_ready, 1)
                act.wait_ge(s.xT_in_psum, 1)
                nc.scalar.copy(xst[:].rearrange("p c t -> p (c t)"), k.bank(4)).then_inc(s.xT_ready, 1)
                for b in range(B):
                    act.wait_ge(s.cmax_ready, b + 1)
                    nc.scalar.activation(comb[:, b], k.ps[:, 0:4].rearrange("p a n -> p (a n)"), ACT.Exp, bias=sm[:, b, 4:5],
                                         accum_out=sm[:, b, 5:6]).then_inc(s.cexp_ready, 1)
                act.wait_ge(k.w_loaded[5], 112)
                for i in range(ne + 3):
                    if i < ne:
                        act.wait_ge(s.dmax_ready, B * (i + 1))
                        if i >= 2:
                            act.wait_ge(s.t_in_psum, i - 1)
                        for b in range(B):
                            nc.scalar.activation(disp[:, i % 2, b * T:(b + 1) * T], k.bank(0, P, T, b * T), ACT.Exp,
                                                 bias=dm[:, i % 2, b, 1:2], accum_out=dm[:, i % 2, b, 2:3]).then_inc(s.dexp_ready, 1)
                    e = i - 3
                    if e < 0:
                        continue
                    act.wait_ge(s.h_in_psum, e + 1)
                    if e >= 2:
                        act.wait_ge(s.so_in_psum, e - 1)
                    nc.scalar.activation(ht[:, e % 2], k.bank(3, HID, BT), ACT.Gelu, bias=b1[:, e:e + 1]).then_inc(s.h_taken, 1)

            @block.vector
            def _(dve):
                link = chain(dve, s.dve_step)
                for b in range(B):
                    link(nc.vector.bn_stats(k.stat[:, b, :], k.xn[:, b]))
                    link(nc.vector.bn_aggr(k.mv[:, b, :], k.stat[:, b, :]))
                    nc.vector.tensor_scalar(sm[:, b, 0:1], k.mv[:, b, 1:2], LN_EPS, None, ALU.add).then_inc(s.var_ready, 1)
                for j in range(4):
                    dve.wait_ge(s.std_ready, j + 1)
                    link(nc.vector.tensor_scalar(rn[:, 0], sq[:, j % 2], L2_EPS, None, ALU.max))
                    nc.vector.reciprocal(rn[:, 1], rn[:, 0]).then_inc(s.ss_taken, 1)
                    dve.wait_ge(s.ss_taken, j + 1)
                    for c in range(DC):
                        sl = mu[:, c, j * 512:(j + 1) * 512]
                        link(nc.vector.tensor_tensor(sl, sl, rn[:, 1], ALU.mult))
                    dve.sem_inc(s.mu_ready, 1)
                dve.wait_ge(s.nstd_ready, 1)
                dve.wait_ge(k.w_loaded[5], 112)
                for b in range(B):
                    link(nc.vector.reciprocal(sm[:, b, 2:3], sm[:, b, 1:2]))
                    link(nc.vector.tensor_scalar(xl[:, b], k.xn[:, b], k.mv[:, b, 0:1], sm[:, b, 2:3], ALU.subtract, ALU.mult))
                    link(nc.vector.tensor_tensor(xl[:, b], xl[:, b], gam[:], ALU.mult))
                    link(nc.vector.tensor_tensor(xl[:, b], xl[:, b], bet[:], ALU.add))
                    link(nc.vector.tensor_tensor(xs[:, b], xl[:, b], xl[:, b], ALU.mult))
                    nc.vector.reduce_sum(sm[:, b, 6:7], xs[:, b], AX.X).then_inc(s.n_ready, 1)
                dve.wait_ge(s.l2_ready, 1)
                for b in range(B):
                    link(nc.vector.tensor_scalar(sm[:, b, 8:9], sm[:, b, 7:8], L2_EPS, None, ALU.max))
                    link(nc.vector.reciprocal(sm[:, b, 9:10], sm[:, b, 8:9]))
                    link(nc.vector.tensor_scalar(xs[:, b], xl[:, b], sm[:, b, 9:10], sca[:, 0:1], ALU.mult, ALU.mult))
                dve.sem_inc(s.xs_ready, 1)
                for b in range(B):
                    dve.wait_ge(s.logits_ready, b + 1)
                    link(nc.vector.reduce_max(sm[:, b, 10:11], k.ps[:, 0:4].rearrange("p a n -> p (a n)"), AX.X))
                    nc.vector.tensor_scalar(sm[:, b, 4:5], sm[:, b, 10:11], -1.0, None, ALU.mult).then_inc(s.cmax_ready, 1)

                def dispatch_max(e):
                    dve.wait_ge(s.dlog_ready, e + 1)
                    r = e % 2
                    link(nc.vector.tensor_reduce(dm[:, r, :, 0], k.bank(0, P, BT).rearrange("p (b t) -> p b t", b=B), AX.X, ALU.max))
                    for b in range(B):
                        nc.vector.tensor_scalar(dm[:, r, b, 1:2], dm[:, r, b, 0:1], -1.0, None, ALU.mult).then_inc(s.dmax_ready, 1)

                def dispatch_norm(e):
                    r = e % 2
                    dve.wait_ge(s.dexp_ready, B * (e + 1))
                    link(nc.vector.reciprocal(dm[:, r, :, 3], dm[:, r, :, 2]))
                    d3 = disp[:, r].rearrange("p (b t) -> p b t", b=B)
                    nc.vector.tensor_tensor(d3, d3, dm[:, r, :, 3].unsqueeze(2).to_broadcast([P, B, T]), ALU.mult).then_inc(s.disp_ready, 1)

                def take_turned(e):
                    dve.wait_ge(s.t_in_psum, e + 1)
                    if e >= 2:
                        dve.wait_ge(s.slot_in_psum, e - 1)
                    link(nc.vector.tensor_copy(dtk[:, e % 2], k.bank(1, P, BT)))
                    if e >= CR:
                        dve.wait_ge(s.out_added, e - CR + 1)
                    nc.vector.tensor_copy(ct[:, e % CR], k.bank(1, P, BT, BT)).then_inc(s.t_taken, 1)

                def take_slots(e):
                    dve.wait_ge(s.slot_in_psum, e + 1)
                    if e >= 2:
                        dve.wait_ge(s.h_in_psum, e - 1)
                    nc.vector.tensor_copy(slot[:, e % 2].rearrange("p c t -> p (c t)"), k.bank(2)).then_inc(s.slot_taken, 1)

                def add_bias(e):
                    dve.wait_ge(s.so_in_psum, e + 1)
                    dve.wait_ge((s.b2_loaded0, s.b2_loaded1)[e % 2], 16 * (e // 2 + 1))
                    if e >= 2:
                        dve.wait_ge(s.out_added, e - 1)
                    for b in range(B):
                        nc.vector.tensor_tensor(so[:, e % 2, b], k.bank(4, P, D, b * D), b2[:, e % 2], ALU.add).then_inc(s.so_taken, 1)
                for i in range(ne + 4):
                    if i < ne:
                        dispatch_max(i)
                    if 0 <= i - 1 < ne:
                        take_turned(i - 1)
                    if 0 <= i - 2 < ne:
                        take_slots(i - 2)
                    if 0 <= i - 4:
                        add_bias(i - 4)
                    if i < ne:
                        dispatch_norm(i)
                for b in range(B):
                    link(nc.vector.reciprocal(sm[:, b, 11:12], sm[:, b, 5:6]))
                dve.wait_ge(s.out_added, ne)
                for b in range(B):
                    nc.vector.scalar_tensor_tensor(out=k.x[:, b], in0=k.bank(5 + b, P, D), scalar=sm[:, b, 11:12], in1=k.x[:, b],
                                                   op0=ALU.mult, op1=ALU.add)


def l2_xattn(k):
    nc, A = k.nc, k.A
    nt = S2 // P
    with ExitStack() as ctx:
        def sb(name, shape, dt=F32):
            return k.sb("x2_" + name, shape, dt, ctx)
        wq, wg, wo = sb("wq", [P, DC, D]), sb("wg", [P, DC, D]), sb("wo", [P, DC, D])
        wkv = sb("wkv", [P, DC, 2 * D])
        bg = sb("bg", [P, DC])
        q, gate, z = sb("q", [P, DC, BT]), sb("gate", [P, DC, BT]), sb("z", [P, DC, BT])
        low, ex = sb("low", [P, 3, 512]), sb("ex", [P, 3, 512])
        kf = sb("k_feat", [P, 4, D])
        va = sb("v_ones", [P, 4, DC, P + 1])
        kvb, kb = sb("kv_heads", [P, DC, B, P]), sb("ksum_heads", [P, DC, B, P])
        flat = lambda t: t[:].rearrange("p c t -> p (c t)")

        def load(sp):
            for t, n in ((wkv, "Wkv"), (wq, "Wq"), (wg, "Wg"), (wo, "Wo")):
                sp.dma_start(t[:], A["L2_xattn_" + n + "_T"].rearrange("(c p) n -> p c n", p=P)).then_inc(k.w_loaded[6], 16)
            sp.dma_start(bg[:], A["L2_xattn_bg"].rearrange("(c p) -> p c", p=P), allow_slow_non_contiguous=True).then_inc(k.w_loaded[6], 16)
        layernorm(k, load)
        names = ("dve_step q_in_psum gate_in_psum kv_in_psum low_ready exp_ready kf_ready v_taken ones_ready sum_taken "
                 "attn_in_psum o_ready out_ready gate_ready tile_used")
        with signals(nc, k.pool, names) as s, nc.Block() as block:
            @block.tensor
            def _(pe):
                pe.wait_ge(k.w_loaded[6], 80)
                for loaded in k.ctx_loaded:
                    pe.wait_ge(loaded, 16)
                for w, bank, sem in ((wq, 0, s.q_in_psum), (wg, 1, s.gate_in_psum)):
                    for m in range(DC):
                        last = matmul_acc(nc, k.bank(bank, P, BT, m * BT), [(w[:, c, m * P:(m + 1) * P], k.xt[:, c]) for c in range(DC)])
                    last.then_inc(sem, 1)
                pe.wait_ge(s.ones_ready, 1)

                def summary(i):
                    pe.wait_ge(s.kf_ready, i + 1)
                    pe.wait_ge(s.v_taken, i + 1)
                    if i == nt:
                        pe.wait_ge(s.sum_taken, 1)
                    for m in range(DC):
                        last = nc.tensor.matmul(k.bank(6 + m, P, P + 1), kf[:, i % 4, m * P:(m + 1) * P], va[:, i % 4, m],
                                                start=(i % nt == 0), stop=(i % nt == nt - 1))
                    last.then_inc(s.tile_used, 1)
                for i in range(NKT):
                    if i >= 4:
                        pe.wait_ge(s.kf_ready, i - 3)
                        pe.wait_ge(s.v_taken, i - 3)
                    matmul_acc(nc, k.bank(2 + i % 4), [(k.ctxt[:, c, i * P:(i + 1) * P], wkv[:, c]) for c in range(DC)]).then_inc(s.kv_in_psum, 1)
                    if i >= 2:
                        summary(i - 2)
                summary(NKT - 2)
                summary(NKT - 1)
                pe.wait_ge(s.sum_taken, 2)
                pe.wait_ge(s.gate_ready, 2)
                for b in range(B):
                    for m in range(DC):
                        nc.tensor.matmul(k.bank(0, P, T, m * BT + b * T), kvb[:, m, b], q[:, m, b * T:(b + 1) * T], start=True, stop=True)
                        last = nc.tensor.matmul(k.bank(1, P, T, m * BT + b * T), kb[:, m, b], q[:, m, b * T:(b + 1) * T], start=True, stop=True)
                last.then_inc(s.attn_in_psum, 1)
                pe.wait_ge(s.o_ready, 1)
                for b in range(B):
                    last = matmul_acc(nc, k.bank(2, P, D, b * D), [(z[:, c, b * T:(b + 1) * T], wo[:, c]) for c in range(DC)])
                last.then_inc(s.out_ready, 1)

            @block.scalar
            def _(act):
                act.wait_ge(k.w_loaded[6], 80)
                act.wait_ge(s.gate_in_psum, 1)
                for m in range(DC):
                    nc.scalar.activation(gate[:, m], k.bank(1, P, BT, m * BT), ACT.Sigmoid, bias=bg[:, m:m + 1]).then_inc(s.gate_ready, 1)
                act.wait_ge(s.low_ready, 1)
                nc.scalar.activation(ex[:, 2], low[:, 2], ACT.Exp).then_inc(s.exp_ready, 1)
                act.wait_ge(s.ones_ready, 1)

                def take_v(i):
                    act.wait_ge(s.kf_ready, i + 1)
                    if i >= 4:
                        act.wait_ge(s.tile_used, i - 3)
                    nc.scalar.copy(va[:, i % 4, :, 0:P], k.bank(2 + i % 4, P, D, D).rearrange("p (m n) -> p m n", m=DC)).then_inc(s.v_taken, 1)
                for i in range(NKT):
                    act.wait_ge(s.low_ready, i + 2)
                    nc.scalar.activation(ex[:, i % 2, 0:D], low[:, i % 2, 0:D], ACT.Exp).then_inc(s.exp_ready, 1)
                    if i >= 1:
                        take_v(i - 1)
                take_v(NKT - 1)

            @block.vector
            def _(dve):
                link = chain(dve, s.dve_step)
                nc.vector.memset(va[:, :, :, P:P + 1], 1.0).then_inc(s.ones_ready, 1)
                dve.wait_ge(s.q_in_psum, 1)
                nc.vector.tensor_scalar(low[:, 2], k.bank(0), 0.0, None, ALU.min).then_inc(s.low_ready, 1)
                dve.wait_ge(s.exp_ready, 1)
                link(nc.vector.scalar_tensor_tensor(out=flat(q), in0=k.bank(0), scalar=0.0, in1=ex[:, 2], op0=ALU.max, op1=ALU.add))

                def feature(i):
                    dve.wait_ge(s.exp_ready, i + 2)
                    if i >= 4:
                        dve.wait_ge(s.tile_used, i - 3)
                    nc.vector.scalar_tensor_tensor(out=kf[:, i % 4], in0=k.bank(2 + i % 4, P, D), scalar=0.0, in1=ex[:, i % 2, 0:D],
                                                   op0=ALU.max, op1=ALU.add).then_inc(s.kf_ready, 1)

                def take_summary(b):
                    dve.wait_ge(s.tile_used, nt * (b + 1))
                    for m in range(DC):
                        link(nc.vector.tensor_tensor(kvb[:, m, b], k.bank(6 + m, P, P), k.blocks[:], ALU.mult))
                        link(nc.vector.tensor_scalar(kb[:, m, b], k.blocks[:], k.bank(6 + m, P, 1, P), None, ALU.mult))
                    dve.sem_inc(s.sum_taken, 1)
                for i in range(NKT):
                    dve.wait_ge(s.kv_in_psum, i + 1)
                    nc.vector.tensor_scalar(low[:, i % 2, 0:D], k.bank(2 + i % 4, P, D), 0.0, None, ALU.min).then_inc(s.low_ready, 1)
                    if i >= 1:
                        feature(i - 1)
                    if i == nt:
                        take_summary(0)
                feature(NKT - 1)
                take_summary(1)
                dve.wait_ge(s.attn_in_psum, 1)
                link(nc.vector.tensor_scalar(low[:, 0], k.bank(1), 1e-6, None, ALU.add))
                link(nc.vector.reciprocal(low[:, 1], low[:, 0]))
                link(nc.vector.tensor_tensor(flat(z), low[:, 1], k.bank(0), ALU.mult))
                dve.wait_ge(s.gate_ready, 2)
                nc.vector.tensor_tensor(flat(z), flat(z), flat(gate), ALU.mult).then_inc(s.o_ready, 1)
                dve.wait_ge(s.out_ready, 1)
                xf = k.x[:].rearrange("p b d -> p (b d)")
                nc.vector.tensor_tensor(xf, xf, k.bank(2), ALU.add)


def l2_attn(k):
    nc, A = k.nc, k.A
    nh = HEADS
    PAD = 32
    GH = P // PAD
    NU = B * nh // GH
    with ExitStack() as ctx:
        def sb(name, shape, dt=F32):
            return k.sb("a2_" + name, shape, dt, ctx)
        w = [sb("w" + n, [P, DC, D]) for n in "qkvo"]
        bias = [sb("b" + n, [P, D]) for n in "qkvo"]
        cos, sin = sb("cos", [P, HD]), sb("sin", [P, HD])
        qk = sb("qk", [P, 2, B, D])
        v = sb("v", [P, B, D])
        t1, t2 = sb("t1", [P, D]), sb("t2", [P, D])
        pad = sb("padded", [P, 2, B, nh, PAD])
        qkt = sb("qkT", [P, 2, GH, BT])
        cb = sb("causal", [P, P])
        sc, et = sb("scores", [P, 2, GH, T]), sb("eT", [P, 2, GH, T])
        sm = sb("small", [P, 2, GH, 2])
        rs = sb("rsum", [P, B, nh])
        attn, att = sb("attn", [P, B, D]), sb("attnT", [P, DC, BT])

        def load(sp):
            for t, n in zip(w, "qkvo"):
                sp.dma_start(t[:], A["L2_attn_W" + n + "_T"].rearrange("(c p) n -> p c n", p=P)).then_inc(k.w_loaded[7], 16)
            for t, n in zip(bias, "qkvo"):
                sp.dma_start(t[:], A["L2_attn_b" + n].rearrange("(a n) -> a n", a=1).to_broadcast([P, D])).then_inc(k.w_loaded[7], 16)
            sp.dma_start(cos[:], A["L2_cos"]).then_inc(k.w_loaded[7], 16)
            sp.dma_start(sin[:], A["L2_sin"]).then_inc(k.w_loaded[7], 16)
        layernorm(k, load)
        names = ("dve_step proj_ready padded_ready zeroed t_in_psum t_taken scores_in_psum centred_ready exp_ready et_in_psum et_ready "
                 "v_ready pv_ready attn_ready attnT_in_psum attnT_ready out_ready pool_step")
        with signals(nc, k.pool, names) as s, nc.Block() as block:
            @block.gpsimd
            def _(pool):
                pool.memset(pad[:], 0.0).then_inc(s.zeroed, 1)
                pool.memset(cb[:], 0.0).then_inc(s.pool_step, 1)
                pool.wait_ge(s.pool_step, 1)
                nc.gpsimd.affine_select(out=cb[:], in_=cb[:], compare_op=ALU.is_ge, fill=NEG, base=0, pattern=[[-1, P]],
                                        channel_multiplier=1).then_inc(s.zeroed, 1)

            @block.tensor
            def _(pe):
                pe.wait_ge(k.w_loaded[7], 160)
                for j in range(3):
                    for b in range(B):
                        last = matmul_acc(nc, k.bank(j, P, D, b * D), [(k.xt[:, c, b * T:(b + 1) * T], w[j][:, c]) for c in range(DC)])
                    last.then_inc(s.proj_ready, 1)
                for j in range(2):
                    for b in range(B):
                        pe.wait_ge(s.padded_ready, 2 * j + b + 1)
                        for g in range(GH):
                            last = nc.tensor.transpose(k.bank(3 + 2 * j + b, P, P, g * P),
                                                       pad[:, j, b, GH * g:GH * (g + 1)].rearrange("p h d -> p (h d)"), k.ident[:])
                        last.then_inc(s.t_in_psum, 1)
                pe.wait_ge(s.t_taken, 4)
                pe.wait_ge(s.v_ready, B)

                def scores(u):
                    b, g = divmod(u, GH)
                    if u >= 1:
                        pe.wait_ge(s.centred_ready, u)
                    for j in range(GH):
                        r = slice(PAD * j, PAD * (j + 1))
                        last = nc.tensor.matmul(k.bank(j, P, T), qkt[r, 0, g, b * T:(b + 1) * T], qkt[r, 1, g, b * T:(b + 1) * T],
                                                start=True, stop=True)
                    last.then_inc(s.scores_in_psum, 1)
                scores(0)
                for u in range(NU + 1):
                    if u + 1 < NU:
                        scores(u + 1)
                    if u < NU:
                        pe.wait_ge(s.exp_ready, u + 1)
                        if u >= 2:
                            pe.wait_ge(s.et_ready, u - 1)
                        for j in range(GH):
                            last = nc.tensor.transpose(k.bank(4 + u % 2, P, T, j * T), sc[:, u % 2, j], k.ident[:])
                        last.then_inc(s.et_in_psum, 1)
                    if u >= 1:
                        done = u - 1
                        b, g = divmod(done, GH)
                        pe.wait_ge(s.et_ready, done + 1)
                        for j in range(GH):
                            a = (GH * g + j) * HD
                            last = nc.tensor.matmul(k.bank(7 if b else 6, P, HD, a), et[:, done % 2, j], v[:, b, a:a + HD], start=True, stop=True)
                        last.then_inc(s.pv_ready, 1)
                for b in range(B):
                    pe.wait_ge(s.attn_ready, b + 1)
                    for c in range(DC):
                        last = nc.tensor.transpose(k.bank(3, P, T, c * BT + b * T), attn[:, b, c * P:(c + 1) * P], k.ident[:])
                last.then_inc(s.attnT_in_psum, 1)
                pe.wait_ge(s.attnT_ready, 1)
                for b in range(B):
                    last = matmul_acc(nc, k.bank(2, P, D, b * D), [(att[:, c, b * T:(b + 1) * T], w[3][:, c]) for c in range(DC)])
                last.then_inc(s.out_ready, 1)

            @block.scalar
            def _(act):
                for j in range(2):
                    for b in range(B):
                        act.wait_ge(s.t_in_psum, 2 * j + b + 1)
                        nc.scalar.copy(qkt[:, j, :, b * T:(b + 1) * T], k.bank(3 + 2 * j + b).rearrange("p (g n) -> p g n", g=GH)).then_inc(s.t_taken, 1)
                for u in range(NU + 1):
                    if u < NU:
                        act.wait_ge(s.centred_ready, u + 1)
                        nc.scalar.activation(sc[:, u % 2], sc[:, u % 2], ACT.Exp).then_inc(s.exp_ready, 1)
                    if u >= 1:
                        done = u - 1
                        act.wait_ge(s.et_in_psum, done + 1)
                        if done >= 2:
                            act.wait_ge(s.pv_ready, done - 1)
                        nc.scalar.copy(et[:, done % 2].rearrange("p g t -> p (g t)"), k.bank(4 + done % 2)).then_inc(s.et_ready, 1)
                act.wait_ge(s.attnT_in_psum, 1)
                nc.scalar.copy(att[:].rearrange("p c t -> p (c t)"), k.bank(3)).then_inc(s.attnT_ready, 1)

            @block.vector
            def _(dve):
                link = chain(dve, s.dve_step)
                dve.wait_ge(k.w_loaded[7], 160)
                dve.wait_ge(s.zeroed, 2)
                half = HD // 2
                for j in range(2):
                    dve.wait_ge(s.proj_ready, j + 1)
                    for b in range(B):
                        link(nc.vector.tensor_tensor(qk[:, j, b], k.bank(j, P, D, b * D), bias[j][:], ALU.add))
                        x3 = qk[:, j, b].rearrange("p (h d) -> p h d", d=HD)
                        a3, b3 = (t[:].rearrange("p (h d) -> p h d", d=HD) for t in (t1, t2))
                        link(nc.vector.tensor_tensor(a3, x3, cos[:].unsqueeze(1).to_broadcast([P, nh, HD]), ALU.mult))
                        link(nc.vector.tensor_tensor(b3[:, :, 0:half], x3[:, :, half:HD], sin[:, 0:half].unsqueeze(1).to_broadcast([P, nh, half]), ALU.mult))
                        link(nc.vector.tensor_tensor(b3[:, :, half:HD], x3[:, :, 0:half], sin[:, half:HD].unsqueeze(1).to_broadcast([P, nh, half]), ALU.mult))
                        nc.vector.tensor_tensor(pad[:, j, b, :, 0:HD], a3, b3, ALU.add).then_inc(s.padded_ready, 1)
                        dve.wait_ge(s.padded_ready, 2 * j + b + 1)
                dve.wait_ge(s.proj_ready, 3)
                for b in range(B):
                    nc.vector.tensor_tensor(v[:, b], k.bank(2, P, D, b * D), bias[2][:], ALU.add).then_inc(s.v_ready, 1)

                def sums(u):
                    b, g = divmod(u, GH)
                    r = u % 2
                    dve.wait_ge(s.exp_ready, u + 1)
                    link(nc.vector.reduce_sum(sm[:, r, :, 1], sc[:, r], AX.X))
                    link(nc.vector.reciprocal(rs[:, b, GH * g:GH * (g + 1)], sm[:, r, :, 1]))
                for u in range(NU):
                    r = u % 2
                    dve.wait_ge(s.scores_in_psum, u + 1)
                    if u >= 2:
                        dve.wait_ge(s.et_in_psum, u - 1)
                    link(nc.vector.scalar_tensor_tensor(out=sc[:, r], in0=k.ps[:, 0:GH, 0:T], scalar=1.0 / float(np.sqrt(HD)),
                                                        in1=cb[:].unsqueeze(1).to_broadcast([P, GH, T]), op0=ALU.mult, op1=ALU.add))
                    link(nc.vector.reduce_max(sm[:, r, :, 0], sc[:, r], AX.X))
                    nc.vector.tensor_tensor(sc[:, r], sc[:, r], sm[:, r, :, 0].unsqueeze(2).to_broadcast([P, GH, T]), ALU.subtract).then_inc(s.centred_ready, 1)
                    if u >= 1:
                        sums(u - 1)
                sums(NU - 1)
                for b in range(B):
                    dve.wait_ge(s.pv_ready, GH * (b + 1))
                    nc.vector.tensor_tensor(attn[:, b].rearrange("p (h d) -> p h d", d=HD), k.bank(7 if b else 6, P, D).rearrange("p (h d) -> p h d", d=HD),
                                            rs[:, b].unsqueeze(2).to_broadcast([P, nh, HD]), ALU.mult).then_inc(s.attn_ready, 1)
                for b in range(B):
                    link(nc.vector.tensor_tensor(k.x[:, b], k.x[:, b], bias[3][:], ALU.add))
                dve.wait_ge(s.out_ready, 1)
                xf = k.x[:].rearrange("p b d -> p (b d)")
                nc.vector.tensor_tensor(xf, xf, k.bank(2), ALU.add)


LORAS = 8
RANK = 16


def l2_ffn(k):
    nc, A = k.nc, k.A
    ne = LORAS
    with ExitStack() as ctx:
        def sb(name, shape, dt=F32):
            return k.sb("f2_" + name, shape, dt, ctx)
        w, wa, wgt = sb("w", [P, DC, D]), sb("lora_a", [P, DC, P]), sb("gate_w", [P, DC, ne])
        wb = sb("lora_b", [P, D])
        bias, gb = sb("bias", [P, D]), sb("gate_b", [P, ne])
        lg, mk = sb("logits", [P, B, 16]), sb("marked", [P, B, 16])
        top, sm = sb("top", [P, B, 8]), sb("small", [P, B, 8])
        g = sb("gates", [P, B, ne])
        xa, xat = sb("xa", [P, B, P]), sb("xaT", [P, BT])

        def load(sp):
            for t, n in ((w, "L2_ffn_W_T"), (wa, "L2_ffn_lora_A_T"), (wgt, "L2_ffn_gate_w_T")):
                sp.dma_start(t[:], A[n].rearrange("(c p) n -> p c n", p=P)).then_inc(k.w_loaded[8], 16)
            sp.dma_start(wb[:], A["L2_ffn_lora_B_T"]).then_inc(k.w_loaded[8], 16)
            sp.dma_start(bias[:], A["L2_ffn_b"].rearrange("(a n) -> a n", a=1).to_broadcast([P, D])).then_inc(k.w_loaded[8], 16)
            sp.dma_start(gb[:], A["L2_ffn_gate_b"].rearrange("(a n) -> a n", a=1).to_broadcast([P, ne])).then_inc(k.w_loaded[8], 16)
        layernorm(k, load)
        with signals(nc, k.pool, "dve_step logits_ready xa_in_psum neg_ready exp_ready xa_ready xaT_in_psum xaT_ready out_ready") as s, \
                nc.Block() as block:
            @block.tensor
            def _(pe):
                pe.wait_ge(k.w_loaded[8], 96)
                for b in range(B):
                    last = matmul_acc(nc, k.bank(0, P, ne, b * ne), [(k.xt[:, c, b * T:(b + 1) * T], wgt[:, c]) for c in range(DC)])
                last.then_inc(s.logits_ready, 1)
                for b in range(B):
                    last = matmul_acc(nc, k.bank(1, P, P, b * P), [(k.xt[:, c, b * T:(b + 1) * T], wa[:, c]) for c in range(DC)])
                last.then_inc(s.xa_in_psum, 1)
                pe.wait_ge(s.xa_ready, B)
                for b in range(B):
                    last = nc.tensor.transpose(k.bank(2, P, P, b * T), xa[:, b], k.ident[:])
                last.then_inc(s.xaT_in_psum, 1)
                pe.wait_ge(s.xaT_ready, 1)
                for b in range(B):
                    sl = slice(b * T, (b + 1) * T)
                    last = matmul_acc(nc, k.bank(3, P, D, b * D), [(k.xt[:, c, sl], w[:, c]) for c in range(DC)] + [(xat[:, sl], wb[:])])
                last.then_inc(s.out_ready, 1)

            @block.scalar
            def _(act):
                act.wait_ge(s.neg_ready, B)
                for b in range(B):
                    nc.scalar.activation(g[:, b], lg[:, b, 0:ne], ACT.Exp, bias=sm[:, b, 0:1]).then_inc(s.exp_ready, 1)
                act.wait_ge(s.xaT_in_psum, 1)
                nc.scalar.copy(xat[:], k.bank(2, P, BT)).then_inc(s.xaT_ready, 1)

            @block.vector
            def _(dve):
                link = chain(dve, s.dve_step)
                dve.wait_ge(k.w_loaded[8], 96)
                for b in range(B):
                    for j in range(ne):
                        last = nc.vector.memset(lg[:, b, ne + j:ne + j + 1], NEG * (j + 1))
                link(last)
                dve.wait_ge(s.logits_ready, 1)
                for b in range(B):
                    link(nc.vector.tensor_tensor(lg[:, b, 0:ne], k.bank(0, P, ne, b * ne), gb[:], ALU.add))
                    link(nc.vector.max(top[:, b], lg[:, b]))
                    nc.vector.tensor_scalar(sm[:, b, 0:1], top[:, b, 0:1], -1.0, None, ALU.mult).then_inc(s.neg_ready, 1)
                    dve.wait_ge(s.neg_ready, b + 1)
                    for j in range(6):
                        last = nc.vector.memset(top[:, b, 2 + j:3 + j], NEG * (j + 1))
                    link(last)
                    link(nc.vector.match_replace(mk[:, b], top[:, b], lg[:, b], 100 * NEG))
                    link(nc.vector.tensor_scalar(mk[:, b, 0:ne], mk[:, b, 0:ne], 100 * NEG, None, ALU.is_equal))
                dve.wait_ge(s.exp_ready, B)
                for b in range(B):
                    link(nc.vector.tensor_tensor(g[:, b], g[:, b], mk[:, b, 0:ne], ALU.mult))
                    link(nc.vector.reduce_sum(sm[:, b, 1:2], g[:, b], AX.X))
                    link(nc.vector.reciprocal(sm[:, b, 2:3], sm[:, b, 1:2]))
                    link(nc.vector.tensor_scalar(g[:, b], g[:, b], sm[:, b, 2:3], None, ALU.mult))
                dve.wait_ge(s.xa_in_psum, 1)
                for b in range(B):
                    nc.vector.tensor_tensor(xa[:, b].rearrange("p (e r) -> p e r", r=RANK), k.bank(1, P, P, b * P).rearrange("p (e r) -> p e r", r=RANK),
                                            g[:, b].unsqueeze(2).to_broadcast([P, ne, RANK]), ALU.mult).then_inc(s.xa_ready, 1)
                for b in range(B):
                    link(nc.vector.tensor_tensor(k.x[:, b], k.x[:, b], bias[:], ALU.add))
                dve.wait_ge(s.out_ready, 1)
                xf = k.x[:].rearrange("p b d -> p (b d)")
                nc.vector.tensor_tensor(xf, xf, k.bank(3), ALU.add)


TWO_PI = 2 * np.pi
TP1 = 6.28125
TP2 = int((TWO_PI - TP1) * 2 ** 21) / 2 ** 21
TP3 = float(np.float32(TWO_PI - TP1 - TP2))
PI_IN = 3.1415925


def reduce_angle(nc, link, ang, turns, src=None):
    src = ang if src is None else src
    link(nc.vector.tensor_scalar(turns, src, float(1 / TWO_PI), ROUND, ALU.mult, ALU.add))
    link(nc.vector.tensor_scalar(turns, turns, ROUND, None, ALU.subtract))
    for part in (TP1, TP2, TP3):
        link(nc.vector.scalar_tensor_tensor(out=ang, in0=turns, scalar=-part, in1=src, op0=ALU.mult, op1=ALU.add))
        src = ang
    link(nc.vector.tensor_scalar(ang, ang, PI_IN, -PI_IN, ALU.min, ALU.max))


H3 = 16
KVH = 4
HD3 = 128
HALF = HD3 // 2
RMS_EPS = 1e-6
KT3 = S2 // P + 1


def l3_xattn(k):
    nc, A = k.nc, k.A
    NQ = H3 // KVH
    NI = NQ + KT3
    NK = KT3 * P
    NG = (KT3 + 3) // 4
    GA = 3
    with ExitStack() as ctx:
        def sb(name, shape, dt=F32):
            return k.sb("x3_" + name, shape, dt, ctx)
        wq, wk, wv = sb("wq", [P, DC, H3 * HD3]), sb("wk", [P, DC, KVH * HD3]), sb("wv", [P, DC, KVH * HD3])
        wo = sb("wo", [P, H3, D])
        nw = sb("norm_w", [P, 2, HD3])
        invf = sb("inv_freq", [P, HALF])
        posi, posf = sb("pos_i", [P, B, KT3], I32), sb("pos_f", [P, B, KT3])
        tc, ts = sb("tab_cos", [P, KT3 + 1, HD3]), sb("tab_sin", [P, KT3 + 1, HD3])
        t1, t2 = sb("t1", [P, 4, 4, HD3]), sb("t2", [P, 2, 4, HD3])
        st = sb("rms", [P, 4, 3, 4])
        kt, vt = sb("kT", [P, KVH, NK]), sb("v", [P, KT3, KVH * HD3])
        qt = sb("qT", [P, H3, T])
        ex = sb("exps", [P, 2, NK])
        ang, turn, sn, cs = (kt[:].rearrange("p a n -> p (a n)").rearrange("p (c t f) -> p c t f", t=KT3, f=HALF)[:, j] for j in range(4))
        et = t2
        sm = sb("small", [P, 2, 4])
        on = k.xn[:].rearrange("p a n -> p (a n)")[:, 0:2 * HD3].rearrange("p (a n) -> p a n", a=2)
        ot = t1[:].rearrange("p a h n -> p (a h) n")

        def load(sp):
            sp.dma_start(invf[:], A["L3_inv_freq"].rearrange("(a n) -> a n", a=1).to_broadcast([P, HALF])).then_inc(k.pos_loaded, 16)
            for b in range(B):
                sp.dma_start(posi[:, b, 0:KT3 - 1], A["pos_BxS2"][b].rearrange("(n p) -> p n", p=P), allow_slow_non_contiguous=True).then_inc(k.pos_loaded, 16)
                sp.dma_start(posi[:, b, KT3 - 1:KT3], A["itok_BxS_4096_4607"][b].rearrange("(n p) -> p n", p=P), allow_slow_non_contiguous=True).then_inc(k.pos_loaded, 16)
            for j, n in enumerate(("q_norm_w", "k_norm_w")):
                sp.dma_start(nw[:, j], A["L3_xattn_" + n].rearrange("(a n) -> a n", a=1).to_broadcast([P, HD3])).then_inc(k.pos_loaded, 16)
            for t, n, sem in ((wq, "Wq", k.w_loaded[9]), (wk, "Wk", k.w_loaded[9]), (wv, "Wv", k.w_loaded[9]), (wo, "Wo", k.wo_loaded)):
                sp.dma_start(t[:], A["L3_xattn_" + n + "_T"].rearrange("(c p) n -> p c n", p=P)).then_inc(sem, 16)
        layernorm(k, load)
        NW = 3 * 16
        names = ("dve_step ang_ready trig_ready tab_ready proj_in_psum v_in_psum v_taken mults_done turned sq_done var_ready std_ready rstd_ready "
                 "normed t_in_psum t_taken scores_in_psum neg_ready exp_done et_in_psum et_ready_act et_ready_dve et_used pv_in_psum on_ready "
                 "ot_in_psum ot_taken out_ready out_taken")
        with signals(nc, k.pool, names) as s, nc.Block() as block:
            def wait_turned(engine, q):
                n, g = divmod(q, NG)
                if g < GA:
                    engine.wait_ge(s.et_ready_act, n * GA + g + 1)
                else:
                    engine.wait_ge(s.et_ready_dve, n * (NG - GA) + g - GA + 1)

            def source(b, i):
                if i < NQ:
                    return [(k.xt[:, c, b * T:(b + 1) * T], wq[:, c, i * 512:(i + 1) * 512]) for c in range(DC)]
                return [(key_src(b, i - NQ, c), wk[:, c]) for c in range(DC)]

            def key_src(b, j, c):
                if j == KT3 - 1:
                    return k.xt[:, c, b * T:(b + 1) * T]
                return k.ctxt[:, c, b * S2 + j * P:b * S2 + (j + 1) * P]

            @block.tensor
            def _(pe):
                pe.wait_ge(k.w_loaded[9], NW)
                for loaded in k.ctx_loaded:
                    pe.wait_ge(loaded, 16)
                for b in range(B):
                    def turn_back(i):
                        n = b * NI + i
                        pe.wait_ge(s.normed, n + 1)
                        if n >= 2:
                            pe.wait_ge(s.t_taken, n - 1)
                        for h in range(4):
                            last = nc.tensor.transpose(k.bank(4 + n % 2, P, P, h * P), t1[:, n % 4, h], k.ident[:])
                        last.then_inc(s.t_in_psum, 1)
                    for i in range(NI):
                        n = b * NI + i
                        if n >= 2:
                            pe.wait_ge(s.sq_done, n - 1)
                        matmul_acc(nc, k.bank(n % 2), source(b, i)).then_inc(s.proj_in_psum, 1)
                        if i >= NQ:
                            m = b * KT3 + i - NQ
                            if m >= 2:
                                pe.wait_ge(s.v_taken, m - 1)
                            matmul_acc(nc, k.bank(2 + m % 2), [(key_src(b, i - NQ, c), wv[:, c]) for c in range(DC)]).then_inc(s.v_in_psum, 1)
                        if i >= 3:
                            turn_back(i - 3)
                    for i in range(NI - 3, NI):
                        turn_back(i)
                    pe.wait_ge(s.t_taken, (b + 1) * NI)
                    pe.wait_ge(s.v_taken, (b + 1) * KT3)

                    def scores(h):
                        n = b * H3 + h
                        if n >= 1:
                            pe.wait_ge(s.exp_done, n)
                        for a in range(0, NK, 512):
                            w = min(512, NK - a)
                            last = nc.tensor.matmul(k.bank(a // 512, P, w), qt[:, h], kt[:, h // NQ, a:a + w], start=True, stop=True)
                        last.then_inc(s.scores_in_psum, 1)

                    def values(h):
                        n = b * H3 + h
                        pe.wait_ge(s.exp_done, n + 1)

                        def pv(g):
                            if g == 0 and n >= 1:
                                pe.wait_ge(s.on_ready, n)
                                if n >= 2:
                                    pe.wait_ge(s.ot_taken, n - 1)
                            wait_turned(pe, n * NG + g)
                            for j in range(4 * g, min(4 * g + 4, KT3)):
                                last = nc.tensor.matmul(k.bank(7, P, HD3), et[:, (n * NG + g) % 2, j % 4], vt[:, j, (h // NQ) * HD3:(h // NQ + 1) * HD3],
                                                        start=(j == 0), stop=(j == KT3 - 1))
                            last.then_inc(s.et_used, 1)
                        for g in range(NG):
                            q = n * NG + g
                            if q >= 2:
                                wait_turned(pe, q - 2)
                            for j in range(4 * g, min(4 * g + 4, KT3)):
                                last = nc.tensor.transpose(k.bank(5 + q % 2, P, P, (j % 4) * P), ex[:, n % 2, j * P:(j + 1) * P], k.ident[:])
                            last.then_inc(s.et_in_psum, 1)
                            if g >= 1:
                                pv(g - 1)
                        pv(NG - 1)

                    def turn_out(h):
                        n = b * H3 + h
                        pe.wait_ge(s.on_ready, n + 1)
                        nc.tensor.transpose(k.bank(7, P, P, 256), on[:, n % 2], k.ident[:]).then_inc(s.ot_in_psum, 1)
                    scores(0)
                    for h in range(H3):
                        if h + 1 < H3:
                            scores(h + 1)
                        if h >= 1:
                            turn_out(h - 1)
                        elif b:
                            pe.wait_ge(s.out_taken, b)
                        values(h)
                    turn_out(H3 - 1)
                    pe.wait_ge(s.ot_taken, (b + 1) * H3)
                    pe.wait_ge(k.wo_loaded, 16)
                    matmul_acc(nc, k.bank(6, P, D), [(ot[:, h], wo[:, h]) for h in range(H3)]).then_inc(s.out_ready, 1)

            @block.gpsimd
            def _(pool):
                def norm(n):
                    pool.wait_ge(s.rstd_ready, n + 1)
                    pool.wait_ge(s.turned, n + 1)
                    r = n % 4
                    nc.gpsimd.tensor_tensor(t1[:, r], t1[:, r], st[:, r, 2].unsqueeze(2).to_broadcast([P, 4, HD3]), ALU.mult).then_inc(s.normed, 1)
                for n in range(B * NI):
                    pool.wait_ge(s.mults_done, n + 1)
                    nc.gpsimd.tensor_tensor(t1[:, n % 4], t1[:, n % 4], t2[:, n % 2], ALU.add).then_inc(s.turned, 1)
                    if n % NI >= 2:
                        norm(n - 2)
                    if n % NI == NI - 1:
                        norm(n - 1)
                        norm(n)

            @block.scalar
            def _(act):
                def sines(b):
                    act.wait_ge(s.ang_ready, 2 * b + 1)
                    flat = lambda t: t.rearrange("p a n -> p (a n)")
                    nc.scalar.activation(flat(sn), flat(ang), ACT.Sin).then_inc(s.trig_ready, 1)
                    act.wait_ge(s.ang_ready, 2 * b + 2)
                    nc.scalar.activation(flat(cs), flat(turn), ACT.Sin).then_inc(s.trig_ready, 1)
                sines(0)
                for b in range(B):

                    def take(i):
                        n = b * NI + i
                        act.wait_ge(s.t_in_psum, n + 1)
                        src = k.bank(4 + n % 2).rearrange("p (h n) -> p h n", h=4)
                        dst = qt[:, 4 * i:4 * i + 4] if i < NQ else kt[:, :, (i - NQ) * P:(i - NQ + 1) * P]
                        nc.scalar.copy(dst, src).then_inc(s.t_taken, 1)

                    def root(i):
                        n = b * NI + i
                        act.wait_ge(s.var_ready, n + 1)
                        nc.scalar.activation(st[:, n % 4, 1], st[:, n % 4, 0], ACT.Sqrt).then_inc(s.std_ready, 1)
                    for i in range(NI):
                        n = b * NI + i
                        act.wait_ge(s.mults_done, n + 1)
                        if n >= 4:
                            act.wait_ge(s.normed, n - 3)
                        for h in range(4):
                            last = nc.scalar.activation(k.bank(n % 2, P, HD3, h * HD3), k.bank(n % 2, P, HD3, h * HD3), ACT.Square, accum_out=st[:, n % 4, 2, h:h + 1])
                        last.then_inc(s.sq_done, 1)
                        if i >= NQ:
                            m = b * KT3 + i - NQ
                            act.wait_ge(s.v_in_psum, m + 1)
                            nc.scalar.copy(vt[:, i - NQ], k.bank(2 + m % 2)).then_inc(s.v_taken, 1)
                        if i >= 1:
                            root(i - 1)
                        if i >= 4:
                            take(i - 4)
                    root(NI - 1)
                    for i in range(NI - 4, NI):
                        take(i)
                    for h in range(H3 + 2):
                        n = b * H3 + h
                        if h >= 2:
                            act.wait_ge(s.ot_in_psum, n - 1)
                            nc.scalar.copy(ot[:, h - 2], k.bank(7, P, P, 256)).then_inc(s.ot_taken, 1)
                        if 1 <= h <= H3:
                            for g in range(GA):
                                q = (n - 1) * NG + g
                                act.wait_ge(s.et_in_psum, q + 1)
                                if q >= 2:
                                    act.wait_ge(s.et_used, q - 1)
                                nc.scalar.copy(et[:, q % 2].rearrange("p a n -> p (a n)"), k.bank(5 + q % 2)).then_inc(s.et_ready_act, 1)
                        if h < H3:
                            act.wait_ge(s.neg_ready, n + 1)
                            if n >= 2:
                                act.wait_ge(s.et_in_psum, NG * (n - 1))
                            nc.scalar.activation(ex[:, n % 2], k.ps[:, 0:5].rearrange("p a n -> p (a n)")[:, 0:NK], ACT.Exp, bias=sm[:, n % 2, 1:2],
                                                 scale=1.0 / float(np.sqrt(HD3)), accum_out=sm[:, n % 2, 2:3]).then_inc(s.exp_done, 1)
                        if h == H3 and b + 1 < B:
                            sines(b + 1)

            @block.vector
            def _(dve):
                link = chain(dve, s.dve_step)
                dve.wait_ge(k.pos_loaded, (3 + 2 * B) * 16)
                link(nc.vector.tensor_copy(posf[:], posi[:]))

                def angles(b):
                    flat = lambda t: t.rearrange("p a n -> p (a n)")
                    link(nc.vector.tensor_tensor(ang, invf[:].unsqueeze(1).to_broadcast([P, KT3, HALF]),
                                                 posf[:, b].unsqueeze(2).to_broadcast([P, KT3, HALF]), ALU.mult))
                    reduce_angle(nc, link, flat(ang), flat(turn))
                    link(nc.vector.scalar_tensor_tensor(out=flat(turn), in0=flat(ang), scalar=-1.0, in1=flat(ang), op0=ALU.mult, op1=ALU.max))
                    dve.sem_inc(s.ang_ready, 1)
                    link(nc.vector.tensor_scalar(flat(turn), flat(turn), -1.0, float(np.pi / 2), ALU.mult, ALU.add))
                    dve.sem_inc(s.ang_ready, 1)

                def tables(b):
                    dve.wait_ge(s.trig_ready, 2 * b + 2)
                    for lo, n, j, a in ((0, KT3, 1, 0), (KT3, 1, 0, KT3 - 1)):
                        cc, ss = cs[:, a:a + n], sn[:, a:a + n]
                        for hf in range(2):
                            o = slice(hf * HALF, (hf + 1) * HALF)
                            other = slice((1 - hf) * HALF, (2 - hf) * HALF)
                            link(nc.vector.tensor_tensor(tc[:, lo:lo + n, o], cc, nw[:, j, o].unsqueeze(1).to_broadcast([P, n, HALF]), ALU.mult))
                            link(nc.vector.tensor_tensor(ts[:, lo:lo + n, o], ss, nw[:, j, other].unsqueeze(1).to_broadcast([P, n, HALF]), ALU.mult))
                        link(nc.vector.tensor_scalar(ts[:, lo:lo + n, 0:HALF], ts[:, lo:lo + n, 0:HALF], -1.0, None, ALU.mult))

                angles(0)
                tables(0)
                for b in range(B):
                    def variance(i):
                        n = b * NI + i
                        dve.wait_ge(s.sq_done, n + 1)
                        nc.vector.tensor_scalar(st[:, n % 4, 0], st[:, n % 4, 2], 1.0 / HD3, RMS_EPS, ALU.mult, ALU.add).then_inc(s.var_ready, 1)

                    def rstd(i):
                        n = b * NI + i
                        dve.wait_ge(s.std_ready, n + 1)
                        nc.vector.reciprocal(st[:, n % 4, 2], st[:, n % 4, 1]).then_inc(s.rstd_ready, 1)
                    for i in range(NI):
                        n = b * NI + i
                        e = KT3 if i < NQ else i - NQ
                        dve.wait_ge(s.proj_in_psum, n + 1)
                        if n >= 4:
                            dve.wait_ge(s.t_in_psum, n - 3)
                        if n >= 2:
                            dve.wait_ge(s.turned, n - 1)
                        src = k.bank(n % 2).rearrange("p (h n) -> p h n", h=4)
                        link(nc.vector.tensor_tensor(t1[:, n % 4], src, tc[:, e:e + 1].to_broadcast([P, 4, HD3]), ALU.mult))
                        for hf in range(2):
                            o = slice(hf * HALF, (hf + 1) * HALF)
                            other = slice((1 - hf) * HALF, (2 - hf) * HALF)
                            last = nc.vector.tensor_tensor(t2[:, n % 2, :, o], src[:, :, other], ts[:, e:e + 1, o].to_broadcast([P, 4, HALF]), ALU.mult)
                            if hf == 0:
                                link(last)
                        last.then_inc(s.mults_done, 1)
                        if i >= 1:
                            variance(i - 1)
                        if i >= 2:
                            rstd(i - 2)
                    variance(NI - 1)
                    rstd(NI - 2)
                    rstd(NI - 1)
                    for h in range(H3 + 1):
                        n = b * H3 + h
                        if h < H3:
                            dve.wait_ge(s.scores_in_psum, n + 1)
                            link(nc.vector.reduce_max(sm[:, n % 2, 0:1], k.ps[:, 0:5].rearrange("p a n -> p (a n)")[:, 0:NK], AX.X))
                            nc.vector.tensor_scalar(sm[:, n % 2, 1:2], sm[:, n % 2, 0:1], -1.0 / float(np.sqrt(HD3)), None, ALU.mult).then_inc(s.neg_ready, 1)
                        if h == 0:
                            continue
                        m = n - 1
                        for g in range(GA, NG):
                            q = m * NG + g
                            w = min(4, KT3 - 4 * g) * P
                            dve.wait_ge(s.et_in_psum, q + 1)
                            if q >= 2:
                                dve.wait_ge(s.et_used, q - 1)
                            nc.vector.tensor_copy(et[:, q % 2].rearrange("p a n -> p (a n)")[:, 0:w], k.bank(5 + q % 2, P, w)).then_inc(s.et_ready_dve, 1)
                        link(nc.vector.reciprocal(sm[:, m % 2, 3:4], sm[:, m % 2, 2:3]))
                        dve.wait_ge(s.et_used, (m + 1) * NG)
                        nc.vector.tensor_scalar(on[:, m % 2], k.bank(7, P, HD3), sm[:, m % 2, 3:4], None, ALU.mult).then_inc(s.on_ready, 1)
                        if h == H3 - 1 and b + 1 < B:
                            angles(b + 1)
                        if h == H3 and b + 1 < B:
                            tables(b + 1)
                    dve.wait_ge(s.out_ready, b + 1)
                    nc.vector.tensor_tensor(k.x[:, b], k.x[:, b], k.bank(6, P, D), ALU.add).then_inc(s.out_taken, 1)


H4 = 64
N4 = 128
P4 = 8
DIN = H4 * P4
HG = 4


def l3_attn(k):
    nc, A = k.nc, k.A
    NTH = 8
    NG4 = H4 // HG
    NU = NG4 * B
    RB = 3
    W = HG * N4
    BC_BANKS = ((1, 2), (0, 5))
    with ExitStack() as ctx:
        def sb(name, shape, dt=F32):
            return k.sb("a3_" + name, shape, dt, ctx)
        wx, wz = sb("wx", [P, DC, DIN]), sb("wz", [P, DC, DIN])
        wdl = sb("w_dt_lam", [P, DC, 2 * H4])
        wout = sb("w_out", [P, DIN // P, D])
        ring = sb("w_ring", [P, RB, 2, DC, W])
        bring = sb("bias_ring", [P, RB, 2, W])
        nw = sb("norm_w", [P, 2, N4])
        al = sb("a_log", [P, H4])
        xw, xg = sb("x_past", [P, B, DIN]), sb("x_diag", [P, B, DIN])
        sz, y = sb("silu_z", [P, B, DIN]), sb("y", [P, B, DIN])
        dtr, dt, lam = sb("dt_raw", [P, 3, B, H4]), sb("dt", [P, B, H4]), sb("lam", [P, B, H4])
        la, gd, vv, ww = (sb(n, [P, B, H4]) for n in ("log_a", "g_diag", "v_next", "w_past"))
        after, strict, shift = sb("after", [P, P]), sb("strict", [P, P]), sb("shift", [P, P])
        cs = sb("cs", [P, B, H4, N4 // 2])
        sn = k.ctxt[:].rearrange("p c s -> p (c s)").rearrange("p (b h n) -> p b h n", b=B, h=H4)
        t1 = sb("t1", [P, 2, 2, HG, 2, N4 // 2])
        r1 = sb("r1", [P, 2, 2, HG, 2, N4 // 2])
        r2 = sb("r2", [P, 2, HG, 2, N4 // 2])
        junk = sb("junk", [P, 2, W], BF16)
        bct = sb("bcT", [P, 2, 2, W])
        dr, dg, ee = sb("decay_rhs", [P, 2, W]), sb("diag", [P, 2, W]), sb("e", [P, 4, W])
        st = sb("rms", [P, 2, 4, 2 * HG])
        yt = t1[:].rearrange("p a b h c n -> p (a b h c n)")[:, 0:DIN // P * BT].rearrange("p (c t) -> p c t", t=BT)
        thdt = r1[:].rearrange("p a b h c n -> p (a b h c n)")[:, 0:1024].rearrange("p (a n) -> p a n", a=2)
        quarter = sb("quarter_turn", [P, 1])
        turn = r2[:].rearrange("p a h c n -> p (a h c n)")[:, 0:512]

        def load(sp):
            def put(dst, src):
                sp.dma_start(dst, src).then_inc(k.w_loaded[10], 16)
            sp.dma_start(wdl[:], A["L3_attn_Wdtlam_T"].rearrange("(c p) n -> p c n", p=P)).then_inc(k.dt_w_loaded, 16)
            sp.dma_start(al[:], A["L3_attn_A_log"].rearrange("(a n) -> a n", a=1).to_broadcast([P, H4])).then_inc(k.dt_w_loaded, 16)
            put(wx[:], A["L3_attn_Wx_T"].rearrange("(c p) n -> p c n", p=P))
            put(wz[:], A["L3_attn_Wz_T"].rearrange("(c p) n -> p c n", p=P))
            put(wout[:], A["L3_attn_Wout_T"].rearrange("(c p) n -> p c n", p=P))
            for j, n in enumerate("BC"):
                put(nw[:, j], A[f"L3_attn_{n}n_w_perm"].rearrange("(a n) -> a n", a=1).to_broadcast([P, N4]))
        layernorm(k, load)
        NW = 5 * 16
        names = ("dve_step pool_step masks_ready slot_loaded0 slot_loaded1 slot_loaded2 w_used bias_used xz_in_psum dl_in_psum dlT_taken "
                 "negabs_ready e_ready e1_ready ln_ready lam_ready xz_taken la_ready sh_ready sh_in_psum ww_ready "
                 "th_in_psum thdt_ready cum_in_psum cum_taken abs_ready trig_done bc_in_psum sq_done var_ready std_ready "
                 "normed biased roped")
        names2 = ("added dr_ready past_ready d_in_psum exp_done bcT_in_psum bcT_ready")
        with signals(nc, k.pool, names + " " + names2 + " g_in_psum") as s, \
                nc.semaphore("mg_ready") as mg_ready, nc.semaphore("y_in_psum") as y_in_psum, \
                nc.semaphore("y_taken") as y_taken, nc.semaphore("yz_ready") as yz_ready, \
                nc.semaphore("yT_in_psum") as yT_in_psum, nc.semaphore("yT_ready") as yT_ready, \
                nc.semaphore("y_out") as y_out, nc.Block() as block:
            slot = (s.slot_loaded0, s.slot_loaded1, s.slot_loaded2)
            need, total = [], [0] * RB
            for i in range(NTH + NG4):
                total[i % RB] += 16 if i < NTH else 64
                need.append(total[i % RB])

            @block.sync
            def _(sp):
                for i in range(NTH + NG4):
                    r = i % RB
                    if i >= RB:
                        sp.wait_ge(s.w_used, i - RB + 1)
                    if i < NTH:
                        sp.dma_start(ring[:, r, 0], A["L3_attn_Wth_T"].rearrange("(c p) n -> p c n", p=P)[:, :, i * 512:(i + 1) * 512]).then_inc(slot[r], 16)
                        continue
                    g = i - NTH
                    if g >= RB:
                        sp.wait_ge(s.bias_used, 2 * (g - RB + 1) * 2)
                    for j, n in enumerate("BC"):
                        sp.dma_start(ring[:, r, j], A[f"L3_attn_W{n}_T"].rearrange("(c p) n -> p c n", p=P)[:, :, g * W:(g + 1) * W]).then_inc(slot[r], 16)
                        sp.dma_start(bring[:, r, j], A[f"L3_attn_{n}_bias_perm"].rearrange("(a n) -> a n", a=1)[:, g * W:(g + 1) * W].to_broadcast([P, W])).then_inc(slot[r], 16)

            @block.tensor
            def _(pe):
                pe.wait_ge(k.dt_w_loaded, 32)
                for b in range(B):
                    sl = slice(b * T, (b + 1) * T)
                    last = matmul_acc(nc, k.bank(4, P, 2 * H4, b * 2 * H4), [(k.xt[:, c, sl], wdl[:, c]) for c in range(DC)])
                last.then_inc(s.dl_in_psum, 1)
                pe.wait_ge(k.w_loaded[10], NW)
                for b in range(B):
                    sl = slice(b * T, (b + 1) * T)
                    for j, w in enumerate((wx, wz)):
                        last = matmul_acc(nc, k.bank(2 * j + b), [(k.xt[:, c, sl], w[:, c]) for c in range(DC)])
                last.then_inc(s.xz_in_psum, 1)
                pe.wait_ge(s.masks_ready, 3)
                pe.wait_ge(s.sh_ready, 1)
                nc.tensor.matmul(k.bank(5, P, B * H4), shift[:], vv[:].rearrange("p b h -> p (b h)"), start=True, stop=True).then_inc(s.sh_in_psum, 1)
                pe.wait_ge(s.xz_taken, 4)
                for m in range(NTH * B + 1):
                    if m < NTH * B:
                        i, b = divmod(m, B)
                        if b == 0:
                            pe.wait_ge(slot[i % RB], need[i])
                        if m >= 2:
                            pe.wait_ge(s.thdt_ready, m - 1)
                        last = matmul_acc(nc, k.bank(m % 2), [(k.xt[:, c, b * T:(b + 1) * T], ring[:, i % RB, 0, c]) for c in range(DC)])
                        last.then_inc(s.th_in_psum, 1)
                        if b == B - 1:
                            pe.wait_ge(s.th_in_psum, m + 1)
                            pe.sem_inc(s.w_used, 1)
                    if m >= 1:
                        q = m - 1
                        pe.wait_ge(s.thdt_ready, q + 1)
                        if q >= 2:
                            pe.wait_ge(s.cum_taken, q - 1)
                        nc.tensor.matmul(k.bank(2 + q % 2), k.keep[:], thdt[:, q % 2], start=True, stop=True).then_inc(s.cum_in_psum, 1)
                pe.wait_ge(s.cum_taken, NTH * B)

                def project(n):
                    g, b = divmod(n, B)
                    i = NTH + g
                    if b == 0:
                        pe.wait_ge(slot[i % RB], need[i])
                    if n >= 2:
                        pe.wait_ge(s.normed, n - 1)
                    for j in range(2):
                        last = matmul_acc(nc, k.bank(BC_BANKS[n % 2][j]), [(k.xt[:, c, b * T:(b + 1) * T], ring[:, i % RB, j, c]) for c in range(DC)])
                    last.then_inc(s.bc_in_psum, 1)
                    if b == B - 1:
                        pe.wait_ge(s.bc_in_psum, n + 1)
                        pe.sem_inc(s.w_used, 1)
                project(0)
                project(1)
                for n in range(NU + 4):

                    def turn(m, j):
                        pe.wait_ge(s.added, m + 1)
                        if m or j:
                            pe.wait_ge(s.bcT_ready, 2 * m + j)
                        for h in range(HG):
                            last = nc.tensor.transpose(k.bank(3, P, P, h * P), r1[:, m % 2, j, h].rearrange("p c n -> p (c n)"), k.ident[:])
                        last.then_inc(s.bcT_in_psum, 1)
                    if 2 <= n < NU + 2:
                        turn(n - 2, 0)
                    if 3 <= n < NU + 3:
                        m = n - 3
                        pe.wait_ge(s.bcT_ready, 2 * (m + 1))
                        if m >= 1:
                            pe.wait_ge(mg_ready, m)
                        for h in range(HG):
                            sl = slice(h * P, (h + 1) * P)
                            last = nc.tensor.matmul(k.bank(6, P, P, h * P), bct[:, m % 2, 0, sl], bct[:, m % 2, 1, sl], start=True, stop=True)
                        last.then_inc(s.g_in_psum, 1)
                    if 1 <= n < NU + 1:
                        m = n - 1
                        pe.wait_ge(s.dr_ready, m + 1)
                        if m >= 1:
                            pe.wait_ge(s.exp_done, m)
                        nc.tensor.matmul(k.bank(4), after[:], dr[:, m % 2], start=True, stop=True).then_inc(s.d_in_psum, 1)

                    if 2 <= n < NU + 2:
                        turn(n - 2, 1)
                    if n >= 4:
                        m = n - 4
                        g, b = divmod(m, B)
                        pe.wait_ge(mg_ready, m + 1)
                        if m >= 1:
                            pe.wait_ge(y_taken, m)
                        for h in range(HG):
                            hh = g * HG + h
                            for j, (of, x) in enumerate(((ee[:, m % 4], xw), (dg[:, m % 2], xg))):
                                last = nc.tensor.matmul(k.bank(7, P, P4, h * P4), of[:, h * P:(h + 1) * P], x[:, b, hh * P4:(hh + 1) * P4],
                                                        start=(j == 0), stop=(j == 1))
                        last.then_inc(y_in_psum, 1)
                    if n + 2 < NU:
                        project(n + 2)
                for b in range(B):
                    pe.wait_ge(yz_ready, b + 1)
                    for c in range(DIN // P):
                        last = nc.tensor.transpose(k.bank(b, P, T, c * T), y[:, b, c * P:(c + 1) * P], k.ident[:])
                    last.then_inc(yT_in_psum, 1)
                pe.wait_ge(yT_ready, B)
                for b in range(B):
                    last = matmul_acc(nc, k.bank(2, P, D, b * D), [(yt[:, c, b * T:(b + 1) * T], wout[:, c]) for c in range(DIN // P)])
                last.then_inc(y_out, 1)

            @block.scalar
            def _(act):
                fl = lambda t: t.rearrange("p b h -> p (b h)")
                act.wait_ge(k.dt_w_loaded, 32)
                nc.scalar.activation(al[:], al[:], ACT.Exp).then_inc(s.e_ready, 1)
                act.wait_ge(s.negabs_ready, 1)
                nc.scalar.activation(fl(dtr[:, 1]), fl(dtr[:, 1]), ACT.Exp).then_inc(s.e_ready, 1)
                act.wait_ge(s.e1_ready, 1)
                nc.scalar.activation(fl(dtr[:, 2]), fl(dtr[:, 2]), ACT.Ln).then_inc(s.ln_ready, 1)
                nc.scalar.activation(lam[:], k.bank(4, P, B * 2 * H4).rearrange("p (b a h) -> p b a h", b=B, a=2)[:, :, 1], ACT.Sigmoid).then_inc(s.lam_ready, 1)
                act.wait_ge(s.xz_in_psum, 1)
                for b in range(B):
                    nc.scalar.activation(sz[:, b], k.bank(2 + b), ACT.Sigmoid).then_inc(s.lam_ready, 1)
                for q in range(NTH * B):
                    i, b = divmod(q, B)
                    sl = slice(i * 8, (i + 1) * 8)
                    act.wait_ge(s.cum_taken, q + 1)
                    a = sn[:, b, sl].rearrange("p h n -> p (h n)")
                    c = cs[:, b, sl].rearrange("p h n -> p (h n)")
                    nc.scalar.activation(c, a, ACT.Abs).then_inc(s.abs_ready, 1)
                    act.wait_ge(s.abs_ready, q + 1)
                    nc.scalar.activation(c, c, ACT.Sin, bias=quarter[:, 0:1], scale=-1.0).then_inc(s.trig_done, 1)
                    nc.scalar.activation(a, a, ACT.Sin).then_inc(s.trig_done, 1)
                def squares(n):
                    r = n % 2
                    act.wait_ge(s.bc_in_psum, n + 1)
                    if n >= 1:
                        act.wait_ge(s.sq_done, n)
                    for j in range(2):
                        for h in range(HG):
                            last = nc.scalar.activation(junk[:, j, h * N4:(h + 1) * N4], k.bank(BC_BANKS[n % 2][j], P, N4, h * N4), ACT.Square,
                                                        accum_out=st[:, r, 0, j * HG + h:j * HG + h + 1])
                    last.then_inc(s.sq_done, 1)

                def root(n):
                    r = n % 2
                    act.wait_ge(s.var_ready, n + 1)
                    nc.scalar.activation(st[:, r, 2], st[:, r, 1], ACT.Sqrt).then_inc(s.std_ready, 1)
                squares(0)
                root(0)
                def take_turned(m, j):
                    if m >= 2 and j == 0:
                        act.wait_ge(s.g_in_psum, m - 1)
                    act.wait_ge(s.bcT_in_psum, 2 * m + j + 1)
                    nc.scalar.copy(bct[:, m % 2, j], k.bank(3)).then_inc(s.bcT_ready, 1)
                def decays(n):
                    g, b = divmod(n, B)
                    if n >= 2:
                        act.wait_ge(s.d_in_psum, n - 1)
                    for h in range(HG):
                        hh = g * HG + h
                        last = nc.scalar.activation(dr[:, n % 2, h * P:(h + 1) * P], k.keep[:], ACT.Copy, scale=la[:, b, hh:hh + 1])
                    last.then_inc(s.dr_ready, 1)
                for n in range(NU + 2):
                    if n >= 2:
                        take_turned(n - 2, 0)
                    if 1 <= n < NU + 1:
                        m = n - 1
                        act.wait_ge(s.d_in_psum, m + 1)
                        if m >= 4:
                            act.wait_ge(y_in_psum, m - 3)
                        nc.scalar.activation(ee[:, m % 4], k.bank(4), ACT.Exp).then_inc(s.exp_done, 1)
                    if n >= 2:
                        take_turned(n - 2, 1)
                    if n + 1 < NU:
                        squares(n + 1)
                    if n < NU:
                        decays(n)
                    if n + 1 < NU:
                        root(n + 1)
                for b in range(B):
                    act.wait_ge(yT_in_psum, b + 1)
                    nc.scalar.copy(yt[:, :, b * T:(b + 1) * T], k.bank(b).rearrange("p (c t) -> p c t", t=T)).then_inc(yT_ready, 1)

            @block.gpsimd
            def _(pool):
                nc.gpsimd.affine_select(out=after[:], in_=k.ones[:], compare_op=ALU.is_gt, fill=0.0, base=0, pattern=[[-1, P]],
                                        channel_multiplier=1).then_inc(s.masks_ready, 1)
                nc.gpsimd.affine_select(out=strict[:], in_=k.ones[:], compare_op=ALU.is_gt, fill=0.0, base=0, pattern=[[1, P]],
                                        channel_multiplier=-1).then_inc(s.masks_ready, 1)
                nc.gpsimd.affine_select(out=shift[:], in_=k.ones[:], compare_op=ALU.is_equal, fill=0.0, base=-1, pattern=[[-1, P]],
                                        channel_multiplier=1).then_inc(s.masks_ready, 1)
                pool.wait_ge(s.masks_ready, 3)
                pool.wait_ge(s.ww_ready, 1)
                for n in range(NU + 2):
                    if n >= 2:
                        m = n - 2
                        pool.wait_ge(s.exp_done, m + 1)
                        e4 = ee[:, m % 4].rearrange("p (h t) -> p h t", t=P)
                        nc.gpsimd.tensor_tensor(e4, e4, strict[:].unsqueeze(1).to_broadcast([P, HG, P]), ALU.mult).then_inc(s.past_ready, 1)
                    if n < NU:
                        g, b = divmod(n, B)
                        i = NTH + g
                        pool.wait_ge(slot[i % RB], need[i])
                        pool.wait_ge(s.normed, n + 1)
                        for j in range(2):
                            a = t1[:, n % 2, j].rearrange("p h c n -> p (h c n)")
                            last = nc.gpsimd.tensor_tensor(a, a, bring[:, i % RB, j], ALU.add).then_inc(s.bias_used, 1)
                    if 1 <= n < NU + 1:
                        m = n - 1
                        pool.wait_ge(s.roped, m + 1)
                        for j in range(2):
                            for hf, op in ((0, ALU.subtract), (1, ALU.add)):
                                a = r1[:, m % 2, j, :, hf]
                                last = nc.gpsimd.tensor_tensor(a, a, r2[:, j, :, hf], op)
                        last.then_inc(s.added, 1)

            @block.vector
            def _(dve):
                link = chain(dve, s.dve_step)
                fl = lambda t: t.rearrange("p b h -> p (b h)")
                link(nc.vector.memset(quarter[:], float(np.pi / 2)))
                dve.wait_ge(s.dl_in_psum, 1)
                dl = k.bank(4, P, B * 2 * H4).rearrange("p (b a h) -> p b a h", b=B, a=2)
                link(nc.vector.tensor_copy(dtr[:, 0], dl[:, :, 0]))
                nc.vector.scalar_tensor_tensor(out=fl(dtr[:, 1]), in0=fl(dtr[:, 0]), scalar=-1.0, in1=fl(dtr[:, 0]), op0=ALU.mult, op1=ALU.min).then_inc(s.negabs_ready, 1)
                dve.wait_ge(s.e_ready, 2)
                nc.vector.tensor_scalar(fl(dtr[:, 2]), fl(dtr[:, 1]), 1.0, None, ALU.add).then_inc(s.e1_ready, 1)
                dve.wait_ge(s.ln_ready, 1)
                link(nc.vector.scalar_tensor_tensor(out=fl(dt[:]), in0=fl(dtr[:, 0]), scalar=0.0, in1=fl(dtr[:, 2]), op0=ALU.max, op1=ALU.add))
                for b in range(B):
                    link(nc.vector.scalar_tensor_tensor(out=la[:, b], in0=dt[:, b], scalar=-1.0, in1=al[:], op0=ALU.mult, op1=ALU.mult))
                dve.wait_ge(s.lam_ready, 1)
                link(nc.vector.tensor_tensor(fl(gd[:]), fl(lam[:]), fl(dt[:]), ALU.mult))
                nc.vector.tensor_tensor(fl(vv[:]), fl(dt[:]), fl(gd[:]), ALU.subtract).then_inc(s.sh_ready, 1)
                dve.wait_ge(s.sh_in_psum, 1)
                nc.vector.tensor_tensor(fl(ww[:]), fl(gd[:]), k.bank(5, P, B * H4), ALU.add).then_inc(s.ww_ready, 1)
                dve.wait_ge(s.lam_ready, 1 + B)
                dve.wait_ge(s.ww_ready, 1)
                for b in range(B):
                    nc.vector.tensor_tensor(sz[:, b], sz[:, b], k.bank(2 + b), ALU.mult).then_inc(s.xz_taken, 1)
                    for x, by in ((xw, ww), (xg, gd)):
                        last = nc.vector.tensor_tensor(x[:, b].rearrange("p (h d) -> p h d", d=P4), k.bank(b).rearrange("p (h d) -> p h d", d=P4),
                                                       by[:, b].unsqueeze(2).to_broadcast([P, H4, P4]), ALU.mult)
                    last.then_inc(s.xz_taken, 1)

                def angles(q):
                    i, b = divmod(q, B)
                    sl = slice(i * 8, (i + 1) * 8)
                    a = sn[:, b, sl].rearrange("p h n -> p (h n)")
                    dve.wait_ge(s.cum_in_psum, q + 1)
                    reduce_angle(nc, link, a, turn, k.bank(2 + q % 2))
                    dve.sem_inc(s.cum_taken, 1)
                for q in range(NTH * B + 1):
                    if q < NTH * B:
                        i, b = divmod(q, B)
                        dve.wait_ge(s.th_in_psum, q + 1)
                        if q >= 2:
                            dve.wait_ge(s.cum_in_psum, q - 1)
                        nc.vector.tensor_tensor(thdt[:, q % 2].rearrange("p (h n) -> p h n", h=8), k.bank(q % 2).rearrange("p (h n) -> p h n", h=8),
                                                dt[:, b, i * 8:(i + 1) * 8].unsqueeze(2).to_broadcast([P, 8, N4 // 2]), ALU.mult).then_inc(s.thdt_ready, 1)
                    if q >= 1:
                        angles(q - 1)
                dve.wait_ge(s.trig_done, 2 * NTH * B)

                def variance(n):
                    dve.wait_ge(s.sq_done, n + 1)
                    nc.vector.tensor_scalar(st[:, n % 2, 1], st[:, n % 2, 0], 1.0 / N4, RMS_EPS, ALU.mult, ALU.add).then_inc(s.var_ready, 1)
                variance(0)
                for n in range(NU + 4):
                    r = n % 2
                    if n < NU:
                        dve.wait_ge(s.std_ready, n + 1)
                        if n >= 2:
                            dve.wait_ge(s.roped, n - 1)
                        link(nc.vector.reciprocal(st[:, r, 3], st[:, r, 2]))
                        for j in range(2):
                            for h in range(HG):
                                last = nc.vector.scalar_tensor_tensor(out=t1[:, r, j, h].rearrange("p c n -> p (c n)"), in0=k.bank(BC_BANKS[n % 2][j], P, N4, h * N4),
                                                                      scalar=st[:, r, 3, j * HG + h:j * HG + h + 1], in1=nw[:, j], op0=ALU.mult, op1=ALU.mult)
                        last.then_inc(s.normed, 1)
                    if 1 <= n < NU + 1:
                        m = n - 1
                        g, b = divmod(m, B)
                        dve.wait_ge(s.bias_used, 2 * (m + 1))
                        if m >= 2:
                            dve.wait_ge(s.bcT_in_psum, 2 * (m - 1))
                        if m >= 1:
                            dve.wait_ge(s.added, m)
                        cc = cs[:, b, g * HG:(g + 1) * HG]
                        ss = sn[:, b, g * HG:(g + 1) * HG]
                        for j in range(2):
                            nc.vector.tensor_tensor(r1[:, m % 2, j], t1[:, m % 2, j], cc.unsqueeze(2).to_broadcast([P, HG, 2, N4 // 2]), ALU.mult)
                            for hf in range(2):
                                last = nc.vector.tensor_tensor(r2[:, j, :, hf], t1[:, m % 2, j, :, 1 - hf], ss, ALU.mult)
                        last.then_inc(s.roped, 1)
                    if 3 <= n < NU + 3:
                        m = n - 3
                        g, b = divmod(m, B)
                        dve.wait_ge(s.past_ready, m + 1)
                        dve.wait_ge(s.g_in_psum, m + 1)
                        if m >= 2:
                            dve.wait_ge(y_in_psum, m - 1)
                        nc.vector.tensor_tensor(ee[:, m % 4], ee[:, m % 4], k.bank(6), ALU.mult)
                        nc.vector.tensor_tensor(dg[:, m % 2].rearrange("p (h t) -> p h t", t=P), k.bank(6).rearrange("p (h t) -> p h t", t=P),
                                                k.ident[:].unsqueeze(1).to_broadcast([P, HG, P]), ALU.mult).then_inc(mg_ready, 1)
                    if n + 1 < NU:
                        variance(n + 1)
                    if n >= 4:
                        m = n - 4
                        g, b = divmod(m, B)
                        dve.wait_ge(y_in_psum, m + 1)
                        nc.vector.tensor_copy(y[:, b, g * HG * P4:(g + 1) * HG * P4], k.bank(7, P, HG * P4)).then_inc(y_taken, 1)
                dve.wait_ge(y_taken, NU)
                for b in range(B):
                    nc.vector.tensor_tensor(y[:, b], y[:, b], sz[:, b], ALU.mult).then_inc(yz_ready, 1)
                dve.wait_ge(y_out, 1)
                xf = k.x[:].rearrange("p b d -> p (b d)")
                nc.vector.tensor_tensor(xf, xf, k.bank(2), ALU.add)


MLP = 2048
MATS = ("gate", "up", "down")
CW = 512


def l3_ffn(k):
    nc, A = k.nc, k.A
    NC = MLP // CW
    NS = NC * 3 * 2
    NT = MLP // P
    TPC = CW // P
    with ExitStack() as ctx:
        def sb(name, shape, dt=F32):
            return k.sb("f3_" + name, shape, dt, ctx)
        packed = sb("packed", [P, 3, MLP], I32)
        scale = sb("scales", [P, 3, MLP])
        xeo = sb("x_even_odd_T", [P, 2, BT])
        wd = sb("weights", [P, 3, 2, 2, CW])
        mg, sg = sb("magnitude", [P, 2, CW], I32), sb("sign_bit", [P, 2, CW], I32)
        m4, m6, ss = sb("max4", [P, 2, CW]), sb("max6", [P, 2, CW]), sb("signed_scale", [P, 2, CW])
        act_g, inter = sb("gelu", [P, 2, BT]), sb("inter", [P, 3, BT])

        def load(sp):
            for c in range(NC):
                sl = slice(c * CW, (c + 1) * CW)
                for j in range(3):
                    sp.dma_start(packed[:, j, sl], A["L3_ffn_packed_T"][j, :, sl]).then_inc(k.p_loaded[c], 16)
                    sp.dma_start(scale[:, j, sl], A["L3_ffn_scales_T"][j, :, sl].unsqueeze(1).to_broadcast([8, 16, CW])).then_inc(k.p_loaded[c], 16)
        layernorm(k, load)
        names = ("dve_step bits_ready pool_step scale_ready w_ready xT_in_psum xT_ready gu_in_psum gelu_ready inter_ready down_done")
        with signals(nc, k.pool, names) as s, nc.Block() as block:
            @block.tensor
            def _(pe):
                for e in range(2):
                    for b in range(B):
                        last = nc.tensor.transpose(k.bank(5, P, T, e * BT + b * T), k.xn[:, b, e::2], k.ident[:])
                last.then_inc(s.xT_in_psum, 1)
                pe.wait_ge(s.xT_ready, 1)

                def down(i):
                    c, j, par = i // TPC, (i % TPC) // 2, i % 2
                    pe.wait_ge(s.inter_ready, i + 1)
                    pe.wait_ge(s.w_ready, 6 * c + 6)
                    for b in range(B):
                        last = nc.tensor.matmul(k.bank(6 + b, P, D), inter[:, i % 3, b * T:(b + 1) * T], wd[:, 2, c % 2, par, j * D:(j + 1) * D],
                                                start=(i == 0), stop=(i == NT - 1))
                    last.then_inc(s.down_done, 1)
                for i in range(NT):
                    c = i // TPC
                    pe.wait_ge(s.w_ready, 6 * c + 4)
                    if i >= 4:
                        pe.wait_ge(s.inter_ready, i - 3)
                    sl = slice((i % TPC) * P, (i % TPC + 1) * P)
                    for j in range(2):
                        last = matmul_acc(nc, k.bank(i % 4, P, BT, j * BT), [(wd[:, j, c % 2, e, sl], xeo[:, e]) for e in range(2)])
                    last.then_inc(s.gu_in_psum, 1)
                    if i >= 1:
                        down(i - 1)
                down(NT - 1)

            @block.scalar
            def _(act):
                act.wait_ge(s.xT_in_psum, 1)
                nc.scalar.copy(xeo[:].rearrange("p c t -> p (c t)"), k.bank(5)).then_inc(s.xT_ready, 1)
                for i in range(NT):
                    act.wait_ge(s.gu_in_psum, i + 1)
                    if i >= 2:
                        act.wait_ge(s.inter_ready, i - 1)
                    nc.scalar.activation(act_g[:, i % 2], k.bank(i % 4, P, BT), ACT.Gelu_apprx_tanh).then_inc(s.gelu_ready, 1)

            @block.gpsimd
            def _(pool):
                for v in range(NS):
                    r = v % 2
                    c, j = divmod(v // 2, 3)
                    pool.wait_ge(k.p_loaded[c], 96)
                    pool.wait_ge(s.bits_ready, v + 1)
                    if v >= 2:
                        pool.wait_ge(s.w_ready, v - 1)
                    nc.gpsimd.tensor_scalar(ss[:, r], sg[:, r], -1.0, 0.5, ALU.mult, ALU.add).then_inc(s.pool_step, 1)
                    pool.wait_ge(s.pool_step, v + 1)
                    nc.gpsimd.tensor_tensor(ss[:, r], ss[:, r], scale[:, j, c * CW:(c + 1) * CW], ALU.mult).then_inc(s.scale_ready, 1)

            @block.vector
            def _(dve):
                link = chain(dve, s.dve_step)

                def bits(v):
                    r = v % 2
                    c, j = divmod(v // 2, 3)
                    dve.wait_ge(k.p_loaded[c], 96)
                    if v >= 2:
                        dve.wait_ge(s.scale_ready, v - 1)
                    w = packed[:, j, c * CW:(c + 1) * CW]
                    nc.vector.tensor_scalar(mg[:, r], w, 4 * (v % 2), 7, ALU.logical_shift_right, ALU.bitwise_and)
                    nc.vector.tensor_scalar(sg[:, r], w, 4 * (v % 2) + 3, 1, ALU.logical_shift_right, ALU.bitwise_and).then_inc(s.bits_ready, 1)

                def weights(v):
                    r = v % 2
                    c, j = divmod(v // 2, 3)
                    dve.wait_ge(s.bits_ready, v + 1)
                    nc.vector.tensor_scalar(m4[:, r], mg[:, r], 7.0, 4.0, ALU.min, ALU.max)
                    link(nc.vector.tensor_scalar(m6[:, r], mg[:, r], 7.0, 6.0, ALU.min, ALU.max))
                    if c >= 2:
                        dve.wait_ge(s.down_done, TPC * (c - 1))
                    link(nc.vector.scalar_tensor_tensor(out=m4[:, r], in0=m6[:, r], scalar=2.0, in1=m4[:, r], op0=ALU.mult, op1=ALU.add))
                    link(nc.vector.scalar_tensor_tensor(out=m4[:, r], in0=mg[:, r], scalar=-16.0, in1=m4[:, r], op0=ALU.add, op1=ALU.add))
                    dve.wait_ge(s.scale_ready, v + 1)
                    nc.vector.tensor_tensor(wd[:, j, c % 2, v % 2], m4[:, r], ss[:, r], ALU.mult).then_inc(s.w_ready, 1)

                def product(i):
                    dve.wait_ge(s.gelu_ready, i + 1)
                    if i >= 3:
                        dve.wait_ge(s.down_done, i - 2)
                    nc.vector.tensor_tensor(inter[:, i % 3], act_g[:, i % 2], k.bank(i % 4, P, BT, BT), ALU.mult).then_inc(s.inter_ready, 1)
                bits(0)
                for v in range(NS):
                    if v + 1 < NS:
                        bits(v + 1)
                    weights(v)
                    c, q = divmod(v, 6)
                    if c >= 1 and q < TPC:
                        product(TPC * (c - 1) + q)
                for q in range(TPC):
                    product(NT - TPC + q)
                dve.wait_ge(s.down_done, NT)
                for b in range(B):
                    nc.vector.tensor_tensor(k.x[:, b], k.x[:, b], k.bank(6 + b, P, D), ALU.add)


def layouts(i):
    c = np.ascontiguousarray
    d = {n: c(a) for n, a in i.items()}
    d["ctxT"] = c(i["ctx_2048"].reshape(KEYS, D).T)
    for n in "ifgo":
        d["L0_attn_W" + n + "_T"] = c(i["L0_attn_W" + n].T)
    d["L0_ffn_gate_w_T"] = c(i["L0_ffn_gate_w"].T)

    def experts(a, b):
        return np.concatenate([a, b.reshape(D, SHARED, INNER).transpose(1, 0, 2)])
    g, u = experts(i["L0_ffn_w_gate"], i["L0_ffn_sw_gate"]), experts(i["L0_ffn_w_up"], i["L0_ffn_sw_up"])
    d["L0_ffn_gate_up"] = c(np.stack([g, u], 2).reshape(EXPERTS + SHARED, DC, P, 2, INNER).transpose(0, 2, 1, 3, 4))
    dn = np.concatenate([i["L0_ffn_w_down"], i["L0_ffn_sw_down"].reshape(SHARED, INNER, D)])
    d["L0_ffn_down"] = c(dn.reshape(EXPERTS + SHARED, 2, IH, D).transpose(0, 2, 1, 3))
    d["L1_decay_ch"] = np.repeat(i["L1_attn_decay_param"], HD)
    d["L1_ffn_b1_T"] = c(i["L1_ffn_b1"].T)
    for n in ("Wq", "Wg", "Wkv", "Wo"):
        d["L2_xattn_" + n + "_T"] = c(i["L2_xattn_" + n].T)
    for n in "qkvo":
        d["L2_attn_W" + n + "_T"] = c(i["L2_attn_W" + n].T)
    ang = np.arange(1, T + 1, dtype=np.float64)[:, None] * 10000.0 ** (-2.0 * np.arange(HD // 2) / HD)[None]
    d["L2_cos"] = np.concatenate([np.cos(ang), np.cos(ang)], 1).astype(np.float32)
    d["L2_sin"] = np.concatenate([-np.sin(ang), np.sin(ang)], 1).astype(np.float32)
    d["L2_ffn_W_T"] = c(i["L2_ffn_W"].T)
    d["L2_ffn_lora_A_T"] = c(i["L2_ffn_lora_A"].reshape(P, D).T)
    d["L2_ffn_lora_B_T"] = c(i["L2_ffn_lora_B"].transpose(0, 2, 1).reshape(P, D))
    d["L2_ffn_gate_w_T"] = c(i["L2_ffn_gate_w"].T)
    for n in ("Wq", "Wk", "Wv", "Wo"):
        d["L3_xattn_" + n + "_T"] = c(i["L3_xattn_" + n].T)
    d["L3_inv_freq"] = (np.float32(1) / np.float32(10000.0) ** (np.arange(0, HD3, 2, dtype=np.float32) / np.float32(HD3))).astype(np.float32)
    even_first = np.concatenate([np.arange(0, N4, 2), np.arange(1, N4, 2)])
    for n in "BC":
        d[f"L3_attn_W{n}_T"] = c(i["L3_attn_W" + n].reshape(H4, N4, D)[:, even_first].reshape(H4 * N4, D).T)
        d[f"L3_attn_{n}_bias_perm"] = c(i[f"L3_attn_{n}_bias"][:, even_first]).reshape(-1)
        d[f"L3_attn_{n}n_w_perm"] = c(i[f"L3_attn_{n}n_w"][even_first])
    for n in ("Wx", "Wz", "Wth", "Wout"):
        d[f"L3_attn_{n}_T"] = c(i["L3_attn_" + n].T)
    d["L3_attn_Wdtlam_T"] = c(np.concatenate([i["L3_attn_Wdt"], i["L3_attn_Wlam"]]).T)
    def by_parity(w):
        return w.reshape(MLP // 256, P, 2, -1).transpose(3, 0, 2, 1).reshape(-1, MLP)
    down = i["L3_ffn_down_W_packed"].T.reshape(8, P, D).transpose(1, 0, 2).reshape(P, MLP)
    d["L3_ffn_packed_T"] = c(np.stack([by_parity(i["L3_ffn_gate_W_packed"]), by_parity(i["L3_ffn_up_W_packed"]), down]))
    down = i["L3_ffn_down_scales"].T.reshape(8, 8, D).transpose(1, 0, 2).reshape(8, MLP)
    d["L3_ffn_scales_T"] = c(np.stack([by_parity(i["L3_ffn_gate_scales"]), by_parity(i["L3_ffn_up_scales"]), down]))
    return d


STAGES = (l0_xattn, l0_attn, l0_ffn, l1_xattn, l1_attn, l1_ffn, l2_xattn, l2_attn, l2_ffn, l3_xattn, l3_attn, l3_ffn)

READ = ("x", "L0_xattn_bkv", "L0_xattn_Wkv", "L0_xattn_Wq", "L0_xattn_bq", "ctxT", "L0_xattn_Wp", "L0_xattn_bp",
        "L0_attn_Wi_T", "L0_attn_Wf_T", "L0_attn_Wg_T", "L0_attn_Wo_T", "L0_attn_gnorm_w", "L0_ffn_gate_w_T",
        "L0_ffn_gate_up", "L0_ffn_down", "mask_BxS2_bk0", "ctx_2048", "L1_decay_ch", "L1_attn_w_qkv",
        "L1_attn_w_out", "L1_ffn_mu", "L1_ffn_gamma", "L1_ffn_beta", "L1_ffn_scale", "L1_ffn_b1_T", "L1_ffn_W1",
        "L1_ffn_W2", "L1_ffn_b2", "L2_xattn_Wkv_T", "L2_xattn_Wq_T", "L2_xattn_Wg_T", "L2_xattn_Wo_T", "L2_xattn_bg",
        "L2_attn_Wq_T", "L2_attn_Wk_T", "L2_attn_Wv_T", "L2_attn_Wo_T", "L2_attn_bq", "L2_attn_bk", "L2_attn_bv",
        "L2_attn_bo", "L2_cos", "L2_sin", "L2_ffn_W_T", "L2_ffn_lora_A_T", "L2_ffn_gate_w_T", "L2_ffn_lora_B_T",
        "L2_ffn_b", "L2_ffn_gate_b", "L3_inv_freq", "pos_BxS2", "itok_BxS_4096_4607", "L3_xattn_q_norm_w",
        "L3_xattn_k_norm_w", "L3_xattn_Wq_T", "L3_xattn_Wk_T", "L3_xattn_Wv_T", "L3_xattn_Wo_T", "L3_attn_Wdtlam_T",
        "L3_attn_A_log", "L3_attn_Wx_T", "L3_attn_Wz_T", "L3_attn_Wout_T", "L3_attn_Bn_w_perm", "L3_attn_Cn_w_perm",
        "L3_attn_Wth_T", "L3_attn_WB_T", "L3_attn_B_bias_perm", "L3_attn_WC_T", "L3_attn_C_bias_perm",
        "L3_ffn_packed_T", "L3_ffn_scales_T")


def build(nc, A, out):
    with ExitStack() as ctx:
        k = Core(nc, ctx, A)
        constants(k, A["x"])
        for stage in STAGES:
            stage(k)
        with nc.semaphore("stored") as stored, nc.Block() as block:
            @block.sync
            def _(sp):
                sp.dma_start(out.rearrange("b t d -> t b d"), k.x[:]).then_inc(stored, 16)
                sp.wait_ge(stored, 16)


def kernel(**inputs):
    import concourse.bacc as bacc
    from concourse.bass_utils import run_bass_kernel_spmd

    arrays = layouts({name: np.asarray(a) for name, a in inputs.items()})
    nc = bacc.Bacc("TRN2", target_bir_lowering=False, num_devices=1)
    A = {name: nc.dram_tensor("in_" + name, arrays[name].shape, mybir.dt.from_np(arrays[name].dtype), kind="ExternalInput").ap()
         for name in READ}
    out = nc.dram_tensor("out_x", (B, T, D), F32, kind="ExternalOutput").ap()
    build(nc, A, out)
    result = run_bass_kernel_spmd(nc, [{"in_" + name: arrays[name] for name in READ}], core_ids=[0])
    return result.results[0]["out_x"]
```
